# Optimizing a Trainium2 kernel written in Bass

```python
import numpy as np
import jax
import jax.numpy as jnp

def _softmax(x, axis=-1):
    return jax.nn.softmax(x, axis=axis)

def _gelu(x):
    return jax.nn.gelu(x, approximate=True)

def _silu(x):
    return jax.nn.silu(x)

def _sigmoid(x):
    return jax.nn.sigmoid(x)

def _layernorm(x, axis=-1, eps=1e-05):
    m = jnp.mean(x, axis=axis, keepdims=True)
    v = jnp.var(x, axis=axis, keepdims=True)
    return (x - m) / jnp.sqrt(v + eps)

def _scatter_add(tgt, idx, src, axis=0):
    return tgt.at[idx].add(src)

def _segment_sum(src, seg, n):
    return jax.ops.segment_sum(src, seg, n)
kernel_name = 'mk_decoder_postln_d4_seqx_r8_afb401'

def setup_inputs(seed: int=0):
    np.random.seed(seed)
    _w = jnp.asarray

    def _rec_inputs():
        import jax
        import jax.numpy as jnp
        _rk = jax.random.key(seed)
        x = 7.22e-05 + 1 * jax.random.normal(jax.random.fold_in(_rk, 1), (4, 256, 256), jnp.float32)
        _lenS = 256 - jax.random.randint(jax.random.fold_in(_rk, 7), (4,), 0, max(1, 256 // 4) + 1, jnp.int32)
        _lenS2 = 64 - jax.random.randint(jax.random.fold_in(_rk, 8), (4,), 0, max(1, 64 // 4) + 1, jnp.int32)
        _ctx_512P = jax.random.normal(jax.random.fold_in(_rk, 11), (4, 16, 64), jnp.float32)
        _ctx_512c = jax.random.dirichlet(jax.random.fold_in(_rk, 511), 0.3 * jnp.ones((16,), jnp.float32), (4, 64))
        _ctx_512t = jnp.einsum('bsk,bkd->bsd', _ctx_512c, _ctx_512P)
        _ctx_512t = _ctx_512t * jax.lax.rsqrt(jnp.mean(jnp.square(_ctx_512t)) + 1e-12) * 0.953939
        ctx_512 = -0.000514642 + 1.00011 * (_ctx_512t + 0.3 * jax.random.normal(jax.random.fold_in(_rk, 611), (4, 64, 64), jnp.float32))
        return (x, ctx_512)
    x, ctx_512 = _rec_inputs()

    def _L0_attn_setup():
        import jax, jax.numpy as jnp
        import numpy as np
        B, N, C, H = (4, 256, 256, 16)
        DH = C // H
        key = jax.random.key(seed)
        ks = jax.random.split(key, 5)
        s = 0.02
        return {'x': jax.random.normal(ks[0], (B, N, C), dtype=jnp.float32), 'w_qkv': jax.random.normal(ks[1], (3 * C, C), dtype=jnp.float32) * s, 'b_qkv': jax.random.normal(ks[2], (3 * C,), dtype=jnp.float32) * s, 'w_out': jax.random.normal(ks[3], (C, C), dtype=jnp.float32) * s, 'b_out': jax.random.normal(ks[4], (C,), dtype=jnp.float32) * s}
    _L0_attn_all = _L0_attn_setup()
    _L0_attn_in = {k: v for k, v in _L0_attn_all.items() if k in ('w_qkv', 'b_qkv', 'w_out', 'b_out')}
    del _L0_attn_all

    def _L0_xattn_setup():
        import jax, jax.numpy as jnp
        import numpy as np
        B, S, H, NH, L = (2, 256, 256, 16, 64)
        HD = H // NH
        key = jax.random.key(seed)
        k1, k2, k3, k4, k5 = jax.random.split(key, 5)
        scale = 0.02
        return {'q': jax.random.normal(k1, (B, S, H), dtype=jnp.float32), 'latent_kv': jax.random.normal(k2, (B, S, L), dtype=jnp.float32), 'Wq': jax.random.normal(k3, (H, H), dtype=jnp.float32) * scale, 'Wkv_expand': jax.random.normal(k4, (2 * H, L), dtype=jnp.float32) * scale, 'Wout': jax.random.normal(k5, (H, H), dtype=jnp.float32) * scale}
    _L0_xattn_all = _L0_xattn_setup()
    _L0_xattn_in = {k: v for k, v in _L0_xattn_all.items() if k in ('Wq', 'Wkv_expand', 'Wout')}
    del _L0_xattn_all

    def _L0_ffn_setup():
        import jax, jax.numpy as jnp
        import numpy as np
        B, S, H = (2, 128, 256)
        E, K = (8, 2)
        I = 176
        IS = 704
        WSCALE = 0.02
        key = jax.random.key(seed)
        ks = jax.random.split(key, 9)
        f32 = jnp.float32
        return {'hidden_states': jax.random.normal(ks[0], (B, S, H), dtype=f32), 'gate_w': jax.random.normal(ks[1], (E, H), dtype=f32) * WSCALE, 'w_gate': jax.random.normal(ks[2], (E, H, I), dtype=f32) * WSCALE, 'w_up': jax.random.normal(ks[3], (E, H, I), dtype=f32) * WSCALE, 'w_down': jax.random.normal(ks[4], (E, I, H), dtype=f32) * WSCALE, 'sw_gate': jax.random.normal(ks[5], (H, IS), dtype=f32) * WSCALE, 'sw_up': jax.random.normal(ks[6], (H, IS), dtype=f32) * WSCALE, 'sw_down': jax.random.normal(ks[7], (IS, H), dtype=f32) * WSCALE, 'shared_gate_w': jax.random.normal(ks[8], (H, 1), dtype=f32) * WSCALE}
    _L0_ffn_all = _L0_ffn_setup()
    _L0_ffn_in = {k: v for k, v in _L0_ffn_all.items() if k in ('gate_w', 'w_gate', 'w_up', 'w_down', 'sw_gate', 'sw_up', 'sw_down', 'shared_gate_w')}
    del _L0_ffn_all

    def _L1_attn_setup():
        import jax, jax.numpy as jnp
        import numpy as np
        BLOCK = 32
        EPS = 1e-06

        def _silu(x):
            return x * jax.nn.sigmoid(x)
        key = jax.random.key(seed)
        k1, k2, k3, k4 = jax.random.split(key, 4)
        embed_dim, hidden_dim = (256, 256)
        b, n, h = (2, 512, 16)
        x = jax.random.normal(k1, (b, n, embed_dim), dtype=jnp.float32)
        slope_rate = jax.random.uniform(k2, (h, 1, 1), dtype=jnp.float32, minval=0.01, maxval=1.0)
        W_qkvu = jax.random.normal(k3, (4 * hidden_dim, embed_dim), dtype=jnp.float32) / np.sqrt(embed_dim)
        W_out = jax.random.normal(k4, (embed_dim, hidden_dim), dtype=jnp.float32) / np.sqrt(hidden_dim)
        return {'x': x, 'slope_rate': slope_rate, 'W_qkvu': W_qkvu, 'W_out': W_out}
    _L1_attn_all = _L1_attn_setup()
    _L1_attn_in = {k: v for k, v in _L1_attn_all.items() if k in ('slope_rate', 'W_qkvu', 'W_out')}
    del _L1_attn_all

    def _L1_xattn_setup():
        import jax, jax.numpy as jnp
        import numpy as np
        B, S, H, NH, L = (2, 256, 256, 16, 64)
        HD = H // NH
        key = jax.random.key(seed)
        k1, k2, k3, k4, k5 = jax.random.split(key, 5)
        scale = 0.02
        return {'q': jax.random.normal(k1, (B, S, H), dtype=jnp.float32), 'latent_kv': jax.random.normal(k2, (B, S, L), dtype=jnp.float32), 'Wq': jax.random.normal(k3, (H, H), dtype=jnp.float32) * scale, 'Wkv_expand': jax.random.normal(k4, (2 * H, L), dtype=jnp.float32) * scale, 'Wout': jax.random.normal(k5, (H, H), dtype=jnp.float32) * scale}
    _L1_xattn_all = _L1_xattn_setup()
    _L1_xattn_in = {k: v for k, v in _L1_xattn_all.items() if k in ('Wq', 'Wkv_expand', 'Wout')}
    del _L1_xattn_all

    def _L1_ffn_setup():
        import jax, jax.numpy as jnp
        import numpy as np
        D_MODEL = 256
        D_FF = 1024
        N_EXPERTS = 4
        B, S = (2, 256)
        key = jax.random.key(seed)
        ks = jax.random.split(key, 6)
        scale = 0.02
        return {'hidden_states': jax.random.normal(ks[0], (B, S, D_MODEL), dtype=jnp.float32), 'Wr': jax.random.normal(ks[1], (D_MODEL, N_EXPERTS), dtype=jnp.float32) * scale, 'br': jnp.zeros((N_EXPERTS,), dtype=jnp.float32), 'Wg': jax.random.normal(ks[2], (N_EXPERTS, D_MODEL, D_FF), dtype=jnp.float32) * scale, 'Wu': jax.random.normal(ks[3], (N_EXPERTS, D_MODEL, D_FF), dtype=jnp.float32) * scale, 'Wd': jax.random.normal(ks[4], (N_EXPERTS, D_FF, D_MODEL), dtype=jnp.float32) * scale}
    _L1_ffn_all = _L1_ffn_setup()
    _L1_ffn_in = {k: v for k, v in _L1_ffn_all.items() if k in ('Wr', 'br', 'Wg', 'Wu', 'Wd')}
    del _L1_ffn_all

    def _L2_attn_setup():
        import jax, jax.numpy as jnp
        import numpy as np
        D_MODEL = 256
        NUM_HEADS = 16
        HEAD_DIM = D_MODEL // NUM_HEADS
        LAYER_IDX = 0
        NUM_LAYERS = 13
        REINIT_LAMBDA = 0.8

        def _heads(t, B, S):
            return t.reshape(B, S, NUM_HEADS, HEAD_DIM).transpose(0, 2, 1, 3)
        key = jax.random.key(seed)
        ks = jax.random.split(key, 8)
        B, S = (2, 256)
        x = jax.random.normal(ks[0], (B, S, D_MODEL), dtype=jnp.float32)
        init = 1.0 / np.sqrt(D_MODEL)

        def w(k):
            return jax.random.uniform(k, (D_MODEL, D_MODEL), dtype=jnp.float32, minval=-init, maxval=init)
        lam_init = REINIT_LAMBDA * ((LAYER_IDX + 1) / NUM_LAYERS)
        return {'x': x, 'q1_w': w(ks[1]), 'k1_w': w(ks[2]), 'q2_w': w(ks[3]), 'k2_w': w(ks[4]), 'v_w': w(ks[5]), 'o_w': w(ks[6]), 'lambda_param': jnp.full((NUM_HEADS,), lam_init, dtype=jnp.float32)}
    _L2_attn_all = _L2_attn_setup()
    _L2_attn_in = {k: v for k, v in _L2_attn_all.items() if k in ('q1_w', 'k1_w', 'q2_w', 'k2_w', 'v_w', 'o_w', 'lambda_param')}
    del _L2_attn_all

    def _L2_xattn_setup():
        import jax, jax.numpy as jnp
        import numpy as np
        B, S, L = (2, 128, 128)
        DIM_Q, H, K, D_C, D_CQ, R = (256, 16, 128, 64, 192, 64)

        def _rope_tables(seq_len, dim, dtype):
            inv_freq = 1.0 / 10000.0 ** (jnp.arange(0, dim, 2, dtype=dtype) / dim)
            t = jnp.arange(seq_len, dtype=dtype)
            freqs = t[:, None] * inv_freq[None, :]
            sin = jnp.repeat(jnp.sin(freqs), 2, axis=-1)
            cos = jnp.repeat(jnp.cos(freqs), 2, axis=-1)
            return (sin, cos)

        def _rotate_half(x):
            h = x.shape[-1] // 2
            return jnp.concatenate([-x[..., h:], x[..., :h]], axis=-1)
        key = jax.random.key(seed)
        ks = jax.random.split(key, 8)
        s_in = 1.0 / np.sqrt(DIM_Q)
        s_k = 1.0 / np.sqrt(K)
        s_cq = 1.0 / np.sqrt(D_CQ)
        s_c = 1.0 / np.sqrt(D_C)
        return {'hidden_q': jax.random.normal(ks[0], (B, S, DIM_Q), jnp.float32), 'kv_c': jax.random.normal(ks[1], (B, L, D_C), jnp.float32), 'Wq': jax.random.normal(ks[2], (H * K, DIM_Q), jnp.float32) * s_in, 'w_kc_q': jax.random.normal(ks[3], (H, K, D_CQ), jnp.float32) * s_k, 'w_kc_kv': jax.random.normal(ks[4], (H, K, D_C), jnp.float32) * s_k, 'W_qr': jax.random.normal(ks[5], (H, D_CQ, R), jnp.float32) * s_cq / np.sqrt(R), 'W_kr': jax.random.normal(ks[6], (H, D_C, R), jnp.float32) * s_c, 'Wo': jax.random.normal(ks[7], (DIM_Q, H * K), jnp.float32) * s_k}
    _L2_xattn_all = _L2_xattn_setup()
    _L2_xattn_in = {k: v for k, v in _L2_xattn_all.items() if k in ('Wq', 'w_kc_q', 'w_kc_kv', 'W_qr', 'W_kr', 'Wo')}
    del _L2_xattn_all

    def _L2_ffn_setup():
        import jax, jax.numpy as jnp
        import numpy as np
        B_, S, D = (2, 256, 256)
        F_ = 1024
        R = 16
        H = 16
        HD = D // H
        MOD_SCALE = 0.1
        EPS = 1e-06

        def _rmsnorm(x, w):
            v = jnp.mean(x * x, axis=-1, keepdims=True)
            return x * jax.lax.rsqrt(v + EPS) * w

        def _attention(x, Wq, Wk, Wv, Wo):
            b, s, d = x.shape
            q = (x @ Wq.T).reshape(b, s, H, HD)
            k = (x @ Wk.T).reshape(b, s, H, HD)
            v = (x @ Wv.T).reshape(b, s, H, HD)
            scores = jnp.einsum('bqhd,bkhd->bhqk', q, k) / np.sqrt(HD).astype(np.float32)
            causal = jnp.tril(jnp.ones((s, s), bool))
            scores = jnp.where(causal, scores, jnp.finfo(scores.dtype).min)
            probs = jax.nn.softmax(scores, axis=-1)
            out = jnp.einsum('bhqk,bkhd->bqhd', probs, v).reshape(b, s, d)
            return out @ Wo.T
        key = jax.random.key(seed)
        ks = jax.random.split(key, 12)
        sd = 0.02
        return {'hidden_states': jax.random.normal(ks[0], (B_, S, D), jnp.float32), 'ln1_w': jnp.ones((D,), jnp.float32), 'ln2_w': jnp.ones((D,), jnp.float32), 'Wq': jax.random.normal(ks[1], (D, D), jnp.float32) * sd, 'Wk': jax.random.normal(ks[2], (D, D), jnp.float32) * sd, 'Wv': jax.random.normal(ks[3], (D, D), jnp.float32) * sd, 'Wo': jax.random.normal(ks[4], (D, D), jnp.float32) * sd, 'A': jax.random.normal(ks[5], (D, R), jnp.float32) * (0.01 / np.sqrt(D)), 'B': jax.random.normal(ks[6], (R, F_), jnp.float32) * (0.01 / np.sqrt(R)), 'W_in_base': jax.random.normal(ks[7], (F_, D), jnp.float32) * sd, 'W_up_base': jax.random.normal(ks[8], (F_, D), jnp.float32) * sd, 'W_down': jax.random.normal(ks[9], (D, F_), jnp.float32) * sd}
    _L2_ffn_all = _L2_ffn_setup()
    _L2_ffn_in = {k: v for k, v in _L2_ffn_all.items() if k in ('ln1_w', 'ln2_w', 'Wq', 'Wk', 'Wv', 'Wo', 'A', 'B', 'W_in_base', 'W_up_base', 'W_down')}
    del _L2_ffn_all

    def _L3_attn_setup():
        import jax, jax.numpy as jnp
        import numpy as np
        D_MODEL = 256
        H = 16
        HKV = 4
        DH = D_MODEL // H
        WINDOW = 32
        GROUP = H // HKV
        ROPE_BASE = 10000.0
        NEG_INF = -1e+30

        def _rotate_half(t):
            t1, t2 = jnp.split(t, 2, axis=-1)
            return jnp.concatenate([-t2, t1], axis=-1)

        def _apply_rope(q, k, positions):
            inv_freq = 1.0 / ROPE_BASE ** (jnp.arange(0, DH, 2, dtype=jnp.float32) / DH)
            ang = positions.astype(jnp.float32)[:, None] * inv_freq[None, :]
            cos = jnp.concatenate([jnp.cos(ang), jnp.cos(ang)], axis=-1)[None, None]
            sin = jnp.concatenate([jnp.sin(ang), jnp.sin(ang)], axis=-1)[None, None]
            q = q * cos + _rotate_half(q) * sin
            k = k * cos + _rotate_half(k) * sin
            return (q, k)
        key = jax.random.key(seed)
        ks = jax.random.split(key, 5)
        B, L = (2, 256)
        x = jax.random.normal(ks[0], (B, L, D_MODEL), dtype=jnp.float32)
        Wq = jax.random.normal(ks[1], (H * DH, D_MODEL), dtype=jnp.float32) * 0.02
        Wkv = jax.random.normal(ks[2], (2 * HKV * DH, D_MODEL), dtype=jnp.float32) * 0.02
        Wo = jax.random.normal(ks[3], (D_MODEL, D_MODEL), dtype=jnp.float32) * 0.02
        qk_temp = jnp.full((H, 1, 1), np.sqrt(DH), dtype=jnp.float32)
        return {'x': x, 'Wq': Wq, 'Wkv': Wkv, 'Wo': Wo, 'qk_temp': qk_temp}
    _L3_attn_all = _L3_attn_setup()
    _L3_attn_in = {k: v for k, v in _L3_attn_all.items() if k in ('Wq', 'Wkv', 'Wo', 'qk_temp')}
    del _L3_attn_all

    def _L3_xattn_setup():
        import jax, jax.numpy as jnp
        import numpy as np
        B, S, L = (2, 128, 128)
        DIM_Q, H, K, D_C, D_CQ, R = (256, 16, 128, 64, 192, 64)

        def _rope_tables(length, dim):
            inv = 1.0 / 10000.0 ** (jnp.arange(0, dim, 2, dtype=jnp.float32) / dim)
            f = jnp.arange(length, dtype=jnp.float32)[:, None] * inv[None, :]
            sin = jnp.repeat(jnp.sin(f), 2, axis=-1)
            cos = jnp.repeat(jnp.cos(f), 2, axis=-1)
            return (sin, cos)

        def _rotate_half(x):
            half = x.shape[-1] // 2
            return jnp.concatenate([-x[..., half:], x[..., :half]], axis=-1)

        def _apply_rope(x, sin, cos):
            return x * cos + _rotate_half(x) * sin
        key = jax.random.key(seed)
        ks = jax.random.split(key, 8)
        return {'hidden_q': jax.random.normal(ks[0], (B, S, DIM_Q), jnp.float32), 'kv_c': jax.random.normal(ks[1], (B, L, D_C), jnp.float32), 'Wq': jax.random.normal(ks[2], (H * K, DIM_Q), jnp.float32) / np.sqrt(DIM_Q).astype(np.float32), 'w_kc_q': jax.random.normal(ks[3], (H, K, D_CQ), jnp.float32) / np.sqrt(K).astype(np.float32), 'w_kc_kv': jax.random.normal(ks[4], (H, K, D_C), jnp.float32) / np.sqrt(K).astype(np.float32), 'W_qr': jax.random.normal(ks[5], (H, D_CQ, R), jnp.float32) / np.float32(np.sqrt(D_CQ) * np.sqrt(R)), 'W_kr': jax.random.normal(ks[6], (H, D_C, R), jnp.float32) / np.sqrt(D_C).astype(np.float32), 'Wo': jax.random.normal(ks[7], (DIM_Q, H * K), jnp.float32) / np.sqrt(H * K).astype(np.float32)}
    _L3_xattn_all = _L3_xattn_setup()
    _L3_xattn_in = {k: v for k, v in _L3_xattn_all.items() if k in ('Wq', 'w_kc_q', 'w_kc_kv', 'W_qr', 'W_kr', 'Wo')}
    del _L3_xattn_all

    def _L3_ffn_setup():
        import jax, jax.numpy as jnp
        import numpy as np
        TOP_K = 2
        key = jax.random.key(seed)
        ks = jax.random.split(key, 5)
        B, T, D, E, H = (4, 256, 256, 8, 176)
        s = 1.0 / np.sqrt(D)
        sh = 1.0 / np.sqrt(H)
        return {'x': jax.random.normal(ks[0], (B, T, D), dtype=jnp.float32), 'Wg': jax.random.normal(ks[1], (E, D), dtype=jnp.float32) * s, 'W1': jax.random.normal(ks[2], (E, H, D), dtype=jnp.float32) * s, 'W2': jax.random.normal(ks[3], (E, H, D), dtype=jnp.float32) * s, 'W3': jax.random.normal(ks[4], (E, D, H), dtype=jnp.float32) * sh}
    _L3_ffn_all = _L3_ffn_setup()
    _L3_ffn_in = {k: v for k, v in _L3_ffn_all.items() if k in ('Wg', 'W1', 'W2', 'W3')}
    del _L3_ffn_all
    return {'x': x, 'ctx_512': ctx_512, 'L0_attn_w_qkv': _L0_attn_in['w_qkv'], 'L0_attn_b_qkv': _L0_attn_in['b_qkv'], 'L0_attn_w_out': _L0_attn_in['w_out'], 'L0_attn_b_out': _L0_attn_in['b_out'], 'L0_xattn_Wq': _L0_xattn_in['Wq'], 'L0_xattn_Wkv_expand': _L0_xattn_in['Wkv_expand'], 'L0_xattn_Wout': _L0_xattn_in['Wout'], 'L0_ffn_gate_w': _L0_ffn_in['gate_w'], 'L0_ffn_w_gate': _L0_ffn_in['w_gate'], 'L0_ffn_w_up': _L0_ffn_in['w_up'], 'L0_ffn_w_down': _L0_ffn_in['w_down'], 'L0_ffn_sw_gate': _L0_ffn_in['sw_gate'], 'L0_ffn_sw_up': _L0_ffn_in['sw_up'], 'L0_ffn_sw_down': _L0_ffn_in['sw_down'], 'L0_ffn_shared_gate_w': _L0_ffn_in['shared_gate_w'], 'L1_attn_slope_rate': _L1_attn_in['slope_rate'], 'L1_attn_W_qkvu': _L1_attn_in['W_qkvu'], 'L1_attn_W_out': _L1_attn_in['W_out'], 'L1_xattn_Wq': _L1_xattn_in['Wq'], 'L1_xattn_Wkv_expand': _L1_xattn_in['Wkv_expand'], 'L1_xattn_Wout': _L1_xattn_in['Wout'], 'L1_ffn_Wr': _L1_ffn_in['Wr'], 'L1_ffn_br': _L1_ffn_in['br'], 'L1_ffn_Wg': _L1_ffn_in['Wg'], 'L1_ffn_Wu': _L1_ffn_in['Wu'], 'L1_ffn_Wd': _L1_ffn_in['Wd'], 'L2_attn_q1_w': _L2_attn_in['q1_w'], 'L2_attn_k1_w': _L2_attn_in['k1_w'], 'L2_attn_q2_w': _L2_attn_in['q2_w'], 'L2_attn_k2_w': _L2_attn_in['k2_w'], 'L2_attn_v_w': _L2_attn_in['v_w'], 'L2_attn_o_w': _L2_attn_in['o_w'], 'L2_attn_lambda_param': _L2_attn_in['lambda_param'], 'L2_xattn_Wq': _L2_xattn_in['Wq'], 'L2_xattn_w_kc_q': _L2_xattn_in['w_kc_q'], 'L2_xattn_w_kc_kv': _L2_xattn_in['w_kc_kv'], 'L2_xattn_W_qr': _L2_xattn_in['W_qr'], 'L2_xattn_W_kr': _L2_xattn_in['W_kr'], 'L2_xattn_Wo': _L2_xattn_in['Wo'], 'L2_ffn_ln1_w': _L2_ffn_in['ln1_w'], 'L2_ffn_ln2_w': _L2_ffn_in['ln2_w'], 'L2_ffn_Wq': _L2_ffn_in['Wq'], 'L2_ffn_Wk': _L2_ffn_in['Wk'], 'L2_ffn_Wv': _L2_ffn_in['Wv'], 'L2_ffn_Wo': _L2_ffn_in['Wo'], 'L2_ffn_A': _L2_ffn_in['A'], 'L2_ffn_B': _L2_ffn_in['B'], 'L2_ffn_W_in_base': _L2_ffn_in['W_in_base'], 'L2_ffn_W_up_base': _L2_ffn_in['W_up_base'], 'L2_ffn_W_down': _L2_ffn_in['W_down'], 'L3_attn_Wq': _L3_attn_in['Wq'], 'L3_attn_Wkv': _L3_attn_in['Wkv'], 'L3_attn_Wo': _L3_attn_in['Wo'], 'L3_attn_qk_temp': _L3_attn_in['qk_temp'], 'L3_xattn_Wq': _L3_xattn_in['Wq'], 'L3_xattn_w_kc_q': _L3_xattn_in['w_kc_q'], 'L3_xattn_w_kc_kv': _L3_xattn_in['w_kc_kv'], 'L3_xattn_W_qr': _L3_xattn_in['W_qr'], 'L3_xattn_W_kr': _L3_xattn_in['W_kr'], 'L3_xattn_Wo': _L3_xattn_in['Wo'], 'L3_ffn_Wg': _L3_ffn_in['Wg'], 'L3_ffn_W1': _L3_ffn_in['W1'], 'L3_ffn_W2': _L3_ffn_in['W2'], 'L3_ffn_W3': _L3_ffn_in['W3']}

def reference(x, ctx_512, L0_attn_w_qkv, L0_attn_b_qkv, L0_attn_w_out, L0_attn_b_out, L0_xattn_Wq, L0_xattn_Wkv_expand, L0_xattn_Wout, L0_ffn_gate_w, L0_ffn_w_gate, L0_ffn_w_up, L0_ffn_w_down, L0_ffn_sw_gate, L0_ffn_sw_up, L0_ffn_sw_down, L0_ffn_shared_gate_w, L1_attn_slope_rate, L1_attn_W_qkvu, L1_attn_W_out, L1_xattn_Wq, L1_xattn_Wkv_expand, L1_xattn_Wout, L1_ffn_Wr, L1_ffn_br, L1_ffn_Wg, L1_ffn_Wu, L1_ffn_Wd, L2_attn_q1_w, L2_attn_k1_w, L2_attn_q2_w, L2_attn_k2_w, L2_attn_v_w, L2_attn_o_w, L2_attn_lambda_param, L2_xattn_Wq, L2_xattn_w_kc_q, L2_xattn_w_kc_kv, L2_xattn_W_qr, L2_xattn_W_kr, L2_xattn_Wo, L2_ffn_ln1_w, L2_ffn_ln2_w, L2_ffn_Wq, L2_ffn_Wk, L2_ffn_Wv, L2_ffn_Wo, L2_ffn_A, L2_ffn_B, L2_ffn_W_in_base, L2_ffn_W_up_base, L2_ffn_W_down, L3_attn_Wq, L3_attn_Wkv, L3_attn_Wo, L3_attn_qk_temp, L3_xattn_Wq, L3_xattn_w_kc_q, L3_xattn_w_kc_kv, L3_xattn_W_qr, L3_xattn_W_kr, L3_xattn_Wo, L3_ffn_Wg, L3_ffn_W1, L3_ffn_W2, L3_ffn_W3):
    import jax
    import jax.numpy as jnp

    def _L0_attn_ref(x, w_qkv, b_qkv, w_out, b_out):
        import jax, jax.numpy as jnp
        import numpy as np
        B, N, C, H = (4, 256, 256, 16)
        DH = C // H
        b, n, c = x.shape
        qkv = x @ w_qkv.T + b_qkv
        qkv = qkv.reshape(b, n, 3, H, c // H)
        q, k, v = (qkv[:, :, 0], qkv[:, :, 1], qkv[:, :, 2])
        attn = jnp.einsum('bnhd,bngd->bnhg', q, k) / jnp.sqrt(jnp.float32(c))
        attn = jax.nn.softmax(attn, axis=-1)
        out = jnp.einsum('bnhg,bngd->bnhd', attn, v)
        out = out.transpose(0, 2, 1, 3).reshape(b, n, c)
        return out @ w_out.T + b_out

    def _L0_xattn_ref(q, latent_kv, Wq, Wkv_expand, Wout):
        import jax, jax.numpy as jnp
        import numpy as np
        B, S, H, NH, L = (2, 256, 256, 16, 64)
        HD = H // NH
        b, sq, _ = q.shape
        sk = latent_kv.shape[1]
        qp = q @ Wq.T
        kv = latent_kv @ Wkv_expand.T
        k, v = jnp.split(kv, 2, axis=-1)
        qh = qp.reshape(b, sq, NH, HD).transpose(0, 2, 1, 3)
        kh = k.reshape(b, sk, NH, HD).transpose(0, 2, 1, 3)
        vh = v.reshape(b, sk, NH, HD).transpose(0, 2, 1, 3)
        inv_sqrt_d = 1.0 / jnp.sqrt(jnp.float32(HD))
        scores = jnp.einsum('bhqd,bhkd->bhqk', qh, kh) * inv_sqrt_d
        causal = jnp.tril(jnp.ones((sq, sk), dtype=bool))
        scores = jnp.where(causal, scores, jnp.finfo(scores.dtype).min)
        attn = jax.nn.softmax(scores, axis=-1)
        out = jnp.einsum('bhqk,bhkd->bhqd', attn, vh)
        out = out.transpose(0, 2, 1, 3).reshape(b, sq, H)
        return out @ Wout.T

    def _L0_ffn_ref(hidden_states, gate_w, w_gate, w_up, w_down, sw_gate, sw_up, sw_down, shared_gate_w):
        import jax, jax.numpy as jnp
        import numpy as np
        B, S, H = (2, 128, 256)
        E, K = (8, 2)
        I = 176
        IS = 704
        WSCALE = 0.02
        x = hidden_states
        logits = jnp.einsum('bsh,eh->bse', x, gate_w)
        probs = jax.nn.softmax(logits, axis=-1)
        top_w, top_i = jax.lax.top_k(probs, K)
        top_w = top_w / jnp.sum(top_w, axis=-1, keepdims=True)
        onehot = jax.nn.one_hot(top_i, E, dtype=x.dtype)
        combine = jnp.einsum('bsk,bske->bse', top_w, onehot)
        g = jnp.einsum('bsh,ehi->besi', x, w_gate)
        u = jnp.einsum('bsh,ehi->besi', x, w_up)
        h = jax.nn.silu(g) * u
        expert_out = jnp.einsum('besi,eih->besh', h, w_down)
        moe_out = jnp.einsum('besh,bse->bsh', expert_out, combine)
        sh = jax.nn.silu(x @ sw_gate) * (x @ sw_up)
        shared_out = sh @ sw_down
        shared_gate = jax.nn.sigmoid(x @ shared_gate_w)
        return moe_out + shared_out * shared_gate

    def _L1_attn_ref(x, slope_rate, W_qkvu, W_out):
        import jax, jax.numpy as jnp
        import numpy as np
        BLOCK = 32
        EPS = 1e-06

        def _silu(x):
            return x * jax.nn.sigmoid(x)
        b, n, embed_dim = x.shape
        h = slope_rate.shape[0]
        hidden_dim = W_qkvu.shape[0] // 4
        d = hidden_dim // h
        NB = n // BLOCK
        qkvu = x @ W_qkvu.T
        q, k, v, u = jnp.split(qkvu, 4, axis=-1)

        def to_heads(t):
            return t.reshape(b, n, h, d).transpose(0, 2, 1, 3)
        q = _silu(to_heads(q))
        k = _silu(to_heads(k))
        v = to_heads(v)
        s = slope_rate
        arr = jnp.arange(1, BLOCK + 1, dtype=x.dtype)
        q_decay = jnp.exp(-s * arr[:, None])
        k_decay = jnp.exp(-s * (BLOCK - arr[:, None]))
        idx = arr[:, None] - arr[None, :]
        diag_decay = jnp.exp(jnp.where(idx >= 0, -s * idx, -jnp.inf))
        block_decay = jnp.exp(-s * BLOCK)

        def blk(t):
            return t.reshape(b, h, NB, BLOCK, d).transpose(2, 0, 1, 3, 4)
        qb, kb, vb = (blk(q), blk(k), blk(v))

        def step(kv, inp):
            qi, ki, vi = inp
            qkv_none_diag = jnp.einsum('bhmd,bhde->bhme', qi * q_decay, kv)
            qk = jnp.einsum('bhmd,bhsd->bhms', qi, ki) * diag_decay
            qkv_diag = jnp.einsum('bhms,bhse->bhme', qk, vi)
            kv_new = block_decay * kv + jnp.einsum('bhsd,bhse->bhde', ki * k_decay, vi)
            return (kv_new, qkv_none_diag + qkv_diag)
        kv0 = jnp.zeros((b, h, d, d), dtype=jnp.float32)
        _, outs = jax.lax.scan(step, kv0, (qb, kb, vb))
        o = outs.transpose(1, 2, 0, 3, 4).reshape(b, h, n, d)
        o = o.transpose(0, 2, 1, 3).reshape(b, n, hidden_dim)
        o = o * jax.lax.rsqrt(jnp.mean(o * o, axis=-1, keepdims=True) + EPS)
        o = u * o
        return o @ W_out.T

    def _L1_xattn_ref(q, latent_kv, Wq, Wkv_expand, Wout):
        import jax, jax.numpy as jnp
        import numpy as np
        B, S, H, NH, L = (2, 256, 256, 16, 64)
        HD = H // NH
        b, sq, _ = q.shape
        sk = latent_kv.shape[1]
        qp = q @ Wq.T
        kv = latent_kv @ Wkv_expand.T
        k, v = jnp.split(kv, 2, axis=-1)
        qh = qp.reshape(b, sq, NH, HD).transpose(0, 2, 1, 3)
        kh = k.reshape(b, sk, NH, HD).transpose(0, 2, 1, 3)
        vh = v.reshape(b, sk, NH, HD).transpose(0, 2, 1, 3)
        inv_sqrt_d = 1.0 / jnp.sqrt(jnp.float32(HD))
        scores = jnp.einsum('bhqd,bhkd->bhqk', qh, kh) * inv_sqrt_d
        causal = jnp.tril(jnp.ones((sq, sk), dtype=bool))
        scores = jnp.where(causal, scores, jnp.finfo(scores.dtype).min)
        attn = jax.nn.softmax(scores, axis=-1)
        out = jnp.einsum('bhqk,bhkd->bhqd', attn, vh)
        out = out.transpose(0, 2, 1, 3).reshape(b, sq, H)
        return out @ Wout.T

    def _L1_ffn_ref(hidden_states, Wr, br, Wg, Wu, Wd):
        import jax, jax.numpy as jnp
        import numpy as np
        D_MODEL = 256
        D_FF = 1024
        N_EXPERTS = 4
        B, S = (2, 256)
        b, s, d = hidden_states.shape
        x = hidden_states.reshape(-1, d)
        logits = x @ Wr + br
        probs = jax.nn.softmax(logits, axis=-1)
        top_w, top_idx = jax.lax.top_k(probs, 1)
        g = jnp.einsum('td,edf->tef', x, Wg)
        u = jnp.einsum('td,edf->tef', x, Wu)
        h = jax.nn.silu(g) * u
        y = jnp.einsum('tef,efd->ted', h, Wd)
        sel = jnp.take_along_axis(y, top_idx[:, :, None], axis=1)[:, 0]
        out = sel * top_w
        return out.reshape(b, s, d)

    def _L2_attn_ref(x, q1_w, k1_w, q2_w, k2_w, v_w, o_w, lambda_param):
        import jax, jax.numpy as jnp
        import numpy as np
        D_MODEL = 256
        NUM_HEADS = 16
        HEAD_DIM = D_MODEL // NUM_HEADS
        LAYER_IDX = 0
        NUM_LAYERS = 13
        REINIT_LAMBDA = 0.8

        def _heads(t, B, S):
            return t.reshape(B, S, NUM_HEADS, HEAD_DIM).transpose(0, 2, 1, 3)
        B, S, _ = x.shape
        q1 = _heads(x @ q1_w.T, B, S)
        k1 = _heads(x @ k1_w.T, B, S)
        q2 = _heads(x @ q2_w.T, B, S)
        k2 = _heads(x @ k2_w.T, B, S)
        v = _heads(x @ v_w.T, B, S)
        scale = jnp.sqrt(jnp.float32(HEAD_DIM))
        attn1 = jax.nn.softmax(jnp.einsum('bhqd,bhkd->bhqk', q1, k1) / scale, axis=-1)
        attn2 = jax.nn.softmax(jnp.einsum('bhqd,bhkd->bhqk', q2, k2) / scale, axis=-1)
        lam = lambda_param.reshape(1, NUM_HEADS, 1, 1)
        out = jnp.einsum('bhqk,bhkd->bhqd', attn1 - lam * attn2, v)
        out = out.transpose(0, 2, 1, 3).reshape(B, S, D_MODEL)
        return out @ o_w.T

    def _L2_xattn_ref(hidden_q, kv_c, Wq, w_kc_q, w_kc_kv, W_qr, W_kr, Wo):
        import jax, jax.numpy as jnp
        import numpy as np
        B, S, L = (2, 128, 128)
        DIM_Q, H, K, D_C, D_CQ, R = (256, 16, 128, 64, 192, 64)

        def _rope_tables(seq_len, dim, dtype):
            inv_freq = 1.0 / 10000.0 ** (jnp.arange(0, dim, 2, dtype=dtype) / dim)
            t = jnp.arange(seq_len, dtype=dtype)
            freqs = t[:, None] * inv_freq[None, :]
            sin = jnp.repeat(jnp.sin(freqs), 2, axis=-1)
            cos = jnp.repeat(jnp.cos(freqs), 2, axis=-1)
            return (sin, cos)

        def _rotate_half(x):
            h = x.shape[-1] // 2
            return jnp.concatenate([-x[..., h:], x[..., :h]], axis=-1)
        b, s, _ = hidden_q.shape
        l = kv_c.shape[1]
        q_hk = (hidden_q @ Wq.T).reshape(b, s, H, K)
        q_big = jnp.einsum('bshk,hkq->bshq', q_hk, w_kc_q)
        sin, cos = _rope_tables(l, D_C, kv_c.dtype)
        kv_rope = kv_c * cos[None] + _rotate_half(kv_c) * sin[None]
        q_r = jnp.einsum('bshq,hqr->bhsr', q_big, W_qr)
        k_r = jnp.einsum('bld,hdr->bhlr', kv_rope, W_kr)
        scores = jnp.einsum('bhsr,bhlr->bhsl', q_r, k_r)
        attn = jax.nn.softmax(scores, axis=-1)
        ctx_c = jnp.einsum('bhsl,bld->bhsd', attn, kv_rope)
        ctx_lat = jnp.einsum('bhsd,hkd->bshk', ctx_c, w_kc_kv)
        out = ctx_lat.reshape(b, s, H * K) @ Wo.T
        return out

    def _L2_ffn_ref(hidden_states, ln1_w, ln2_w, Wq, Wk, Wv, Wo, A, B, W_in_base, W_up_base, W_down):
        import jax, jax.numpy as jnp
        import numpy as np
        B_, S, D = (2, 256, 256)
        F_ = 1024
        R = 16
        H = 16
        HD = D // H
        MOD_SCALE = 0.1
        EPS = 1e-06

        def _rmsnorm(x, w):
            v = jnp.mean(x * x, axis=-1, keepdims=True)
            return x * jax.lax.rsqrt(v + EPS) * w

        def _attention(x, Wq, Wk, Wv, Wo):
            b, s, d = x.shape
            q = (x @ Wq.T).reshape(b, s, H, HD)
            k = (x @ Wk.T).reshape(b, s, H, HD)
            v = (x @ Wv.T).reshape(b, s, H, HD)
            scores = jnp.einsum('bqhd,bkhd->bhqk', q, k) / np.sqrt(HD).astype(np.float32)
            causal = jnp.tril(jnp.ones((s, s), bool))
            scores = jnp.where(causal, scores, jnp.finfo(scores.dtype).min)
            probs = jax.nn.softmax(scores, axis=-1)
            out = jnp.einsum('bhqk,bkhd->bqhd', probs, v).reshape(b, s, d)
            return out @ Wo.T
        residual = hidden_states
        x = _rmsnorm(hidden_states, ln1_w)
        attn = _attention(x, Wq, Wk, Wv, Wo)
        mod = MOD_SCALE * jnp.tanh(attn @ A)
        h = _rmsnorm(residual, ln2_w)
        gate_pre = h @ W_in_base.T + mod * (h @ A) @ B
        gate = jax.nn.silu(gate_pre)
        up = h @ W_up_base.T
        mlp_out = gate * up @ W_down.T
        return residual + mlp_out

    def _L3_attn_ref(x, Wq, Wkv, Wo, qk_temp):
        import jax, jax.numpy as jnp
        import numpy as np
        D_MODEL = 256
        H = 16
        HKV = 4
        DH = D_MODEL // H
        WINDOW = 32
        GROUP = H // HKV
        ROPE_BASE = 10000.0
        NEG_INF = -1e+30

        def _rotate_half(t):
            t1, t2 = jnp.split(t, 2, axis=-1)
            return jnp.concatenate([-t2, t1], axis=-1)

        def _apply_rope(q, k, positions):
            inv_freq = 1.0 / ROPE_BASE ** (jnp.arange(0, DH, 2, dtype=jnp.float32) / DH)
            ang = positions.astype(jnp.float32)[:, None] * inv_freq[None, :]
            cos = jnp.concatenate([jnp.cos(ang), jnp.cos(ang)], axis=-1)[None, None]
            sin = jnp.concatenate([jnp.sin(ang), jnp.sin(ang)], axis=-1)[None, None]
            q = q * cos + _rotate_half(q) * sin
            k = k * cos + _rotate_half(k) * sin
            return (q, k)
        B, L, _ = x.shape
        q = (x @ Wq.T).reshape(B, L, H, DH).transpose(0, 2, 1, 3)
        kv = (x @ Wkv.T).reshape(B, L, 2, HKV, DH).transpose(2, 0, 3, 1, 4)
        k, v = (kv[0], kv[1])
        positions = jnp.arange(L)
        q, k = _apply_rope(q, k, positions)
        k = jnp.repeat(k, GROUP, axis=1)
        v = jnp.repeat(v, GROUP, axis=1)
        q = q / jnp.linalg.norm(q, axis=-1, keepdims=True).clip(1e-12) * qk_temp[None]
        k = k / jnp.linalg.norm(k, axis=-1, keepdims=True).clip(1e-12)
        row = jnp.arange(L)[:, None]
        col = jnp.arange(L)[None, :]
        allowed = (row >= col) & (row - col < WINDOW)
        scores = jnp.einsum('bhqd,bhkd->bhqk', q, k)
        scores = jnp.where(allowed[None, None], scores, NEG_INF)
        attn = jax.nn.softmax(scores, axis=-1)
        out = jnp.einsum('bhqk,bhkd->bhqd', attn, v)
        out = out.transpose(0, 2, 1, 3).reshape(B, L, D_MODEL)
        return out @ Wo.T

    def _L3_xattn_ref(hidden_q, kv_c, Wq, w_kc_q, w_kc_kv, W_qr, W_kr, Wo):
        import jax, jax.numpy as jnp
        import numpy as np
        B, S, L = (2, 128, 128)
        DIM_Q, H, K, D_C, D_CQ, R = (256, 16, 128, 64, 192, 64)

        def _rope_tables(length, dim):
            inv = 1.0 / 10000.0 ** (jnp.arange(0, dim, 2, dtype=jnp.float32) / dim)
            f = jnp.arange(length, dtype=jnp.float32)[:, None] * inv[None, :]
            sin = jnp.repeat(jnp.sin(f), 2, axis=-1)
            cos = jnp.repeat(jnp.cos(f), 2, axis=-1)
            return (sin, cos)

        def _rotate_half(x):
            half = x.shape[-1] // 2
            return jnp.concatenate([-x[..., half:], x[..., :half]], axis=-1)

        def _apply_rope(x, sin, cos):
            return x * cos + _rotate_half(x) * sin
        Bv, Sv, _ = hidden_q.shape
        _, Lv, _ = kv_c.shape
        q_hk = (hidden_q @ Wq.T).reshape(Bv, Sv, H, K)
        q_big = jnp.einsum('bshk,hkq->bshq', q_hk, w_kc_q)
        sin_q, cos_q = _rope_tables(Sv, D_CQ)
        q_big = _apply_rope(q_big, sin_q[None, :, None, :], cos_q[None, :, None, :])
        sin_k, cos_k = _rope_tables(Lv, D_C)
        kv_r = _apply_rope(kv_c, sin_k[None], cos_k[None])
        q_r = jnp.einsum('bshq,hqr->bhsr', q_big, W_qr)
        k_r = jnp.einsum('bld,hdr->bhlr', kv_r, W_kr)
        scores = jnp.einsum('bhsr,bhlr->bhsl', q_r, k_r)
        attn = jax.nn.softmax(scores, axis=-1)
        ctx_c = jnp.einsum('bhsl,bld->bhsd', attn, kv_r)
        ctx_lat = jnp.einsum('bhsd,hkd->bhsk', ctx_c, w_kc_kv)
        ctx = ctx_lat.transpose(0, 2, 1, 3).reshape(Bv, Sv, H * K)
        return ctx @ Wo.T

    def _L3_ffn_ref(x, Wg, W1, W2, W3):
        import jax, jax.numpy as jnp
        import numpy as np
        TOP_K = 2
        E = Wg.shape[0]
        scores = jnp.einsum('btd,ed->bte', x, Wg)
        topk_s, topk_i = jax.lax.top_k(scores, TOP_K)
        probs = jax.nn.softmax(topk_s, axis=-1)
        onehot = (topk_i[..., None] == jnp.arange(E)).astype(x.dtype)
        w = jnp.einsum('btk,btke->bte', probs, onehot)
        y = jnp.zeros_like(x)
        for e in range(E):
            h = jax.nn.silu(jnp.einsum('btd,hd->bth', x, W1[e])) * jnp.einsum('btd,hd->bth', x, W2[e])
            y = y + w[..., e:e + 1] * jnp.einsum('bth,dh->btd', h, W3[e])
        return y
    x = _layernorm(x + _L0_attn_ref(x, L0_attn_w_qkv, L0_attn_b_qkv, L0_attn_w_out, L0_attn_b_out), axis=-1)
    x = _layernorm(x + _L0_xattn_ref(x, ctx_512, L0_xattn_Wq, L0_xattn_Wkv_expand, L0_xattn_Wout), axis=-1)
    x = _layernorm(x + _L0_ffn_ref(x, L0_ffn_gate_w, L0_ffn_w_gate, L0_ffn_w_up, L0_ffn_w_down, L0_ffn_sw_gate, L0_ffn_sw_up, L0_ffn_sw_down, L0_ffn_shared_gate_w), axis=-1)
    x = _layernorm(x + _L1_attn_ref(x, L1_attn_slope_rate, L1_attn_W_qkvu, L1_attn_W_out), axis=-1)
    x = _layernorm(x + _L1_xattn_ref(x, ctx_512, L1_xattn_Wq, L1_xattn_Wkv_expand, L1_xattn_Wout), axis=-1)
    x = _layernorm(x + _L1_ffn_ref(x, L1_ffn_Wr, L1_ffn_br, L1_ffn_Wg, L1_ffn_Wu, L1_ffn_Wd), axis=-1)
    x = _layernorm(x + _L2_attn_ref(x, L2_attn_q1_w, L2_attn_k1_w, L2_attn_q2_w, L2_attn_k2_w, L2_attn_v_w, L2_attn_o_w, L2_attn_lambda_param), axis=-1)
    x = _layernorm(x + _L2_xattn_ref(x, ctx_512, L2_xattn_Wq, L2_xattn_w_kc_q, L2_xattn_w_kc_kv, L2_xattn_W_qr, L2_xattn_W_kr, L2_xattn_Wo), axis=-1)
    x = _layernorm(x + _L2_ffn_ref(x, L2_ffn_ln1_w, L2_ffn_ln2_w, L2_ffn_Wq, L2_ffn_Wk, L2_ffn_Wv, L2_ffn_Wo, L2_ffn_A, L2_ffn_B, L2_ffn_W_in_base, L2_ffn_W_up_base, L2_ffn_W_down), axis=-1)
    x = _layernorm(x + _L3_attn_ref(x, L3_attn_Wq, L3_attn_Wkv, L3_attn_Wo, L3_attn_qk_temp), axis=-1)
    x = _layernorm(x + _L3_xattn_ref(x, ctx_512, L3_xattn_Wq, L3_xattn_w_kc_q, L3_xattn_w_kc_kv, L3_xattn_W_qr, L3_xattn_W_kr, L3_xattn_Wo), axis=-1)
    x = _layernorm(x + _L3_ffn_ref(x, L3_ffn_Wg, L3_ffn_W1, L3_ffn_W2, L3_ffn_W3), axis=-1)
    return x

_drawn_inputs = setup_inputs


def setup_inputs(seed=0):
    import zlib

    import numpy as np

    out = dict(_drawn_inputs(seed))
    spreads = {'L1_ffn_br': (0.0, 0.686),
     'L2_attn_lambda_param': (0.0615384615957737, 0.6),
     'L2_ffn_ln1_w': (1.0, 0.6),
     'L2_ffn_ln2_w': (1.0, 0.6),
     'L3_attn_qk_temp': (4.0, 0.6)}
    factors = {'L0_attn_b_qkv': 7.544,
     'L0_xattn_Wq': 21.604,
     'L0_ffn_gate_w': 2.686,
     'L0_ffn_w_up': 2.82,
     'L0_ffn_shared_gate_w': 5.126,
     'L1_xattn_Wq': 33.435,
     'L1_ffn_Wr': 4.155,
     'L1_ffn_Wg': 2.936,
     'L1_ffn_Wu': 2.737,
     'L1_ffn_Wd': 3.073,
     'L2_attn_k1_w': 3.316,
     'L2_attn_q2_w': 8.0,
     'L2_attn_k2_w': 8.0,
     'L2_ffn_Wq': 200.0,
     'L2_ffn_Wk': 200.0,
     'L2_ffn_Wv': 200.0,
     'L2_ffn_Wo': 200.0,
     'L2_ffn_A': 200.0,
     'L2_ffn_B': 200.0}
    for name, (base, spread) in spreads.items():
        noise = np.random.default_rng([zlib.crc32(name.encode()), seed]).standard_normal(out[name].shape)
        drawn = base * np.exp(spread * noise) if base else spread * noise
        out[name] = jnp.asarray(drawn.astype(out[name].dtype))
    for name, factor in factors.items():
        out[name] = (out[name] * factor).astype(out[name].dtype)
    return out
```

```python
from contextlib import ExitStack

import numpy as np

import concourse.bass as bass
from concourse import mybir

F32 = mybir.dt.float32
ALU = mybir.AluOpType
ACT = mybir.ActivationFunctionType
AX = mybir.AxisListType.X

P = 128
B, S, D = 4, 256, 256
T = S // P
KD = D // P
NH, HD = 16, 16
NK = 64
LN_EPS, RMS_EPS = 1e-5, 1e-6
NEG = -1e30
HID = 176


class Scope(ExitStack):

    def __init__(self, nc, name):
        super().__init__()
        self.nc, self.name, self.sems = nc, name, []

    def semaphore(self, name):
        self.sems.append(self.nc.alloc_semaphore(f"{self.name}_{name}"))
        return self.sems[-1]

    def __exit__(self, *failure):
        if failure[0] is None:
            self.nc.clear_and_free_semaphores(self.sems)
            self.nc.all_engine_barrier()
        return super().__exit__(*failure)


class Signal:

    def __init__(self, ctx, nc, name, per, credit=0):
        self.sem = ctx.semaphore(name)
        self.name, self.per, self.credit = name, per, credit

    def at(self, i, k):
        return i * self.per + (k + self.credit)

    def give(self, eng):
        eng.sem_inc(self.sem, self.credit)


class Accumulators:

    def __init__(self, ctx, nc, banks, fills, elsewhere=()):
        self.banks, self.fills, self.elsewhere = banks, fills, elsewhere
        self.full = Signal(ctx, nc, "acc_full", fills - len(elsewhere))
        self.empty = Signal(ctx, nc, "acc_empty", fills, credit=len(banks))

    def bank(self, k):
        return self.banks[k % len(self.banks)]

    def wait_empty(self, pe, i, k):
        pe.wait_ge(self.empty.sem, self.empty.at(i, k + 1 - len(self.banks)))

    def wait_full(self, act, i, k):
        before = sum(1 for f in self.elsewhere if f < k)
        act.wait_ge(self.full.sem, self.full.at(i, k + 1 - before))

    def wait_emptied(self, eng, i, k):
        eng.wait_ge(self.empty.sem, self.empty.at(i, k + 1))


class Chain:

    def __init__(self, counter, eng, i):
        self.counter, self.eng, self.i, self.k = counter, eng, i, 0

    def step(self, instruction):
        self.k += 1
        instruction.then_inc(self.counter.sem, 1)
        self.eng.wait_ge(self.counter.sem, self.counter.at(self.i, self.k))

    def done(self):
        assert self.k == self.counter.per, (self.counter.name, self.k, self.counter.per)



def ptile(a):
    k = a.shape[0] // P
    return a.reshape(k, P, -1).transpose(1, 0, 2).reshape(P, -1)


def pack(pieces):
    at, where, cols = 0, {}, []
    for name, a in pieces:
        a = a.reshape(a.shape[0], -1)
        if a.shape[0] < P:
            a = np.concatenate([a, np.zeros((P - a.shape[0], a.shape[1]), np.float32)])
        where[name] = (at, a.shape[1])
        at += a.shape[1]
        cols.append(a)
    return np.ascontiguousarray(np.concatenate(cols, axis=1)), where


def hidden_tiles(w, width):
    w = np.concatenate([w, np.zeros((D, width - w.shape[1]), np.float32)], axis=1)
    return w.reshape(KD, P, width // P, P).transpose(1, 2, 0, 3)


def xattn_small(wq, wkv, wo):
    wkT, wvT = wkv[:D].T, wkv[D:].T
    return [("wq", ptile(wq.T)), ("wo", ptile(wo.T)), ("wk", wkT), ("wv", wvT)]


def xattn_latent(wq, w_kc_q, w_kc_kv, w_qr, w_kr, wo, rope_q):
    q = w_kc_q.transpose(1, 0, 2) if rope_q else w_kc_q.transpose(2, 0, 1).reshape(2, 96, 16, P).transpose(1, 0, 2, 3)
    return [("wq", wq.reshape(NH, P, D).transpose(1, 0, 2)),
            ("kcq", q),
            ("kckv", w_kc_kv.transpose(1, 0, 2)),
            ("qr", w_qr.transpose(2, 0, 1)),
            ("kr", w_kr.transpose(2, 0, 1)),
            ("wo", wo.T.reshape(NH, P, D).transpose(1, 0, 2))]


def moe_weights(gate, g, u, d, width):
    if d is None:
        return [("gate", ptile(gate)), ("g", hidden_tiles(g, width)), ("u", hidden_tiles(u, width))]
    return [("gate", ptile(gate)), ("g", hidden_tiles(g, width)), ("u", hidden_tiles(u, width)),
            ("d", ptile(np.concatenate([d, np.zeros((width - d.shape[0], D), np.float32)])))]


def rope_angles(length, dim):
    inv = (1.0 / np.float32(10000.0) ** (np.arange(0, dim, 2, dtype=np.float32) / np.float32(dim))).astype(np.float32)
    return np.arange(length, dtype=np.float32)[:, None] * inv[None, :]


def owners(tiles, edges):
    e = np.zeros((len(edges), tiles * P), np.float32)
    lo = 0
    for n, hi in enumerate(edges):
        e[n, lo:hi] = 1.0
        lo = hi
    return e


def constants():
    p = np.arange(P)
    f = np.float32
    ident = np.eye(P, dtype=f)
    mask8 = (p[:, None] // HD == np.arange(8)).astype(f)
    par2 = ((p[:, None] // HD) % 2 == np.arange(2)).astype(f)
    half2 = (p[:, None] // NK == np.arange(2)).astype(f)
    causal = np.where(p[:, None] >= p[None, :], 0.0, NEG).astype(f)
    near = np.where((causal == 0) & (p[:, None] - p[None, :] < 32), 0.0, NEG).astype(f)
    before = np.where(p[:, None] + P - p[None, :] < 32, 0.0, NEG).astype(f)
    dist = np.maximum(np.arange(S)[None, :] - p[:, None], 0).astype(f)
    valid = (np.arange(S)[None, :] >= p[:, None]).astype(f)
    tri = (np.arange(8)[None, :] < np.arange(8)[:, None]).astype(f).reshape(1, 64).repeat(P, 0)
    ang = rope_angles(S, HD)
    cos = np.concatenate([np.cos(ang)] * 2, -1).reshape(T, P, HD).transpose(1, 0, 2)
    sin = np.concatenate([-np.sin(ang), np.sin(ang)], -1).reshape(T, P, HD).transpose(1, 0, 2)
    a = np.repeat(rope_angles(NK, 64), 2, axis=-1)
    kcos = np.cos(a)
    ksin = np.sin(a) * np.where(np.arange(64) < 32, -1.0, 1.0)
    kcos, ksin = (np.concatenate([t, t]).astype(f) for t in (kcos, ksin))
    return [("ident", ident), ("mask8", mask8), ("par2", par2), ("half2", half2), ("causal", causal),
            ("near", near), ("before", before), ("tri", tri), ("cos", cos.astype(f)), ("sin", sin.astype(f)),
            ("minus_half", np.full((P, 64), -0.5, f)), ("kcos", kcos), ("ksin", ksin)], dist, valid


def layouts(w):
    consts, dist, valid = constants()
    qa = np.repeat(rope_angles(S, 192), 2, axis=-1).T.reshape(2, 96, S).transpose(1, 0, 2)
    sign = np.array([-1.0, 1.0], np.float32)[None, :, None]
    qcos, qsin = np.cos(qa).astype(np.float32), (np.sin(qa) * sign).astype(np.float32)
    L = {}
    rows = lambda v: np.broadcast_to(v.reshape(1, -1), (P, v.size))
    L[0] = [("w", ptile(w["L0_attn_w_qkv"].T)), ("wo", ptile(w["L0_attn_w_out"].T)),
            ("b", rows(w["L0_attn_b_qkv"])), ("bo", rows(w["L0_attn_b_out"]))]
    L[1] = xattn_small(w["L0_xattn_Wq"], w["L0_xattn_Wkv_expand"], w["L0_xattn_Wout"])
    cat = lambda a: np.concatenate(list(a), axis=-1)
    L[2] = moe_weights(np.concatenate([w["L0_ffn_gate_w"].T, w["L0_ffn_shared_gate_w"]], axis=1),
                       np.concatenate([cat(w["L0_ffn_w_gate"]), w["L0_ffn_sw_gate"]], axis=1),
                       np.concatenate([cat(w["L0_ffn_w_up"]), w["L0_ffn_sw_up"]], axis=1),
                       np.concatenate([w["L0_ffn_w_down"].reshape(-1, D), w["L0_ffn_sw_down"]]), 17 * P)
    L[2].append(("owner", owners(17, [HID * (e + 1) for e in range(8)] + [8 * HID + 704])))
    L[3] = [("w", ptile(w["L1_attn_W_qkvu"].T)), ("wo", ptile(w["L1_attn_W_out"].T)),
            ("slope", rows(w["L1_attn_slope_rate"])), ("dist", dist), ("valid", valid)]
    L[4] = xattn_small(w["L1_xattn_Wq"], w["L1_xattn_Wkv_expand"], w["L1_xattn_Wout"])
    L[5] = moe_weights(w["L1_ffn_Wr"], cat(w["L1_ffn_Wg"]), cat(w["L1_ffn_Wu"]),
                       None, 32 * P) + [("br", rows(w["L1_ffn_br"]))]
    L[6] = [(n, ptile(w[f"L2_attn_{n}_w"].T)) for n in ("q1", "k1", "q2", "k2", "v", "o")] \
        + [("lam", rows(w["L2_attn_lambda_param"]))]
    L[7] = xattn_latent(*[w[f"L2_xattn_{n}"] for n in ("Wq", "w_kc_q", "w_kc_kv", "W_qr", "W_kr", "Wo")], False)
    L[8] = [("q", ptile(w["L2_ffn_Wq"].T)), ("k", ptile(w["L2_ffn_Wk"].T)), ("v", ptile(w["L2_ffn_Wv"].T)),
            ("o", ptile(w["L2_ffn_Wo"].T)), ("A", ptile(w["L2_ffn_A"])), ("B", w["L2_ffn_B"]),
            ("ln1", w["L2_ffn_ln1_w"].reshape(KD, P).T), ("ln2", w["L2_ffn_ln2_w"].reshape(KD, P).T),
            ("g", hidden_tiles(w["L2_ffn_W_in_base"].T, 1024)), ("u", hidden_tiles(w["L2_ffn_W_up_base"].T, 1024)),
            ("d", ptile(w["L2_ffn_W_down"].T))]
    overflow = {5: ptile(w["L1_ffn_Wd"].reshape(-1, D))}
    wk, wv = w["L3_attn_Wkv"][:64], w["L3_attn_Wkv"][64:]
    L[9] = [("w", ptile(np.concatenate([w["L3_attn_Wq"].T, wk.T, wv.T], axis=1))),
            ("wo", ptile(w["L3_attn_Wo"].T)), ("temp", rows(w["L3_attn_qk_temp"]))]
    L[10] = xattn_latent(*[w[f"L3_xattn_{n}"] for n in ("Wq", "w_kc_q", "w_kc_kv", "W_qr", "W_kr", "Wo")], True) \
        + [("qcos", qcos), ("qsin", qsin)]
    rowcat = lambda a: a.reshape(-1, a.shape[-1])
    L[11] = moe_weights(w["L3_ffn_Wg"].T, rowcat(w["L3_ffn_W1"]).T, rowcat(w["L3_ffn_W2"]).T,
                        w["L3_ffn_W3"].transpose(0, 2, 1).reshape(-1, D), 11 * P)
    L[11].append(("owner", owners(11, [HID * (e + 1) for e in range(8)])))
    return consts, L, overflow


SUBLAYERS = list(range(12))
SPARE = {3: NH * (S + P) + NH, 7: 4096, 10: 4096}
SPARE_AT = {3: 1600, 7: 10000, 10: 9900}


class Program:

    INPUT_LOADS = 16 * 6

    def __init__(self, nc, ctx, where, dram):
        self.nc, self.where, self.dram, self.order = nc, where, dram, where["order"]
        self.x = ctx.enter_context(nc.sbuf_tensor("x_all", [P, B, T, D], F32))
        self.const = ctx.enter_context(nc.sbuf_tensor("const", [P, where["const"]["size"]], F32))
        self.arena = [ctx.enter_context(nc.sbuf_tensor(f"weights{n}", [P, where["arena"][n]], F32)) for n in range(2)]
        self.ctxT = ctx.enter_context(nc.sbuf_tensor("ctxT", [NK, B, P], F32))
        self.ctx2 = ctx.enter_context(nc.sbuf_tensor("ctx2", [P, B, NK], F32))
        self.inputs_loaded = ctx.enter_context(nc.semaphore("inputs_loaded"))
        self.loaded = {n: ctx.enter_context(nc.semaphore(f"weights_loaded_{n}")) for n in where["order"]}
        self.stored = ctx.enter_context(nc.semaphore("stored"))
        self.bank = [ctx.enter_context(nc.psum_tensor(f"bank{n}", [P, 512], F32)) for n in range(8)]

    def c(self, name, *dims):
        at, n = self.where["const"][name]
        return shaped(self.const[:, at:at + n], dims)

    def w(self, n, name, *dims, rows=P):
        at, size = self.where[n][name]
        return shaped(self.arena[n % 2][0:rows, at:at + size], dims)

    def overflow(self, n, *dims):
        at, size = self.where["overflow"][n]
        return shaped(self.arena[1 - n % 2][:, at:at + size], dims)

    def over_weights(self, n, name, at, *dims):
        at += self.where[n][name][0]
        size = int(np.prod(dims))
        return shaped(self.arena[n % 2][:, at:at + size], dims)

    def spare(self, n, at, *dims, rows=P):
        at += SPARE_AT[n]
        size = int(np.prod(dims))
        return shaped(self.arena[1 - n % 2][0:rows, at:at + size], dims)


def shaped(ap, dims):
    if len(dims) < 2:
        return ap
    names = "abcdef"[:len(dims)]
    return ap.rearrange(f"p ({' '.join(names)}) -> p {' '.join(names)}", **dict(zip(names[1:], dims[1:])))


def over(ap, axis, n):
    ap = ap.unsqueeze(axis)
    shape = list(ap.shape)
    shape[axis] = n
    return ap.broadcast_to(shape)


def start(pg, eng, n):
    eng.wait_ge(pg.inputs_loaded, pg.INPUT_LOADS)
    eng.wait_ge(pg.loaded[n], 32 if n in pg.where["overflow"] else 16)


class Body:

    def __init__(self, pg, ctx, fills, vector_steps, name, roots=(), elsewhere=()):
        nc = self.nc = pg.nc
        self.pg = pg
        sb = lambda n, dims: ctx.enter_context(nc.sbuf_tensor(f"{name}_{n}", [P, *dims], F32))
        self.acc = Accumulators(ctx, nc, pg.bank[0:2], fills, elsewhere)
        self.x_staged = Signal(ctx, nc, "x_staged", 1)
        self.out_ready = Signal(ctx, nc, "out_ready", 1)
        self.out_taken = Signal(ctx, nc, "out_taken", 1, credit=1)
        self.vchain = Signal(ctx, nc, "vector_chain", vector_steps + 5)
        widths = [*roots, T]
        self.squares_ready = Signal(ctx, nc, "squares_ready", len(widths))
        self.roots_ready = Signal(ctx, nc, "roots_ready", len(widths))
        self.root = [ctx.enter_context(nc.sbuf_tensor(f"{name}_root{k}", [P, wd], F32)) for k, wd in enumerate(widths)]
        self.passed = Signal(ctx, nc, "passed", 2)
        self.xs = sb("xs", [T, D])
        self.xT = sb("xT", [KD, S])
        self.r = sb("r", [T, D])
        self.stats = sb("stats", [T, 6])
        self.mv = sb("mv", [T, 2])

    def stage(self, pool, i):
        self.nc.gpsimd.tensor_copy(self.xs[:], self.pg.x[:, i, :, :]).then_inc(self.x_staged.sem, 1)
        self.acc.wait_full(pool, i, 0)

    def roots(self, pool, i):
        for k, r in enumerate(self.root):
            pool.wait_ge(self.squares_ready.sem, self.squares_ready.at(i, k + 1))
            self.nc.gpsimd.tensor_tensor(r[:], r[:], self.pg.c("minus_half")[:, 0:r.shape[1]], ALU.pow)\
                .then_inc(self.roots_ready.sem, 1)

    def wait_root(self, eng, i, k):
        eng.wait_ge(self.roots_ready.sem, self.roots_ready.at(i, k + 1))

    def transpose_x(self, pe, i):
        pe.wait_ge(self.x_staged.sem, self.x_staged.at(i, 1))
        self.acc.wait_empty(pe, i, 0)
        transpose_tokens(self.nc, pe, self.acc.bank(0), self.xs, self.pg.c("ident")).then_inc(self.acc.full.sem, 1)

    def take_xT(self, act, i):
        self.acc.wait_full(act, i, 0)
        self.nc.scalar.activation(self.xT[:], shaped(self.acc.bank(0)[:], (KD, S)), ACT.Copy)\
            .then_inc(self.acc.empty.sem, 1)

    def project_out(self, pe, i, xT, w, bank, chunks, last_tile=None):
        pe.wait_ge(self.out_taken.sem, self.out_taken.at(i, 0))
        y = shaped(bank[:], (T, D))
        for t in range(T):
            for k in range(chunks):
                last = self.nc.tensor.matmul(y[:, t, :], xT[:, k, t * P:(t + 1) * P], w[:, k, :],
                                             start=(k == 0), stop=(k == chunks - 1))
        last.then_inc(self.out_ready.sem, 1)

    def add_norm(self, dve, i, chain, bank, x_times=1.0, wait_out=True, bias=None):
        nc = self.nc
        if wait_out:
            dve.wait_ge(self.out_ready.sem, self.out_ready.at(i, 1))
        nc.vector.scalar_tensor_tensor(out=self.r[:], in0=self.pg.x[:, i, :, :], scalar=float(x_times),
                                       in1=shaped(bank[:], (T, D)), op0=ALU.mult, op1=ALU.add)\
            .then_inc(self.out_taken.sem, 1)
        dve.wait_ge(self.out_taken.sem, self.out_taken.at(i, 1))
        if bias is not None:
            chain.step(nc.vector.tensor_tensor(self.r[:], self.r[:], over(bias, 1, T), ALU.add))
        self.norm(dve, i, chain)

    def norm(self, dve, i, chain):
        nc = self.nc
        for t in range(T):
            chain.step(nc.vector.bn_stats(self.stats[:, t, :], self.r[:, t, :]))
        dve.sem_inc(self.passed.sem, 1)
        for t in range(T):
            last_aggr = nc.vector.bn_aggr(self.mv[:, t, :], self.stats[:, t, :])
        chain.step(last_aggr)
        last = len(self.root) - 1
        nc.vector.tensor_scalar(self.root[last][:], self.mv[:, :, 1], LN_EPS, None, ALU.add)\
            .then_inc(self.squares_ready.sem, 1)
        self.wait_root(dve, i, last)
        for t in range(T):
            chain.step(nc.vector.tensor_scalar(self.pg.x[:, i, t, :], self.r[:, t, :], self.mv[:, t, 0:1],
                                               self.root[last][:, t:t + 1], ALU.subtract, ALU.mult))


def transpose_tokens(nc, pe, bank, src, ident, chunks=KD):
    for t in range(T):
        for k in range(chunks):
            last = nc.tensor.transpose(bank[:, k * S + t * P:k * S + (t + 1) * P],
                                       src[:, t, k * P:(k + 1) * P], ident)
    return last


def project_features(nc, bank, w, xT, tiles=KD):
    for m in range(tiles):
        for k in range(KD):
            last = nc.tensor.matmul(bank[:, m * S:(m + 1) * S], w[:, k, m * P:(m + 1) * P], xT[:, k, :],
                                    start=(k == 0), stop=(k == KD - 1))
    return last


def project_tokens(nc, out, w, xT, t):
    for k in range(KD):
        last = nc.tensor.matmul(out, xT[:, k, t * P:(t + 1) * P], w[:, k, :], start=(k == 0), stop=(k == KD - 1))
    return last


class Attention:
    SCORES, PROBS, TURNED = 2, 3, 3

    def __init__(self, pg, ctx, name, body, units, few_keys):
        nc = self.nc = pg.nc
        self.pg, self.body, self.units, self.few = pg, body, units, few_keys
        n = len(units)
        sig = lambda s, per, credit=0: Signal(ctx, nc, s, per, credit)
        sb = lambda s, dims: ctx.enter_context(nc.sbuf_tensor(f"{name}_{s}", [P, *dims], F32))
        self.s_bank, self.t_bank = pg.bank[2:4], pg.bank[5:7]
        self.scored = sig("scored", n)
        self.maxed = sig("maxed", n)
        self.probs_ready = sig("probs_ready", n, self.SCORES)
        self.transposed = sig("transposed", n, self.PROBS)
        self.turned = sig("turned", n, len(self.t_bank))
        self.valued = sig("valued", n, self.TURNED)
        self.probs = sb("probs", [self.PROBS, 512])
        self.probsT = sb("probsT", [self.TURNED, 512])
        heads = units[0]["heads"]
        self.nmax = sb("nmax", [n, heads])
        self.sums = sb("sums", [n, heads])
        self.rinv = sb("rinv", [n, heads])

    def credits_scalar(self, act):
        self.probs_ready.give(act)
        if self.few:
            self.turned.give(act)

    def credits_tensor(self, pe):
        self.transposed.give(pe)
        self.valued.give(pe)

    def credits_vector(self, dve):
        if not self.few:
            self.turned.give(dve)

    @staticmethod
    def chunks(unit):
        heads, keys = unit["heads"], unit["keys"]
        return max(1, heads * keys // P)

    def tensor(self, pe, i, score, value, before_values=None):
        n = len(self.units)
        for s in range(n + 3):
            if s < n:
                pe.wait_ge(self.probs_ready.sem, self.probs_ready.at(i, s + 1 - self.SCORES))
                score(s, self.units[s], self.s_bank[s % 2]).then_inc(self.scored.sem, 1)
            u = s - 2
            if 0 <= u < n:
                pe.wait_ge(self.probs_ready.sem, self.probs_ready.at(i, u + 1))
                pe.wait_ge(self.turned.sem, self.turned.at(i, u + 1 - 2))
                for c in range(self.chunks(self.units[u])):
                    last = self.nc.tensor.transpose(self.t_bank[u % 2][:, c * P:(c + 1) * P],
                                                    self.probs[:, u % self.PROBS, c * P:(c + 1) * P],
                                                    self.pg.c("ident"))
                last.then_inc(self.transposed.sem, 1)
            u = s - 3
            if 0 <= u < n:
                if u == 0 and before_values:
                    before_values()
                pe.wait_ge(self.turned.sem, self.turned.at(i, u + 1))
                value(u, self.units[u], self.probsT[:, u % self.TURNED, :]).then_inc(self.valued.sem, 1)

    def scalar(self, act, i):
        n = len(self.units)
        for s in range(n + 2):
            if s < n:
                unit = self.units[s]
                h, k = unit["heads"], unit["keys"]
                act.wait_ge(self.maxed.sem, self.maxed.at(i, s + 1))
                act.wait_ge(self.transposed.sem, self.transposed.at(i, s + 1 - self.PROBS))
                src, dst = self.s_bank[s % 2], self.probs[:, s % self.PROBS, :]
                if self.few:
                    last = self.nc.scalar.activation(dst[:, 0:h * k], src[:, 0:h * k], ACT.Exp)
                else:
                    for j in range(h):
                        last = self.nc.scalar.activation(dst[:, j * k:(j + 1) * k], src[:, j * k:(j + 1) * k], ACT.Exp,
                                                         bias=self.nmax[:, s, j:j + 1],
                                                         accum_out=self.sums[:, s, j:j + 1])
                last.then_inc(self.probs_ready.sem, 1)
            if self.few and s >= 2:
                self.turn(act, i, s - 2)

    def turn(self, eng, i, u):
        size = self.chunks(self.units[u]) * P
        eng.wait_ge(self.transposed.sem, self.transposed.at(i, u + 1))
        eng.wait_ge(self.valued.sem, self.valued.at(i, u + 1 - self.TURNED))
        dst, src = self.probsT[:, u % self.TURNED, 0:size], self.t_bank[u % 2][:, 0:size]
        if self.few:
            self.nc.scalar.activation(dst, src, ACT.Copy).then_inc(self.turned.sem, 1)
        else:
            self.nc.vector.tensor_copy(dst, src).then_inc(self.turned.sem, 1)

    def vector(self, dve, i, chain):
        n = len(self.units)
        nc = self.nc
        for s in range(n + 2):
            if s < n:
                unit = self.units[s]
                h, k = unit["heads"], unit["keys"]
                bank = shaped(self.s_bank[s % 2][:, 0:h * k], (h, k))
                dve.wait_ge(self.scored.sem, self.scored.at(i, s + 1))
                for lo, hi, mask in unit.get("masks", ()):
                    chain.step(nc.vector.tensor_tensor(bank[:, :, lo:hi], bank[:, :, lo:hi], over(mask, 1, h), ALU.add))
                if self.few:
                    chain.step(nc.vector.tensor_reduce(self.nmax[:, s, 0:h], bank, AX, ALU.max))
                    nc.vector.tensor_tensor(bank, bank, over(self.nmax[:, s, 0:h], 2, k), ALU.subtract)\
                        .then_inc(self.maxed.sem, 1)
                else:
                    nc.vector.tensor_reduce(self.nmax[:, s, 0:h], bank, AX, ALU.max, negate=True)\
                        .then_inc(self.maxed.sem, 1)
            u = s - 1
            if self.few and 0 <= u < n:
                h, k = self.units[u]["heads"], self.units[u]["keys"]
                dve.wait_ge(self.probs_ready.sem, self.probs_ready.at(i, u + 1))
                chain.step(nc.vector.tensor_reduce(self.sums[:, u, 0:h],
                                                   shaped(self.probs[:, u % self.PROBS, 0:h * k], (h, k)), AX, ALU.add))
            if not self.few and s >= 2:
                self.turn(dve, i, s - 2)
        dve.wait_ge(self.probs_ready.sem, self.probs_ready.at(i, n))
        h = self.units[0]["heads"]
        chain.step(nc.vector.reciprocal(self.rinv[:, :, 0:h], self.sums[:, :, 0:h]))

def attention_steps(units, few):
    return sum(len(u["masks"]) for u in units) + 1 + (2 * len(units) if few else 0)


def pair_units(masks_of, keys_of):
    return [{"t": t, "g": g, "heads": 2, "keys": keys_of[t], "masks": masks_of[t]} for t in range(T) for g in range(8)]


def pair_scores(nc, u, qT, kblk, bank):
    r, m, keys = 32 * (u["g"] % 4), u["g"] // 4, u["keys"]
    return nc.tensor.matmul(bank[:, 0:2 * keys], qT[r:r + 32, m, u["t"] * P:(u["t"] + 1) * P],
                            kblk[r:r + 32, m, :, 0:keys], start=True, stop=True)


def pair_values(nc, u, probsT, out, value_of):
    tiles = u["keys"] // P
    for j in range(2):
        head = 2 * u["g"] + j
        for c in range(tiles):
            at = (j * tiles + c) * P
            last = nc.tensor.matmul(out[:, u["t"] * D + head * HD:u["t"] * D + (head + 1) * HD],
                                    probsT[:, at:at + P], value_of(c, head), start=(c == 0), stop=(c == tiles - 1))
    return last


def spread_keys(nc, kblk, src, par2):
    for par in range(2):
        last = nc.scalar.activation(kblk[:, :, par, :], src, ACT.Copy, scale=par2[:, par:par + 1])
    return last


def flat(ap):
    names = "abcdef"[:len(ap.shape) - 1]
    return ap.rearrange(f"p {' '.join(names)} -> p ({' '.join(names)})")


def differential_attention(pg, n):
    nc = pg.nc
    with Scope(nc, f"s{n}") as ctx:
        base = pair_units([[], []], [S, S])
        units = [dict(u, which=w) for w in range(2) for u in base]
        body = Body(pg, ctx, 7, attention_steps(units, False) + 3, f"s{n}")
        att = Attention(pg, ctx, f"s{n}", body, units, few_keys=False)
        acc = body.acc
        sb = lambda s, dims: ctx.enter_context(nc.sbuf_tensor(f"s{n}_{s}", [P, *dims], F32))
        qT = [sb(f"q{w}T", [KD, S]) for w in range(2)]
        kblk = [sb(f"k{w}", [KD, 2, S]) for w in range(2)]
        v, o, second, oT = sb("v", [T, D]), sb("o", [T, D]), sb("second", [T, D]), sb("oT", [KD, S])
        lam_rinv = sb("lam_rinv", [T, NH])
        o_scaled = Signal(ctx, nc, "o_scaled", 1, credit=1)
        w = {k: pg.w(n, k, KD, D) for k in ("q1", "k1", "q2", "k2", "v", "o")}
        o_bank, y_bank = [pg.bank[7], pg.bank[4]], pg.bank[4]
        with nc.Block() as block:
            prefetch(pg, block, n)

            @block.gpsimd
            def _(pool):
                start(pg, pool, n)
                with pool.Fori(0, B) as i:
                    body.stage(pool, i)
                    body.roots(pool, i)

            @block.tensor
            def _(pe):
                start(pg, pe, n)
                att.credits_tensor(pe)
                with pe.Fori(0, B) as i:
                    body.transpose_x(pe, i)
                    acc.wait_emptied(pe, i, 0)
                    for k, name in ((1, "q1"), (2, "k1")):
                        acc.wait_empty(pe, i, k)
                        project_features(nc, acc.bank(k), w[name], body.xT).then_inc(acc.full.sem, 1)
                    acc.wait_empty(pe, i, 3)
                    for t in range(T):
                        last = project_tokens(nc, acc.bank(3)[:, t * D:(t + 1) * D], w["v"], body.xT, t)
                    last.then_inc(acc.full.sem, 1)
                    for k, name in ((4, "q2"), (5, "k2")):
                        acc.wait_empty(pe, i, k)
                        project_features(nc, acc.bank(k), w[name], body.xT).then_inc(acc.full.sem, 1)
                    acc.wait_emptied(pe, i, 5)

                    def before_values():
                        pe.wait_ge(o_scaled.sem, o_scaled.at(i, 0))
                        pe.wait_ge(body.out_taken.sem, body.out_taken.at(i, 0))
                    att.tensor(pe, i,
                               lambda s, u, bank: pair_scores(nc, u, qT[u["which"]], kblk[u["which"]], bank),
                               lambda s, u, probsT: pair_values(
                                   nc, u, probsT, o_bank[u["which"]],
                                   lambda c, head: v[:, c, head * HD:(head + 1) * HD]),
                               before_values)
                    pe.wait_ge(o_scaled.sem, o_scaled.at(i, 1))
                    acc.wait_empty(pe, i, 6)
                    transpose_tokens(nc, pe, acc.bank(6), o, pg.c("ident")).then_inc(acc.full.sem, 1)
                    acc.wait_emptied(pe, i, 6)
                    body.project_out(pe, i, oT, w["o"], y_bank, KD)

            @block.scalar
            def _(act):
                start(pg, act, n)
                acc.empty.give(act)
                att.credits_scalar(act)
                with act.Fori(0, B) as i:
                    body.take_xT(act, i)
                    for which, k in ((0, 1), (None, 3), (1, 4)):
                        acc.wait_full(act, i, k)
                        view = shaped(acc.bank(k)[:], (KD, S))
                        if which is None:
                            nc.scalar.activation(v[:], view, ACT.Copy).then_inc(acc.empty.sem, 1)
                            continue
                        nc.scalar.activation(qT[which][:], view, ACT.Copy, scale=0.25).then_inc(acc.empty.sem, 1)
                        acc.wait_full(act, i, k + 1)
                        spread_keys(nc, kblk[which], shaped(acc.bank(k + 1)[:], (KD, S)), pg.c("par2"))\
                            .then_inc(acc.empty.sem, 1)
                    att.scalar(act, i)
                    acc.wait_full(act, i, 6)
                    nc.scalar.activation(oT[:], shaped(acc.bank(6)[:], (KD, S)), ACT.Copy).then_inc(acc.empty.sem, 1)

            @block.vector
            def _(dve):
                start(pg, dve, n)
                body.out_taken.give(dve)
                o_scaled.give(dve)
                att.credits_vector(dve)
                heads = lambda ap: ap.rearrange("p (h d) -> p h d", d=HD)
                with dve.Fori(0, B) as i:
                    chain = Chain(body.vchain, dve, i)
                    att.vector(dve, i, chain)
                    chain.step(nc.vector.scalar_tensor_tensor(
                        out=lam_rinv[:], in0=shaped(flat(att.rinv[:, 16:32, :]), (T, NH)), scalar=-1.0,
                        in1=over(pg.w(n, "lam"), 1, T), op0=ALU.mult, op1=ALU.mult))
                    dve.wait_ge(att.valued.sem, att.valued.at(i, len(units)))
                    chain.step(nc.vector.tensor_tensor(heads(flat(second[:])), heads(o_bank[1][:]),
                                                       over(flat(lam_rinv[:]), 2, HD), ALU.mult))
                    chain.step(nc.vector.tensor_tensor(heads(flat(o[:])), heads(o_bank[0][:]),
                                                       over(flat(att.rinv[:, 0:16, :]), 2, HD), ALU.mult))
                    nc.vector.tensor_tensor(o[:], o[:], second[:], ALU.add).then_inc(o_scaled.sem, 1)
                    body.add_norm(dve, i, chain, y_bank)
                    chain.done()


class GatedTiles:
    SLOTS = 3

    def __init__(self, pg, ctx, name, tiles, gu_banks, w_banks=()):
        self.nc, self.tiles, self.banks, self.w_banks = pg.nc, tiles, gu_banks, w_banks
        sig = lambda s, credit=0: Signal(ctx, pg.nc, s, tiles, credit)
        sb = lambda s, dims: ctx.enter_context(pg.nc.sbuf_tensor(f"{name}_{s}", [P, *dims], F32))
        self.gu_full = sig("gu_full")
        self.tanh_ready = sig("tanh_ready")
        self.half_done = sig("half_done")
        self.hidden_ready = sig("hidden_ready", len(gu_banks))
        self.down_done = sig("down_done", self.SLOTS)
        self.tanh, self.half = sb("tanh", [2, S]), sb("half", [2, S])
        self.hidden = sb("hidden", [self.SLOTS, S])
        if w_banks:
            self.w_full = sig("w_full")
            self.w_ready = sig("w_ready", 2)
            self.scaled_ready = sig("scaled_ready", self.SLOTS)
            self.wsb, self.scaled = sb("wsb", [2, S]), sb("scaled", [self.SLOTS, S])
        self.down_src = self.scaled if w_banks else self.hidden
        self.down_ready = self.scaled_ready if w_banks else self.hidden_ready

    def credits(self, pe=None, act=None, dve=None, pool=None):
        if pe:
            self.down_done.give(pe)
        if act and self.w_banks:
            self.w_ready.give(act)
        if dve:
            self.hidden_ready.give(dve)
        if pool and self.w_banks:
            self.scaled_ready.give(pool)

    def gate_up(self, pe, i, g, xT, wg, wu, extra=None):
        pe.wait_ge(self.hidden_ready.sem, self.hidden_ready.at(i, g + 1 - len(self.banks)))
        bank = self.banks[g % len(self.banks)]
        for half, w in enumerate((wg, wu)):
            out = bank[:, half * S:(half + 1) * S]
            for k in range(KD):
                more = extra if half == 0 else None
                last = self.nc.tensor.matmul(out, w[:, g, k, :], xT[:, k, :], start=(k == 0),
                                             stop=(k == KD - 1 and not more))
            if more:
                more(out, g)
        last.then_inc(self.gu_full.sem, 1)

    def spread_weights(self, pe, i, g, owner, combT):
        pe.wait_ge(self.w_ready.sem, self.w_ready.at(i, g + 1 - 2))
        self.nc.tensor.matmul(self.w_banks[g % 2][:, 0:S], owner[:, g * P:(g + 1) * P], combT, start=True, stop=True)\
            .then_inc(self.w_full.sem, 1)

    def down(self, pe, i, g, wd, bank, first, last_one):
        pe.wait_ge(self.down_ready.sem, self.down_ready.at(i, g + 1))
        y = shaped(bank[:], (T, D))
        for t in range(T):
            last = self.nc.tensor.matmul(y[:, t, :], self.down_src[:, g % self.SLOTS, t * P:(t + 1) * P], wd[:, g, :],
                                         start=(first and t == 0), stop=last_one, skip_group_check=True)
        last.then_inc(self.down_done.sem, 1)
        return last

    def scalar(self, act, i, g):
        act.wait_ge(self.gu_full.sem, self.gu_full.at(i, g + 1))
        act.wait_ge(self.hidden_ready.sem, self.hidden_ready.at(i, g + 1 - 2))
        self.nc.scalar.activation(self.tanh[:, g % 2, :], self.banks[g % len(self.banks)][:, 0:S], ACT.Tanh, scale=0.5)\
            .then_inc(self.tanh_ready.sem, 1)

    def scalar_weights(self, act, i, g):
        act.wait_ge(self.w_full.sem, self.w_full.at(i, g + 1))
        act.wait_ge(self.scaled_ready.sem, self.scaled_ready.at(i, g + 1 - 2))
        self.nc.scalar.activation(self.wsb[:, g % 2, :], self.w_banks[g % 2][:, 0:S], ACT.Copy).then_inc(self.w_ready.sem, 1)

    def vector(self, dve, i, g):
        bank = self.banks[g % len(self.banks)]
        dve.wait_ge(self.tanh_ready.sem, self.tanh_ready.at(i, g + 1))
        self.nc.vector.scalar_tensor_tensor(out=self.half[:, g % 2, :], in0=self.tanh[:, g % 2, :], scalar=1.0,
                                            in1=bank[:, 0:S], op0=ALU.add, op1=ALU.mult).then_inc(self.half_done.sem, 1)
        dve.wait_ge(self.half_done.sem, self.half_done.at(i, g + 1))
        freed = self.scaled_ready if self.w_banks else self.down_done
        dve.wait_ge(freed.sem, freed.at(i, g + 1 - self.SLOTS))
        self.nc.vector.scalar_tensor_tensor(out=self.hidden[:, g % self.SLOTS, :], in0=self.half[:, g % 2, :], scalar=0.5,
                                            in1=bank[:, S:2 * S], op0=ALU.mult, op1=ALU.mult)\
            .then_inc(self.hidden_ready.sem, 1)

    def pool(self, pool, i, g):
        pool.wait_ge(self.w_ready.sem, self.w_ready.at(i, g + 1))
        pool.wait_ge(self.hidden_ready.sem, self.hidden_ready.at(i, g + 1))
        pool.wait_ge(self.down_done.sem, self.down_done.at(i, g + 1 - self.SLOTS))
        self.nc.gpsimd.tensor_tensor(self.scaled[:, g % self.SLOTS, :], self.hidden[:, g % self.SLOTS, :],
                                     self.wsb[:, g % 2, :], ALU.mult).then_inc(self.scaled_ready.sem, 1)


class Routing:

    def __init__(self, pg, ctx, name, experts, top, shared, over_all, bias=None):
        nc = self.nc = pg.nc
        self.pg, self.E, self.top, self.shared, self.over_all, self.bias = pg, experts, top, shared, over_all, bias
        self.cols = experts + (1 if shared else 0)
        sb = lambda s, dims: ctx.enter_context(nc.sbuf_tensor(f"{name}_{s}", [P, *dims], F32))
        E = experts
        self.logits, self.comb = sb("logits", [T, self.cols]), sb("comb", [T, self.cols])
        self.beats, self.ties = sb("beats", [T, E, E]), sb("ties", [T, E, E])
        self.rank, self.top1, self.shifted = sb("rank", [T, E]), sb("top1", [T]), sb("shifted", [T, self.cols])
        self.exps, self.total = sb("exps", [T, self.cols]), sb("total", [T])
        self.shifted_ready = Signal(ctx, nc, "shifted_ready", 1)
        self.exps_ready = Signal(ctx, nc, "exps_ready", 1)
        self.comb_ready = Signal(ctx, nc, "comb_ready", 1)
        self.steps = 9 + (1 if bias is not None else 0) + (2 if shared else 0)

    def project(self, pe, i, acc, k, xT, gate):
        for t in range(T):
            last = project_tokens(self.nc, acc.bank(k)[:, t * self.cols:(t + 1) * self.cols], gate, xT, t)
        last.then_inc(acc.full.sem, 1)

    def take_logits(self, act, i, acc, k):
        acc.wait_full(act, i, k)
        self.nc.scalar.activation(self.logits[:], shaped(acc.bank(k)[:, 0:T * self.cols], (T, self.cols)), ACT.Copy)\
            .then_inc(acc.empty.sem, 1)

    def scalar(self, act, i):
        act.wait_ge(self.shifted_ready.sem, self.shifted_ready.at(i, 1))
        self.nc.scalar.activation(self.exps[:], self.shifted[:], ACT.Exp).then_inc(self.exps_ready.sem, 1)

    def vector(self, dve, i, chain, acc, k):
        nc, E = self.nc, self.E
        acc.wait_emptied(dve, i, k)
        l = self.logits[:, :, 0:E]
        if self.bias is not None:
            chain.step(nc.vector.tensor_tensor(l, l, over(self.bias, 1, T), ALU.add))
        for t in range(T):
            mine, other = over(l[:, t, :], 2, E), over(l[:, t, :], 1, E)
            nc.vector.tensor_tensor(self.beats[:, t, :, :], other, mine, ALU.is_gt)
            last = nc.vector.tensor_tensor(self.ties[:, t, :, :], other, mine, ALU.is_equal)
        chain.step(last)
        tri = shaped(self.pg.c("tri"), (8, 8))[:, 0:E, 0:E]
        chain.step(nc.vector.tensor_tensor(self.ties[:], self.ties[:], over(tri, 1, T), ALU.mult))
        chain.step(nc.vector.tensor_tensor(self.beats[:], self.beats[:], self.ties[:], ALU.add))
        chain.step(nc.vector.tensor_reduce(self.rank[:], self.beats[:], AX, ALU.add))
        chain.step(nc.vector.tensor_reduce(self.top1[:], l, AX, ALU.max))
        if self.shared:
            chain.step(nc.vector.tensor_scalar(self.shifted[:, :, E:E + 1], self.logits[:, :, E:E + 1], -1.0, None, ALU.mult))
        nc.vector.tensor_tensor(self.shifted[:, :, 0:E], l, over(self.top1[:], 2, E), ALU.subtract)\
            .then_inc(self.shifted_ready.sem, 1)
        chain.step(nc.vector.tensor_scalar(self.rank[:], self.rank[:], float(self.top), None, ALU.is_lt))
        dve.wait_ge(self.exps_ready.sem, self.exps_ready.at(i, 1))
        e, c = self.exps[:, :, 0:E], self.comb[:, :, 0:E]
        chain.step(nc.vector.tensor_tensor(c, e, self.rank[:], ALU.mult))
        chain.step(nc.vector.tensor_reduce(self.total[:], e if self.over_all else c, AX, ALU.add))
        chain.step(nc.vector.reciprocal(self.total[:], self.total[:]))
        if self.shared:
            z = self.comb[:, :, E:E + 1]
            chain.step(nc.vector.tensor_scalar(z, self.exps[:, :, E:E + 1], 1.0, None, ALU.add))
            nc.vector.reciprocal(z, z)
        nc.vector.tensor_tensor(c, c, over(self.total[:], 2, E), ALU.mult).then_inc(self.comb_ready.sem, 1)


def weighted_experts(pg, n, experts, top, shared, tiles):
    nc = pg.nc
    with Scope(nc, f"s{n}") as ctx:
        route = Routing(pg, ctx, f"s{n}", experts, top, shared, over_all=False)
        body = Body(pg, ctx, 3, route.steps, f"s{n}")
        acc = body.acc
        ff = GatedTiles(pg, ctx, f"s{n}", tiles, [pg.bank[2], pg.bank[3], pg.bank[7]], pg.bank[5:7])
        cols = route.cols
        combT = ctx.enter_context(nc.sbuf_tensor(f"s{n}_combT", [cols, S], F32))
        gate = pg.w(n, "gate", KD, cols)
        wg, wu, wd = pg.w(n, "g", tiles, KD, P), pg.w(n, "u", tiles, KD, P), pg.w(n, "d", tiles, D)
        owner, y_bank = pg.w(n, "owner", rows=cols), pg.bank[4]
        with nc.Block() as block:
            prefetch(pg, block, n)

            @block.gpsimd
            def _(pool):
                start(pg, pool, n)
                ff.credits(pool=pool)
                with pool.Fori(0, B) as i:
                    body.stage(pool, i)
                    for g in range(tiles):
                        ff.pool(pool, i, g)
                    body.roots(pool, i)

            @block.tensor
            def _(pe):
                start(pg, pe, n)
                ff.credits(pe=pe)
                with pe.Fori(0, B) as i:
                    body.transpose_x(pe, i)
                    acc.wait_emptied(pe, i, 0)
                    acc.wait_empty(pe, i, 1)
                    route.project(pe, i, acc, 1, body.xT, gate)
                    for s in range(tiles + 3):
                        if s < tiles:
                            ff.gate_up(pe, i, s, body.xT, wg, wu)
                        if s == 2:
                            pe.wait_ge(route.comb_ready.sem, route.comb_ready.at(i, 1))
                            acc.wait_empty(pe, i, 2)
                            for t in range(T):
                                last = nc.tensor.transpose(acc.bank(2)[0:cols, t * P:(t + 1) * P], route.comb[:, t, :],
                                                           pg.c("ident"))
                            last.then_inc(acc.full.sem, 1)
                            acc.wait_emptied(pe, i, 2)
                        if 0 <= s - 2 < tiles:
                            ff.spread_weights(pe, i, s - 2, owner, combT[:])
                        if s == 3:
                            pe.wait_ge(body.out_taken.sem, body.out_taken.at(i, 0))
                        if 0 <= s - 3 < tiles:
                            ff.down(pe, i, s - 3, wd, y_bank, first=(s == 3), last_one=(s - 3 == tiles - 1))

            @block.scalar
            def _(act):
                start(pg, act, n)
                acc.empty.give(act)
                ff.credits(act=act)
                with act.Fori(0, B) as i:
                    body.take_xT(act, i)
                    route.take_logits(act, i, acc, 1)
                    ff.scalar(act, i, 0)
                    route.scalar(act, i)
                    acc.wait_full(act, i, 2)
                    nc.scalar.activation(combT[:], acc.bank(2)[0:cols, 0:S], ACT.Copy).then_inc(acc.empty.sem, 1)
                    for g in range(tiles):
                        if g:
                            ff.scalar(act, i, g)
                        ff.scalar_weights(act, i, g)

            @block.vector
            def _(dve):
                start(pg, dve, n)
                body.out_taken.give(dve)
                ff.credits(dve=dve)
                with dve.Fori(0, B) as i:
                    chain = Chain(body.vchain, dve, i)
                    route.vector(dve, i, chain, acc, 1)
                    for g in range(tiles):
                        ff.vector(dve, i, g)
                    dve.wait_ge(ff.down_done.sem, ff.down_done.at(i, tiles))
                    body.add_norm(dve, i, chain, y_bank, wait_out=False)
                    chain.done()


def top1_experts(pg, n):
    nc = pg.nc
    E, per, tiles = 4, 8, 32
    with Scope(nc, f"s{n}") as ctx:
        route = Routing(pg, ctx, f"s{n}", E, 1, False, over_all=True, bias=pg.w(n, "br"))
        body = Body(pg, ctx, 2, route.steps, f"s{n}")
        acc = body.acc
        ff = GatedTiles(pg, ctx, f"s{n}", tiles, [pg.bank[2], pg.bank[3], pg.bank[5]])
        gate = pg.w(n, "gate", KD, E)
        wg, wu, wd = pg.w(n, "g", tiles, KD, P), pg.w(n, "u", tiles, KD, P), pg.overflow(n, tiles, D)
        y_banks = [pg.bank[4], pg.bank[7]]
        expert_taken = Signal(ctx, nc, "expert_taken", E, credit=2)
        with nc.Block() as block:
            prefetch(pg, block, n)

            @block.gpsimd
            def _(pool):
                start(pg, pool, n)
                with pool.Fori(0, B) as i:
                    body.stage(pool, i)
                    body.roots(pool, i)

            @block.tensor
            def _(pe):
                start(pg, pe, n)
                ff.credits(pe=pe)
                with pe.Fori(0, B) as i:
                    body.transpose_x(pe, i)
                    acc.wait_emptied(pe, i, 0)
                    acc.wait_empty(pe, i, 1)
                    route.project(pe, i, acc, 1, body.xT, gate)
                    for s in range(tiles + 2):
                        if s < tiles:
                            ff.gate_up(pe, i, s, body.xT, wg, wu)
                        g = s - 2
                        if 0 <= g < tiles:
                            e = g // per
                            if g % per == 0:
                                pe.wait_ge(expert_taken.sem, expert_taken.at(i, e + 1 - 2))
                            ff.down(pe, i, g, wd, y_banks[e % 2], first=(g % per == 0), last_one=(g % per == per - 1))

            @block.scalar
            def _(act):
                start(pg, act, n)
                acc.empty.give(act)
                with act.Fori(0, B) as i:
                    body.take_xT(act, i)
                    route.take_logits(act, i, acc, 1)
                    ff.scalar(act, i, 0)
                    route.scalar(act, i)
                    for g in range(1, tiles):
                        ff.scalar(act, i, g)

            @block.vector
            def _(dve):
                start(pg, dve, n)
                expert_taken.give(dve)
                ff.credits(dve=dve)
                with dve.Fori(0, B) as i:
                    chain = Chain(body.vchain, dve, i)
                    route.vector(dve, i, chain, acc, 1)

                    def take(e):
                        dve.wait_ge(ff.down_done.sem, ff.down_done.at(i, (e + 1) * per))
                        y = shaped(y_banks[e % 2][:], (T, D))
                        for t in range(T):
                            before = pg.x[:, i, t, :] if e == 0 else body.r[:, t, :]
                            last = nc.vector.scalar_tensor_tensor(out=body.r[:, t, :], in0=y[:, t, :],
                                                                  scalar=route.comb[:, t, e:e + 1], in1=before,
                                                                  op0=ALU.mult, op1=ALU.add)
                        last.then_inc(expert_taken.sem, 1)
                        dve.wait_ge(expert_taken.sem, expert_taken.at(i, e + 1))
                    dve.wait_ge(route.comb_ready.sem, route.comb_ready.at(i, 1))
                    for g in range(tiles):
                        ff.vector(dve, i, g)
                        if g % per == 3 and g > per:
                            take(g // per - 1)
                    take(E - 1)
                    body.norm(dve, i, chain)
                    chain.done()


def modulated_ffn(pg, n):
    nc = pg.nc
    R, tiles = 16, 8
    with Scope(nc, f"s{n}") as ctx:
        causal = pg.c("causal")
        units = pair_units([[(0, P, causal)], [(P, S, causal)]], [P, S])
        body = Body(pg, ctx, 7, attention_steps(units, False), f"s{n}", roots=(T,))
        att = Attention(pg, ctx, f"s{n}", body, units, few_keys=False)
        ff = GatedTiles(pg, ctx, f"s{n}", tiles, pg.bank[2:4])
        acc = body.acc
        sb = lambda s, dims, p=P: ctx.enter_context(nc.sbuf_tensor(f"s{n}_{s}", [p, *dims], F32))
        x_rms, h1T, h2T = sb("x_rms", [T, D]), sb("h1T", [KD, S]), sb("h2T", [KD, S])
        squares, sumsq = sb("squares", [T, D]), sb("sumsq", [T])
        qT, kblk, v = sb("qT", [KD, S]), sb("kblk", [KD, 2, S]), sb("v", [T, D])
        o, oT, attnT = sb("o", [T, D]), sb("oT", [KD, S]), sb("attnT", [KD, S])
        mod, hA, prod = sb("mod", [S], R), sb("hA", [S], R), sb("prod", [S], R)
        o_scaled = Signal(ctx, nc, "o_scaled", 1, credit=1)
        summed = Signal(ctx, nc, "summed", 1)
        rms_ready = Signal(ctx, nc, "rms_ready", 1)
        mod_ready = Signal(ctx, nc, "mod_ready", 1)
        w = {k: pg.w(n, k, KD, D) for k in ("q", "k", "v", "o")}
        A, Bw = pg.w(n, "A", KD, R), pg.w(n, "B", rows=R)
        wg, wu, wd = pg.w(n, "g", tiles, KD, P), pg.w(n, "u", tiles, KD, P), pg.w(n, "d", tiles, D)
        o_bank, y_bank = pg.bank[7], pg.bank[4]
        with nc.Block() as block:
            prefetch(pg, block, n)

            @block.gpsimd
            def _(pool):
                start(pg, pool, n)
                with pool.Fori(0, B) as i:
                    nc.gpsimd.tensor_copy(body.xs[:], pg.x[:, i, :, :]).then_inc(body.x_staged.sem, 1)
                    body.roots(pool, i)

            @block.tensor
            def _(pe):
                start(pg, pe, n)
                att.credits_tensor(pe)
                ff.credits(pe=pe)
                with pe.Fori(0, B) as i:
                    pe.wait_ge(rms_ready.sem, rms_ready.at(i, 1))
                    acc.wait_empty(pe, i, 0)
                    transpose_tokens(nc, pe, acc.bank(0), x_rms, pg.c("ident")).then_inc(acc.full.sem, 1)
                    acc.wait_emptied(pe, i, 0)
                    for k, name in ((1, "q"), (2, "k")):
                        acc.wait_empty(pe, i, k)
                        project_features(nc, acc.bank(k), w[name], h1T).then_inc(acc.full.sem, 1)
                    acc.wait_empty(pe, i, 3)
                    for t in range(T):
                        last = project_tokens(nc, acc.bank(3)[:, t * D:(t + 1) * D], w["v"], h1T, t)
                    last.then_inc(acc.full.sem, 1)
                    acc.wait_emptied(pe, i, 3)
                    att.tensor(pe, i, lambda s, u, bank: pair_scores(nc, u, qT, kblk, bank),
                               lambda s, u, probsT: pair_values(nc, u, probsT, o_bank,
                                                                lambda c, head: v[:, c, head * HD:(head + 1) * HD]),
                               lambda: pe.wait_ge(o_scaled.sem, o_scaled.at(i, 0)))
                    pe.wait_ge(o_scaled.sem, o_scaled.at(i, 1))
                    acc.wait_empty(pe, i, 4)
                    transpose_tokens(nc, pe, acc.bank(4), o, pg.c("ident")).then_inc(acc.full.sem, 1)
                    acc.wait_emptied(pe, i, 4)
                    acc.wait_empty(pe, i, 5)
                    project_features(nc, acc.bank(5), w["o"], oT).then_inc(acc.full.sem, 1)
                    acc.wait_emptied(pe, i, 5)
                    acc.wait_empty(pe, i, 6)
                    for half, src in enumerate((attnT, h2T)):
                        for k in range(KD):
                            last = nc.tensor.matmul(acc.bank(6)[0:R, half * S:(half + 1) * S], A[:, k, :], src[:, k, :],
                                                    start=(k == 0), stop=(k == KD - 1))
                    last.then_inc(acc.full.sem, 1)

                    def modulate(out, g):
                        if g == 0:
                            pe.wait_ge(mod_ready.sem, mod_ready.at(i, 1))
                        return nc.tensor.matmul(out, Bw[:, g * P:(g + 1) * P], prod[:], start=False, stop=True)
                    for s in range(tiles + 2):
                        if s < tiles:
                            ff.gate_up(pe, i, s, h2T, wg, wu, extra=modulate)
                        if s == 2:
                            pe.wait_ge(body.out_taken.sem, body.out_taken.at(i, 0))
                        if s >= 2:
                            ff.down(pe, i, s - 2, wd, y_bank, first=(s == 2), last_one=(s == tiles + 1))

            @block.scalar
            def _(act):
                start(pg, act, n)
                acc.empty.give(act)
                att.credits_scalar(act)
                with act.Fori(0, B) as i:
                    act.wait_ge(body.x_staged.sem, body.x_staged.at(i, 1))
                    for t in range(T):
                        last = nc.scalar.activation(squares[:, t, :], body.xs[:, t, :], ACT.Square,
                                                    accum_out=sumsq[:, t:t + 1])
                    last.then_inc(summed.sem, 1)
                    acc.wait_full(act, i, 0)
                    for name, dst in (("ln1", h1T), ("ln2", h2T)):
                        for k in range(KD):
                            last = nc.scalar.activation(dst[:, k, :], acc.bank(0)[:, k * S:(k + 1) * S], ACT.Copy,
                                                        scale=pg.w(n, name)[:, k:k + 1])
                    last.then_inc(acc.empty.sem, 1)
                    view = lambda k: shaped(acc.bank(k)[:], (KD, S))
                    acc.wait_full(act, i, 1)
                    nc.scalar.activation(qT[:], view(1), ACT.Copy, scale=0.25).then_inc(acc.empty.sem, 1)
                    acc.wait_full(act, i, 2)
                    spread_keys(nc, kblk, view(2), pg.c("par2")).then_inc(acc.empty.sem, 1)
                    acc.wait_full(act, i, 3)
                    nc.scalar.activation(v[:], view(3), ACT.Copy).then_inc(acc.empty.sem, 1)
                    att.scalar(act, i)
                    for k, dst in ((4, oT), (5, attnT)):
                        acc.wait_full(act, i, k)
                        nc.scalar.activation(dst[:], view(k), ACT.Copy).then_inc(acc.empty.sem, 1)
                    acc.wait_full(act, i, 6)
                    nc.scalar.activation(mod[:], acc.bank(6)[0:R, 0:S], ACT.Tanh)
                    nc.scalar.activation(hA[:], acc.bank(6)[0:R, S:2 * S], ACT.Copy).then_inc(acc.empty.sem, 1)
                    for g in range(tiles):
                        ff.scalar(act, i, g)

            @block.vector
            def _(dve):
                start(pg, dve, n)
                body.out_taken.give(dve)
                o_scaled.give(dve)
                att.credits_vector(dve)
                ff.credits(dve=dve)
                with dve.Fori(0, B) as i:
                    chain = Chain(body.vchain, dve, i)
                    dve.wait_ge(summed.sem, summed.at(i, 1))
                    nc.vector.tensor_scalar(body.root[0][:], sumsq[:], 1.0 / D, RMS_EPS, ALU.mult, ALU.add)\
                        .then_inc(body.squares_ready.sem, 1)
                    body.wait_root(dve, i, 0)
                    nc.vector.tensor_tensor(x_rms[:], body.xs[:], over(body.root[0][:], 2, D), ALU.mult)\
                        .then_inc(rms_ready.sem, 1)
                    att.vector(dve, i, chain)
                    dve.wait_ge(att.valued.sem, att.valued.at(i, len(units)))
                    nc.vector.tensor_tensor(flat(o[:]).rearrange("p (h d) -> p h d", d=HD),
                                            o_bank[:].rearrange("p (h d) -> p h d", d=HD),
                                            over(flat(att.rinv[:]), 2, HD), ALU.mult).then_inc(o_scaled.sem, 1)
                    acc.wait_emptied(dve, i, 6)
                    nc.vector.scalar_tensor_tensor(out=prod[:], in0=mod[:], scalar=0.1, in1=hA[:],
                                                   op0=ALU.mult, op1=ALU.mult).then_inc(mod_ready.sem, 1)
                    for g in range(tiles):
                        ff.vector(dve, i, g)
                    dve.wait_ge(ff.down_done.sem, ff.down_done.at(i, tiles))
                    body.add_norm(dve, i, chain, y_bank, x_times=2.0, wait_out=False)
                    chain.done()


def windowed_attention(pg, n):
    nc = pg.nc
    HK = 4
    H = NH + HK
    with Scope(nc, f"s{n}") as ctx:
        near, before = pg.c("near"), pg.c("before")
        units = pair_units([[(0, P, near)], [(0, P, before), (P, S, near)]], [P, S])
        body = Body(pg, ctx, 6, attention_steps(units, False) + 7, f"s{n}", roots=(T * H,))
        att = Attention(pg, ctx, f"s{n}", body, units, few_keys=False)
        acc = body.acc
        sb = lambda s, dims: ctx.enter_context(nc.sbuf_tensor(f"s{n}_{s}", [P, *dims], F32))
        qk, turned, v = sb("qk", [T, H, HD]), sb("turned", [T, H, HD]), sb("v", [T, HK, HD])
        sumsq, krep = sb("sumsq", [T, H]), sb("krep", [T, NH, HD])
        qT, kblk, o, oT = sb("qT", [KD, S]), sb("kblk", [KD, 2, S]), sb("o", [T, D]), sb("oT", [KD, S])
        o_scaled = Signal(ctx, nc, "o_scaled", 1, credit=1)
        unit_ready = Signal(ctx, nc, "unit_ready", 1)
        w, wo = pg.w(n, "w", KD, D + 2 * HK * HD), pg.w(n, "wo", KD, D)
        o_bank, y_bank = pg.bank[7], pg.bank[4]
        with nc.Block() as block:
            prefetch(pg, block, n)

            @block.gpsimd
            def _(pool):
                start(pg, pool, n)
                with pool.Fori(0, B) as i:
                    body.stage(pool, i)
                    body.roots(pool, i)

            @block.tensor
            def _(pe):
                start(pg, pe, n)
                att.credits_tensor(pe)
                with pe.Fori(0, B) as i:
                    body.transpose_x(pe, i)
                    acc.wait_emptied(pe, i, 0)
                    for k, lo, hi in ((1, 0, D), (2, D, D + 2 * HK * HD)):
                        acc.wait_empty(pe, i, k)
                        for t in range(T):
                            last = project_tokens(nc, acc.bank(k)[:, t * (hi - lo):(t + 1) * (hi - lo)],
                                                  w[:, :, lo:hi], body.xT, t)
                        last.then_inc(acc.full.sem, 1)
                    pe.wait_ge(unit_ready.sem, unit_ready.at(i, 1))
                    acc.wait_empty(pe, i, 3)
                    for t in range(T):
                        for k in range(KD):
                            last = nc.tensor.transpose(acc.bank(3)[:, k * S + t * P:k * S + (t + 1) * P],
                                                       qk[:, t, k * 8:(k + 1) * 8, :].rearrange("p h d -> p (h d)"), pg.c("ident"))
                    last.then_inc(acc.full.sem, 1)
                    acc.wait_empty(pe, i, 4)
                    for t in range(T):
                        for k in range(KD):
                            last = nc.tensor.transpose(acc.bank(4)[:, k * S + t * P:k * S + (t + 1) * P],
                                                       krep[:, t, k * 8:(k + 1) * 8, :].rearrange("p h d -> p (h d)"), pg.c("ident"))
                    last.then_inc(acc.full.sem, 1)
                    acc.wait_emptied(pe, i, 4)
                    att.tensor(pe, i, lambda s, u, bank: pair_scores(nc, u, qT, kblk, bank),
                               lambda s, u, probsT: pair_values(nc, u, probsT, o_bank,
                                                                lambda c, head: v[:, c, head // (NH // HK), :]),
                               lambda: pe.wait_ge(o_scaled.sem, o_scaled.at(i, 0)))
                    pe.wait_ge(o_scaled.sem, o_scaled.at(i, 1))
                    acc.wait_empty(pe, i, 5)
                    transpose_tokens(nc, pe, acc.bank(5), o, pg.c("ident")).then_inc(acc.full.sem, 1)
                    acc.wait_emptied(pe, i, 5)
                    body.project_out(pe, i, oT, wo, y_bank, KD)

            @block.scalar
            def _(act):
                start(pg, act, n)
                acc.empty.give(act)
                att.credits_scalar(act)
                with act.Fori(0, B) as i:
                    body.take_xT(act, i)
                    acc.wait_full(act, i, 1)
                    nc.scalar.activation(qk[:, :, 0:NH, :].rearrange("p t h d -> p t (h d)"),
                                         shaped(acc.bank(1)[:], (T, D)), ACT.Copy).then_inc(acc.empty.sem, 1)
                    acc.wait_full(act, i, 2)
                    kv = shaped(acc.bank(2)[:, 0:T * 2 * HK * HD], (T, 2, HK * HD))
                    nc.scalar.activation(qk[:, :, NH:H, :].rearrange("p t h d -> p t (h d)"), kv[:, :, 0, :], ACT.Copy)
                    nc.scalar.activation(v[:].rearrange("p t h d -> p t (h d)"), kv[:, :, 1, :], ACT.Copy)\
                        .then_inc(acc.empty.sem, 1)
                    acc.wait_full(act, i, 3)
                    nc.scalar.activation(qT[:], shaped(acc.bank(3)[:], (KD, S)), ACT.Copy).then_inc(acc.empty.sem, 1)
                    acc.wait_full(act, i, 4)
                    spread_keys(nc, kblk, shaped(acc.bank(4)[:], (KD, S)), pg.c("par2")).then_inc(acc.empty.sem, 1)
                    att.scalar(act, i)
                    acc.wait_full(act, i, 5)
                    nc.scalar.activation(oT[:], shaped(acc.bank(5)[:], (KD, S)), ACT.Copy).then_inc(acc.empty.sem, 1)

            @block.vector
            def _(dve):
                start(pg, dve, n)
                body.out_taken.give(dve)
                o_scaled.give(dve)
                att.credits_vector(dve)
                cos, sin = (over(shaped(pg.c(k), (T, HD)), 2, H) for k in ("cos", "sin"))
                half = HD // 2
                with dve.Fori(0, B) as i:
                    chain = Chain(body.vchain, dve, i)
                    acc.wait_emptied(dve, i, 2)
                    nc.vector.tensor_tensor(turned[:, :, :, 0:half], qk[:, :, :, half:HD], sin[:, :, :, 0:half], ALU.mult)
                    chain.step(nc.vector.tensor_tensor(turned[:, :, :, half:HD], qk[:, :, :, 0:half],
                                                       sin[:, :, :, half:HD], ALU.mult))
                    chain.step(nc.vector.tensor_tensor(qk[:], qk[:], cos, ALU.mult))
                    chain.step(nc.vector.tensor_tensor(qk[:], qk[:], turned[:], ALU.add))
                    chain.step(nc.vector.tensor_tensor(turned[:], qk[:], qk[:], ALU.mult))
                    chain.step(nc.vector.tensor_reduce(sumsq[:], turned[:], AX, ALU.add))
                    nc.vector.tensor_scalar(body.root[0][:], flat(sumsq[:]), 1e-24, None, ALU.max)\
                        .then_inc(body.squares_ready.sem, 1)
                    body.wait_root(dve, i, 0)
                    rt = shaped(body.root[0][:], (T, H))
                    chain.step(nc.vector.tensor_tensor(rt[:, :, 0:NH], rt[:, :, 0:NH], over(pg.w(n, "temp"), 1, T), ALU.mult))
                    chain.step(nc.vector.tensor_tensor(qk[:], qk[:], over(rt, 3, HD), ALU.mult))
                    for t in range(T):
                        last = nc.vector.tensor_copy(krep[:, t, :, :].rearrange("p (g r) d -> p g r d", g=HK),
                                                     over(qk[:, t, NH:H, :], 2, NH // HK))
                    last.then_inc(unit_ready.sem, 1)
                    att.vector(dve, i, chain)
                    dve.wait_ge(att.valued.sem, att.valued.at(i, len(units)))
                    nc.vector.tensor_tensor(flat(o[:]).rearrange("p (h d) -> p h d", d=HD),
                                            o_bank[:].rearrange("p (h d) -> p h d", d=HD),
                                            over(flat(att.rinv[:]), 2, HD), ALU.mult).then_inc(o_scaled.sem, 1)
                    body.add_norm(dve, i, chain, y_bank)
                    chain.done()


def decay_attention(pg, n):
    nc = pg.nc
    W = S + P
    with Scope(nc, f"s{n}") as ctx:
        body = Body(pg, ctx, 6, 3, f"s{n}", roots=(T,))
        acc = body.acc
        sb = lambda s, dims: ctx.enter_context(nc.sbuf_tensor(f"s{n}_{s}", [P, *dims], F32))
        sig = lambda s, per, credit=0: Signal(ctx, nc, s, per, credit)
        raw, th = sb("raw", [2, KD, S]), sb("th", [2, KD, S])
        q2T, k2T, kblk, v, u = sb("q2T", [KD, S]), sb("k2T", [KD, S]), sb("kblk", [KD, 2, S]), sb("v", [T, D]), sb("u", [T, D])
        o, oT, squares, sumsq = sb("o", [T, D]), sb("oT", [KD, S]), sb("squares", [T, D]), sb("sumsq", [T])
        weighted = sb("weighted", [3, W])
        decay = pg.spare(n, 0, NH, W)
        minus_slope = pg.spare(n, NH * W, NH)
        slope_ready, exps_done, decay_ready = sig("slope_ready", 1), sig("exps_done", 1), sig("decay_ready", 1)
        keys_ready = sig("keys_ready", 1)
        scored = sig("scored", NH)
        s_banks = [pg.bank[2], pg.bank[3], pg.bank[5], pg.bank[6]]
        weighted_ready = sig("weighted_ready", NH, len(s_banks))
        valued = sig("valued", NH, 3)
        o_taken = sig("o_taken", 1, 1)
        o_ready = sig("o_ready", 1)
        w, wo = pg.w(n, "w", KD, 4 * D), pg.w(n, "wo", KD, D)
        o_bank, y_bank = pg.bank[7], pg.bank[4]
        with nc.Block() as block:
            prefetch(pg, block, n)

            @block.gpsimd
            def _(pool):
                start(pg, pool, n)
                with pool.Fori(0, B) as i:
                    body.stage(pool, i)
                    body.roots(pool, i)

            @block.tensor
            def _(pe):
                start(pg, pe, n)
                valued.give(pe)
                with pe.Fori(0, B) as i:
                    body.transpose_x(pe, i)
                    acc.wait_emptied(pe, i, 0)
                    for k in range(2):
                        acc.wait_empty(pe, i, 1 + k)
                        project_features(nc, acc.bank(1 + k), w[:, :, k * D:(k + 1) * D], body.xT).then_inc(acc.full.sem, 1)
                    for k in range(2, 4):
                        acc.wait_empty(pe, i, 1 + k)
                        for t in range(T):
                            last = project_tokens(nc, acc.bank(1 + k)[:, t * D:(t + 1) * D], w[:, :, k * D:(k + 1) * D],
                                                  body.xT, t)
                        last.then_inc(acc.full.sem, 1)
                    pe.wait_ge(keys_ready.sem, keys_ready.at(i, 1))
                    acc.wait_emptied(pe, i, 3)
                    for s in range(NH + 2):
                        if s < NH:
                            pe.wait_ge(weighted_ready.sem, weighted_ready.at(i, s + 1 - len(s_banks)))
                            r, m, j = 32 * (s % 8 // 2), s // 8, s % 2
                            for c in range(T):
                                last = nc.tensor.matmul(s_banks[s % 4][:, c * S:c * S + S - c * P],
                                                        kblk[r:r + 32, m, j, c * P:(c + 1) * P],
                                                        q2T[r:r + 32, m, c * P:S], start=True, stop=True)
                            last.then_inc(scored.sem, 1)
                        h = s - 2
                        if h == 0:
                            pe.wait_ge(o_taken.sem, o_taken.at(i, 0))
                        if h >= 0:
                            pe.wait_ge(weighted_ready.sem, weighted_ready.at(i, h + 1))
                            p = weighted[:, h % 3, :]
                            cols = slice(h * HD, (h + 1) * HD)
                            nc.tensor.matmul(o_bank[:, cols], p[:, 0:P], v[:, 0, cols], start=True, stop=True)
                            late = o_bank[:, D + h * HD:D + (h + 1) * HD]
                            nc.tensor.matmul(late, p[:, P:S], v[:, 0, cols], start=True, stop=False)
                            nc.tensor.matmul(late, p[:, S:W], v[:, 1, cols], start=False, stop=True)\
                                .then_inc(valued.sem, 1)
                    pe.wait_ge(o_ready.sem, o_ready.at(i, 1))
                    acc.wait_empty(pe, i, 5)
                    transpose_tokens(nc, pe, acc.bank(5), o, pg.c("ident")).then_inc(acc.full.sem, 1)
                    acc.wait_emptied(pe, i, 5)
                    body.project_out(pe, i, oT, wo, y_bank, KD)

            @block.scalar
            def _(act):
                start(pg, act, n)
                acc.empty.give(act)
                act.wait_ge(slope_ready.sem, 1)
                for h in range(NH):
                    last = nc.scalar.activation(decay[:, h, 0:S], pg.w(n, "dist"), ACT.Exp, scale=minus_slope[:, h:h + 1])
                last.then_inc(exps_done.sem, 1)
                with act.Fori(0, B) as i:
                    body.take_xT(act, i)
                    for k in range(2):
                        acc.wait_full(act, i, 1 + k)
                        view = shaped(acc.bank(1 + k)[:], (KD, S))
                        nc.scalar.activation(raw[:, k, :, :], view, ACT.Copy)
                        nc.scalar.activation(th[:, k, :, :], view, ACT.Tanh, scale=0.5).then_inc(acc.empty.sem, 1)
                    for k, dst in ((3, v), (4, u), (5, oT)):
                        acc.wait_full(act, i, k)
                        nc.scalar.activation(dst[:], shaped(acc.bank(k)[:], (KD, S)), ACT.Copy).then_inc(acc.empty.sem, 1)

            @block.vector
            def _(dve):
                start(pg, dve, n)
                body.out_taken.give(dve)
                weighted_ready.give(dve)
                o_taken.give(dve)
                nc.vector.tensor_scalar(minus_slope, pg.w(n, "slope"), -1.0, None, ALU.mult).then_inc(slope_ready.sem, 1)
                dve.wait_ge(exps_done.sem, 1)
                for h in range(NH):
                    last = nc.vector.scalar_tensor_tensor(out=decay[:, h, 0:S], in0=decay[:, h, 0:S], scalar=0.25,
                                                          in1=pg.w(n, "valid"), op0=ALU.mult, op1=ALU.mult)
                last.then_inc(decay_ready.sem, 1)
                dve.wait_ge(decay_ready.sem, 1)
                nc.vector.tensor_copy(decay[:, :, S:W], decay[:, :, 0:P]).then_inc(decay_ready.sem, 1)
                dve.wait_ge(decay_ready.sem, 2)
                with dve.Fori(0, B) as i:
                    chain = Chain(body.vchain, dve, i)
                    acc.wait_emptied(dve, i, 2)
                    for k, dst in ((0, q2T), (1, k2T)):
                        last = nc.vector.scalar_tensor_tensor(out=dst[:], in0=th[:, k, :, :], scalar=1.0,
                                                              in1=raw[:, k, :, :], op0=ALU.add, op1=ALU.mult)
                    chain.step(last)
                    for par in range(2):
                        last = nc.vector.tensor_scalar(kblk[:, :, par, :], k2T[:], pg.c("par2")[:, par:par + 1], None,
                                                       ALU.mult)
                    last.then_inc(keys_ready.sem, 1)
                    for h in range(NH):
                        dve.wait_ge(scored.sem, scored.at(i, h + 1))
                        dve.wait_ge(valued.sem, valued.at(i, h + 1 - 3))
                        nc.vector.tensor_tensor(weighted[:, h % 3, :], s_banks[h % 4][:, 0:W], decay[:, h, :], ALU.mult)\
                            .then_inc(weighted_ready.sem, 1)
                    dve.wait_ge(valued.sem, valued.at(i, NH))
                    nc.vector.tensor_copy(o[:], shaped(o_bank[:], (T, D))).then_inc(o_taken.sem, 1)
                    dve.wait_ge(o_taken.sem, o_taken.at(i, 1))
                    chain.step(nc.vector.tensor_tensor(squares[:], o[:], o[:], ALU.mult))
                    chain.step(nc.vector.tensor_reduce(sumsq[:], squares[:], AX, ALU.add))
                    nc.vector.tensor_scalar(body.root[0][:], sumsq[:], 1.0 / D, RMS_EPS, ALU.mult, ALU.add)\
                        .then_inc(body.squares_ready.sem, 1)
                    body.wait_root(dve, i, 0)
                    acc.wait_emptied(dve, i, 4)
                    for t in range(T):
                        last = nc.vector.scalar_tensor_tensor(out=o[:, t, :], in0=o[:, t, :],
                                                              scalar=body.root[0][:, t:t + 1], in1=u[:, t, :],
                                                              op0=ALU.mult, op1=ALU.mult)
                    last.then_inc(o_ready.sem, 1)
                    body.add_norm(dve, i, chain, y_bank)
                    chain.done()


def head_attention(pg, n):
    nc = pg.nc
    HG = 8
    units = [(t, g) for t in range(T) for g in range(NH // HG)]
    U = len(units)
    with Scope(nc, f"s{n}") as ctx:
        body = Body(pg, ctx, 5, 4, f"s{n}")
        acc = body.acc
        sb = lambda s, dims: ctx.enter_context(nc.sbuf_tensor(f"s{n}_{s}", [P, *dims], F32))
        sig = lambda s, per, credit=0: Signal(ctx, nc, s, per, credit)
        raw, qkv = sb("raw", [T, 3, D]), sb("qkv", [T, 3, D])
        products = sb("products", [2, HG, NH, HD])
        scores, top, sums = sb("scores", [T, NH, NH]), sb("top", [T, NH]), sb("sums", [T, NH])
        o, regrouped, oT = sb("o", [T, NH, HD]), sb("regrouped", [T, D]), sb("oT", [KD, S])
        regroup = nc.dram_tensor(f"regroup{n}", [B, NH, S, HD], F32, kind="Internal").ap()
        biased = sig("biased", 1)
        product_ready = sig("product_ready", 2 * U)
        product_used = sig("product_used", 2 * U, 2)
        shifted_ready, exps_ready, probs_ready = sig("shifted_ready", 1), sig("exps_ready", 1), sig("probs_ready", 1)
        written = sig("written", 16 * T)
        read_back = sig("read_back", 16)
        w, wo = pg.w(n, "w", KD, 3 * D), pg.w(n, "wo", KD, D)
        y_bank = pg.bank[4]

        def regroup_rows(sp):
            with sp.Fori(0, B) as i:
                sp.wait_ge(product_used.sem, product_used.at(i, 2 * U))
                for t in range(T):
                    sp.dma_start(regroup[i, :, t * P:(t + 1) * P, :].rearrange("h p d -> p h d"), o[:, t, :, :])\
                        .then_inc(written.sem, 16)
                sp.wait_ge(written.sem, written.at(i, 16 * T))
                sp.dma_start(regrouped[:], regroup[i].rearrange("h (r c) d -> (h r) (c d)", c=NH)
                             .rearrange("(t p) d -> p t d", p=P)).then_inc(read_back.sem, 16)
        with nc.Block() as block:
            prefetch(pg, block, n, regroup_rows)

            @block.gpsimd
            def _(pool):
                start(pg, pool, n)
                with pool.Fori(0, B) as i:
                    body.stage(pool, i)
                    acc.wait_emptied(pool, i, 3)
                    nc.gpsimd.tensor_tensor(qkv[:].rearrange("p t a d -> p t (a d)"), raw[:].rearrange("p t a d -> p t (a d)"),
                                            over(pg.w(n, "b"), 1, T), ALU.add).then_inc(biased.sem, 1)
                    pool.wait_ge(biased.sem, biased.at(i, 1))
                    head = lambda t, a: shaped(qkv[:, t, a, :], (NH, HD))
                    for k in range(2 * U):
                        t, g = units[k % U]
                        mine = slice(g * HG, (g + 1) * HG)
                        if k < U:
                            in0, in1 = over(head(t, 0)[:, mine, :], 2, NH), over(head(t, 1), 1, HG)
                        else:
                            if k == U:
                                pool.wait_ge(probs_ready.sem, probs_ready.at(i, 1))
                            in0 = over(scores[:, t, mine, :], 2, HD)
                            in1 = over(head(t, 2).rearrange("p g d -> p d g"), 1, HG)
                        pool.wait_ge(product_used.sem, product_used.at(i, k + 1 - 2))
                        nc.gpsimd.tensor_tensor(products[:, k % 2, :, :, :], in0, in1, ALU.mult)\
                            .then_inc(product_ready.sem, 1)
                    body.roots(pool, i)

            @block.tensor
            def _(pe):
                start(pg, pe, n)
                with pe.Fori(0, B) as i:
                    body.transpose_x(pe, i)
                    acc.wait_emptied(pe, i, 0)
                    acc.wait_empty(pe, i, 1)
                    project_tokens(nc, acc.bank(1)[:], w[:, :, 0:2 * D], body.xT, 0).then_inc(acc.full.sem, 1)
                    acc.wait_empty(pe, i, 2)
                    for t in range(T):
                        last = project_tokens(nc, acc.bank(2)[:, t * D:(t + 1) * D], w[:, :, 2 * D:3 * D], body.xT, t)
                    last.then_inc(acc.full.sem, 1)
                    acc.wait_empty(pe, i, 3)
                    project_tokens(nc, acc.bank(3)[:], w[:, :, 0:2 * D], body.xT, 1).then_inc(acc.full.sem, 1)
                    pe.wait_ge(read_back.sem, read_back.at(i, 16))
                    acc.wait_empty(pe, i, 4)
                    transpose_tokens(nc, pe, acc.bank(4), regrouped, pg.c("ident")).then_inc(acc.full.sem, 1)
                    acc.wait_emptied(pe, i, 4)
                    body.project_out(pe, i, oT, wo, y_bank, KD)

            @block.scalar
            def _(act):
                start(pg, act, n)
                acc.empty.give(act)
                with act.Fori(0, B) as i:
                    body.take_xT(act, i)
                    for k, dst in ((1, raw[:, 0, 0:2, :]), (2, raw[:, :, 2, :]), (3, raw[:, 1, 0:2, :])):
                        acc.wait_full(act, i, k)
                        nc.scalar.activation(dst, shaped(acc.bank(k)[:], (2, D)), ACT.Copy).then_inc(acc.empty.sem, 1)
                    act.wait_ge(shifted_ready.sem, shifted_ready.at(i, 1))
                    nc.scalar.activation(scores[:], scores[:], ACT.Exp, scale=1.0 / 16).then_inc(exps_ready.sem, 1)
                    acc.wait_full(act, i, 4)
                    nc.scalar.activation(oT[:], shaped(acc.bank(4)[:], (KD, S)), ACT.Copy).then_inc(acc.empty.sem, 1)

            @block.vector
            def _(dve):
                start(pg, dve, n)
                body.out_taken.give(dve)
                product_used.give(dve)
                rows = lambda ap: ap.rearrange("p t h g -> p (t h) g")
                with dve.Fori(0, B) as i:
                    chain = Chain(body.vchain, dve, i)
                    for k in range(2 * U):
                        t, g = units[k % U]
                        if k == U:
                            dve.wait_ge(product_used.sem, product_used.at(i, U))
                            chain.step(nc.vector.tensor_reduce(flat(top[:]), rows(scores[:]), AX, ALU.max))
                            nc.vector.tensor_tensor(rows(scores[:]), rows(scores[:]), over(flat(top[:]), 2, NH), ALU.subtract)\
                                .then_inc(shifted_ready.sem, 1)
                            dve.wait_ge(exps_ready.sem, exps_ready.at(i, 1))
                            chain.step(nc.vector.tensor_reduce(flat(sums[:]), rows(scores[:]), AX, ALU.add))
                            chain.step(nc.vector.reciprocal(sums[:], sums[:]))
                            nc.vector.tensor_tensor(rows(scores[:]), rows(scores[:]), over(flat(sums[:]), 2, NH), ALU.mult)\
                                .then_inc(probs_ready.sem, 1)
                        dst = (scores if k < U else o)[:, t, g * HG:(g + 1) * HG, :]
                        dve.wait_ge(product_ready.sem, product_ready.at(i, k + 1))
                        nc.vector.tensor_reduce(dst, products[:, k % 2, :, :, :], AX, ALU.add).then_inc(product_used.sem, 1)
                    body.add_norm(dve, i, chain, y_bank, bias=pg.w(n, "bo"))
                    chain.done()


def latent_attention(pg, n, rotate_queries):
    nc = pg.nc
    CQ, DC, PAIRS = 96, 64, NH // 2
    with Scope(nc, f"s{n}") as ctx:
        units = [{"t": t, "g": g, "heads": 8, "keys": NK, "masks": []} for t in range(T) for g in range(2)]
        U = len(units)
        fills = 1 + 4 + U
        body = Body(pg, ctx, fills, attention_steps(units, True), f"s{n}",
                    elsewhere=range(1, 5) if rotate_queries else ())
        att = Attention(pg, ctx, f"s{n}", body, units, few_keys=True)
        acc = body.acc
        sb = lambda s, dims, p=P: ctx.enter_context(nc.sbuf_tensor(f"s{n}_{s}", [p, *dims], F32))
        sig = lambda s, per, credit=0: Signal(ctx, nc, s, per, credit)
        wq, kckv = pg.w(n, "wq", NH, D), pg.w(n, "kckv", NH, DC)
        qr, kr, wo = pg.w(n, "qr", NH, 2 * CQ, rows=DC), pg.w(n, "kr", NH, DC, rows=DC), pg.w(n, "wo", NH, D)
        QR = pg.spare(n, 0, NH, 2, DC, rows=CQ)
        OUT = pg.spare(n, 2048, PAIRS, D)
        if rotate_queries:
            kcq = pg.w(n, "kcq", NH, 2 * CQ)
            BIG = pg.over_weights(n, "kckv", 0, NH, KD, 2 * CQ)
            qcos, qsin = pg.w(n, "qcos", 2, S, rows=CQ), pg.w(n, "qsin", 2, S, rows=CQ)
        else:
            kcq = pg.w(n, "kcq", 2, NH, P, rows=CQ)
            MID = pg.over_weights(n, "kckv", 0, NH, DC)
            Q = pg.over_weights(n, "kckv", NH * DC, KD, NH, DC)
        kv, swapped = sb("kv", [B, DC]), sb("swapped", [B, DC])
        vblk, kblk = sb("vblk", [B, P]), sb("kblk", [B, P])
        qT, o = sb("qT", [PAIRS, S]), sb("o", [U, 512])
        oT = qT
        v_bank = [pg.bank[7], pg.bank[4]]
        y_bank = pg.bank[4]
        kv_steps = sig("kv_steps", 0)
        kv_spread = sig("kv_spread", 1)
        fold_full, fold_empty = sig("fold_full", 0), sig("fold_empty", 0)
        o_scaled = sig("o_scaled", U, 2)
        ring = [pg.bank[2], pg.bank[3], pg.bank[5], pg.bank[6]]

        folds, stage_starts = [], []

        def qr_fold(q):
            def mm(bank):
                for h in range(4 * q, 4 * q + 4):
                    for half in range(2):
                        at = ((h % 4) * 2 + half) * DC
                        last = nc.tensor.matmul(bank[0:CQ, at:at + DC], qr[:, h, half * CQ:(half + 1) * CQ], kr[:, h, :],
                                                start=True, stop=True)
                return last
            return mm, flat(QR[:, 4 * q:4 * q + 4, :, :]), slice(0, CQ), 512

        def out_fold(q):
            def mm(bank):
                for pair in (2 * q, 2 * q + 1):
                    for j in range(2):
                        last = nc.tensor.matmul(bank[j * DC:(j + 1) * DC, (pair % 2) * D:(pair % 2 + 1) * D],
                                                kckv[:, 2 * pair + j, :], wo[:, 2 * pair + j, :], start=True, stop=True)
                return last
            return mm, flat(OUT[:, 2 * q:2 * q + 2, :]), slice(0, P), 512

        def big_fold(h):
            def mm(bank):
                for m in range(KD):
                    last = nc.tensor.matmul(bank[:, m * 2 * CQ:(m + 1) * 2 * CQ], wq[:, h, m * P:(m + 1) * P], kcq[:, h, :],
                                            start=True, stop=True)
                return last
            return mm, flat(BIG[:, h, :, :]), slice(0, P), KD * 2 * CQ

        def mid_fold(q):
            def mm(bank):
                for h in range(8 * q, 8 * q + 8):
                    for half in range(2):
                        last = nc.tensor.matmul(bank[:, (h % 8) * DC:(h % 8 + 1) * DC], kcq[:, half, h, :], QR[:, h, half, :],
                                                start=(half == 0), stop=(half == 1))
                return last
            return mm, flat(MID[:, 8 * q:8 * q + 8, :]), slice(0, P), 512

        def q_fold(q):
            m, quarter = q // 2, q % 2
            def mm(bank):
                for h in range(8 * quarter, 8 * quarter + 8):
                    last = nc.tensor.matmul(bank[:, (h % 8) * DC:(h % 8 + 1) * DC], wq[:, h, m * P:(m + 1) * P], MID[:, h, :],
                                            start=True, stop=True)
                return last
            return mm, flat(Q[:, m, 8 * quarter:8 * quarter + 8, :]), slice(0, P), 512

        stages = [[qr_fold(q) for q in range(4)] + [out_fold(q) for q in range(4)]]
        stages += [[big_fold(h) for h in range(NH)]] if rotate_queries else \
            [[mid_fold(q) for q in range(2)], [q_fold(q) for q in range(4)]]

        if rotate_queries:
            big_full = sig("big_full", NH)
            products_ready = sig("products_ready", NH, len(ring))
            rotated_ready = sig("rotated_ready", NH, 2)
            rotated_used = sig("rotated_used", NH, 3)
            rotated, crossed = sb("rotated", [3, 2, S], CQ), sb("crossed", [2, 2, S], CQ)
        with nc.Block() as block:
            prefetch(pg, block, n)

            @block.gpsimd
            def _(pool):
                start(pg, pool, n)
                if rotate_queries:
                    rotated_ready.give(pool)
                with pool.Fori(0, B) as i:
                    body.stage(pool, i)
                    if rotate_queries:
                        for h in range(NH):
                            pool.wait_ge(products_ready.sem, products_ready.at(i, h + 1))
                            nc.gpsimd.tensor_tensor(rotated[:, h % 3, :, :], rotated[:, h % 3, :, :], crossed[:, h % 2, :, :],
                                                    ALU.add).then_inc(rotated_ready.sem, 1)
                    body.roots(pool, i)

            @block.tensor
            def _(pe):
                start(pg, pe, n)
                k = 0
                for stage in stages:
                    if k:
                        pe.wait_ge(fold_empty.sem, k)
                    for mm, _, _, _ in stage:
                        if k >= len(ring):
                            pe.wait_ge(fold_empty.sem, k + 1 - len(ring))
                        mm(ring[k % len(ring)]).then_inc(fold_full.sem, 1)
                        k += 1
                pe.wait_ge(fold_empty.sem, k)
                pe.wait_ge(kv_spread.sem, 1)
                for b in range(B):
                    last = nc.tensor.transpose(ring[0][:, b * P:(b + 1) * P], vblk[:, b, :], pg.c("ident"))
                last.then_inc(fold_full.sem, 1)
                pe.wait_ge(fold_empty.sem, k + 1)
                att.credits_tensor(pe)
                if rotate_queries:
                    rotated_used.give(pe)
                with pe.Fori(0, B) as i:
                    body.transpose_x(pe, i)
                    acc.wait_emptied(pe, i, 0)
                    if rotate_queries:
                        for s in range(NH + 2):
                            if s < NH:
                                pe.wait_ge(products_ready.sem, products_ready.at(i, s + 1 - len(ring)))
                                for half in range(2):
                                    for m in range(KD):
                                        last = nc.tensor.matmul(ring[s % 4][0:CQ, half * S:(half + 1) * S],
                                                                BIG[:, s, m, half * CQ:(half + 1) * CQ], body.xT[:, m, :],
                                                                start=(m == 0), stop=(m == KD - 1))
                                last.then_inc(big_full.sem, 1)
                            h = s - 2
                            if h >= 0:
                                fill, at = 1 + h // 4, (h // 2 % 2) * S
                                if h % 4 == 0:
                                    acc.wait_empty(pe, i, fill)
                                pe.wait_ge(rotated_ready.sem, rotated_ready.at(i, h + 1))
                                out = acc.bank(fill)[(h % 2) * DC:(h % 2 + 1) * DC, at:at + S]
                                for half in range(2):
                                    last = nc.tensor.matmul(out, QR[:, h, half, :], rotated[:, h % 3, half, :],
                                                            start=(half == 0), stop=(half == 1))
                                last.then_inc(rotated_used.sem, 1)
                    else:
                        for f in range(4):
                            acc.wait_empty(pe, i, 1 + f)
                            for pair in (2 * f, 2 * f + 1):
                                for m in range(KD):
                                    last = nc.tensor.matmul(acc.bank(1 + f)[:, (pair % 2) * S:(pair % 2 + 1) * S],
                                                            flat(Q[:, m, 2 * pair:2 * pair + 2, :]), body.xT[:, m, :],
                                                            start=(m == 0), stop=(m == KD - 1))
                            last.then_inc(acc.full.sem, 1)
                    acc.wait_emptied(pe, i, 4)

                    def score(s, u, bank):
                        for c in range(4):
                            last = nc.tensor.matmul(bank[:, c * P:(c + 1) * P], qT[:, 4 * u["g"] + c, u["t"] * P:(u["t"] + 1) * P],
                                                    kblk[:, i, :], start=True, stop=True)
                        return last

                    def value(s, u, probsT):
                        pe.wait_ge(o_scaled.sem, o_scaled.at(i, s + 1 - 2))
                        for c in range(4):
                            last = nc.tensor.matmul(v_bank[s % 2][:, c * P:(c + 1) * P], probsT[:, c * P:(c + 1) * P],
                                                    vblk[:, i, :], start=True, stop=True)
                        return last
                    att.tensor(pe, i, score, value, lambda: pe.wait_ge(body.out_taken.sem, body.out_taken.at(i, 0)))
                    for s in range(U):
                        pe.wait_ge(o_scaled.sem, o_scaled.at(i, s + 1))
                        acc.wait_empty(pe, i, 5 + s)
                        for c in range(4):
                            last = nc.tensor.transpose(acc.bank(5 + s)[:, c * P:(c + 1) * P], o[:, s, c * P:(c + 1) * P],
                                                       pg.c("ident"))
                        last.then_inc(acc.full.sem, 1)
                    acc.wait_emptied(pe, i, 4 + U)
                    body.project_out(pe, i, oT, OUT, y_bank, PAIRS)

            @block.scalar
            def _(act):
                start(pg, act, n)
                acc.empty.give(act)
                att.credits_scalar(act)
                with act.Fori(0, B) as i:
                    body.take_xT(act, i)
                    for f in range(4):
                        if rotate_queries:
                            act.wait_ge(rotated_used.sem, rotated_used.at(i, 4 * f + 4))
                        else:
                            acc.wait_full(act, i, 1 + f)
                        nc.scalar.activation(qT[:, 2 * f:2 * f + 2, :], shaped(acc.bank(1 + f)[:], (2, S)), ACT.Copy)\
                            .then_inc(acc.empty.sem, 1)
                    att.scalar(act, i)
                    for s, u in enumerate(units):
                        acc.wait_full(act, i, 5 + s)
                        nc.scalar.activation(oT[:, 4 * u["g"]:4 * u["g"] + 4, u["t"] * P:(u["t"] + 1) * P],
                                             shaped(acc.bank(5 + s)[:], (4, P)), ACT.Copy).then_inc(acc.empty.sem, 1)

            @block.vector
            def _(dve):
                start(pg, dve, n)
                body.out_taken.give(dve)
                o_scaled.give(dve)
                if rotate_queries:
                    products_ready.give(dve)
                cos, sin = over(pg.c("kcos"), 1, B), over(pg.c("ksin"), 1, B)
                h = DC // 2
                nc.vector.tensor_tensor(swapped[:, :, 0:h], pg.ctx2[:, :, h:DC], sin[:, :, 0:h], ALU.mult)
                nc.vector.tensor_tensor(swapped[:, :, h:DC], pg.ctx2[:, :, 0:h], sin[:, :, h:DC], ALU.mult)
                nc.vector.tensor_tensor(kv[:], pg.ctx2[:], cos, ALU.mult)
                nc.vector.memset(vblk[:], 0.0).then_inc(kv_steps.sem, 1)
                dve.wait_ge(kv_steps.sem, 1)
                nc.vector.tensor_tensor(kv[:], kv[:], swapped[:], ALU.add).then_inc(kv_steps.sem, 1)
                dve.wait_ge(kv_steps.sem, 2)
                nc.vector.tensor_copy(vblk[0:NK, :, 0:DC], kv[0:NK, :, :])
                nc.vector.tensor_copy(vblk[NK:P, :, DC:P], kv[NK:P, :, :]).then_inc(kv_spread.sem, 1)
                k = 0
                for stage in stages:
                    for _, dst, rows, size in stage:
                        dve.wait_ge(fold_full.sem, k + 1)
                        nc.vector.tensor_copy(dst, ring[k % len(ring)][rows, 0:size]).then_inc(fold_empty.sem, 1)
                        k += 1
                dve.wait_ge(fold_full.sem, k + 1)
                nc.vector.tensor_copy(kblk[:], shaped(ring[0][:], (B, P))).then_inc(fold_empty.sem, 1)
                with dve.Fori(0, B) as i:
                    chain = Chain(body.vchain, dve, i)
                    if rotate_queries:
                        for h in range(NH):
                            src = shaped(ring[h % 4][0:CQ, :], (2, S))
                            dve.wait_ge(big_full.sem, big_full.at(i, h + 1))
                            dve.wait_ge(rotated_ready.sem, rotated_ready.at(i, h + 1 - 2))
                            dve.wait_ge(rotated_used.sem, rotated_used.at(i, h + 1 - 3))
                            nc.vector.tensor_tensor(rotated[:, h % 3, :, :], src, qcos, ALU.mult)
                            for half in range(2):
                                last = nc.vector.tensor_tensor(crossed[:, h % 2, half, :], src[:, 1 - half, :],
                                                               qsin[:, half, :], ALU.mult)
                            last.then_inc(products_ready.sem, 1)
                    att.vector(dve, i, chain)
                    for s in range(U):
                        dve.wait_ge(att.valued.sem, att.valued.at(i, s + 1))
                        nc.vector.tensor_tensor(o[:, s, :].rearrange("p (h d) -> p h d", d=DC),
                                                v_bank[s % 2][:].rearrange("p (h d) -> p h d", d=DC),
                                                over(att.rinv[:, s, :], 2, DC), ALU.mult).then_inc(o_scaled.sem, 1)
                    body.add_norm(dve, i, chain, y_bank)
                    chain.done()


def small_xattn(pg, n):
    nc = pg.nc
    with Scope(nc, f"s{n}") as ctx:
        units = [{"t": t, "g": g, "heads": 8, "keys": NK, "masks": [(0, NK, pg.c("causal")[:, 0:NK])] if t == 0 else []}
                 for t in range(T) for g in range(KD)]
        body = Body(pg, ctx, 3, attention_steps(units, True), f"s{n}")
        att = Attention(pg, ctx, f"s{n}", body, units, few_keys=True)
        acc = body.acc
        sb = lambda s, dims: ctx.enter_context(nc.sbuf_tensor(f"s{n}_{s}", [P, *dims], F32))
        qT, o, oT = sb("qT", [KD, S]), sb("o", [T, D]), sb("oT", [KD, S])
        kblk, vblk = sb("kblk", [B, KD, 8, NK]), sb("vblk", [B, 8, 2, HD])
        kv_ready = Signal(ctx, nc, "kv_ready", 1)
        kv_spread = Signal(ctx, nc, "kv_spread", 1)
        o_scaled = Signal(ctx, nc, "o_scaled", 1, credit=1)
        ctxT = pg.ctxT
        wq, wo = pg.w(n, "wq", KD, D), pg.w(n, "wo", KD, D)
        wk, wv = pg.w(n, "wk", rows=NK), pg.w(n, "wv", rows=NK)
        o_bank, y_bank = pg.bank[7], pg.bank[4]
        with nc.Block() as block:
            prefetch(pg, block, n)

            @block.gpsimd
            def _(pool):
                start(pg, pool, n)
                with pool.Fori(0, B) as i:
                    body.stage(pool, i)
                    body.roots(pool, i)

            @block.tensor
            def _(pe):
                start(pg, pe, n)
                for m in range(KD):
                    nc.tensor.matmul(pg.bank[2][:, m * S:(m + 1) * S], wk[:, m * P:(m + 1) * P], ctxT[:, :, 0:NK],
                                     start=True, stop=True)
                for b in range(B):
                    last = nc.tensor.matmul(pg.bank[5 + b // 2][:, (b % 2) * D:(b % 2 + 1) * D], ctxT[:, b, :], wv,
                                            start=True, stop=True)
                last.then_inc(kv_ready.sem, 1)
                att.credits_tensor(pe)
                pe.wait_ge(kv_spread.sem, 1)
                with pe.Fori(0, B) as i:
                    body.transpose_x(pe, i)
                    acc.wait_emptied(pe, i, 0)
                    acc.wait_empty(pe, i, 1)
                    project_features(nc, acc.bank(1), wq, body.xT).then_inc(acc.full.sem, 1)
                    acc.wait_emptied(pe, i, 1)

                    def score(s, u, bank):
                        return nc.tensor.matmul(bank[:], qT[:, u["g"], u["t"] * P:(u["t"] + 1) * P],
                                                kblk[:, i, u["g"], :, :], start=True, stop=True)

                    def value(s, u, probsT):
                        for c in range(4):
                            pair = 4 * u["g"] + c
                            last = nc.tensor.matmul(o_bank[:, u["t"] * D + pair * 32:u["t"] * D + pair * 32 + 32],
                                                    probsT[:, c * P:(c + 1) * P], vblk[:, i, pair, :, :],
                                                    start=True, stop=True)
                        return last
                    att.tensor(pe, i, score, value,
                               lambda: pe.wait_ge(o_scaled.sem, o_scaled.at(i, 0)))
                    pe.wait_ge(o_scaled.sem, o_scaled.at(i, 1))
                    acc.wait_empty(pe, i, 2)
                    transpose_tokens(nc, pe, acc.bank(2), o, pg.c("ident")).then_inc(acc.full.sem, 1)
                    acc.wait_emptied(pe, i, 2)
                    body.project_out(pe, i, oT, wo, y_bank, KD)

            @block.scalar
            def _(act):
                start(pg, act, n)
                acc.empty.give(act)
                att.credits_scalar(act)
                with act.Fori(0, B) as i:
                    body.take_xT(act, i)
                    acc.wait_full(act, i, 1)
                    nc.scalar.activation(qT[:], shaped(acc.bank(1)[:], (KD, S)), ACT.Copy, scale=0.25)\
                        .then_inc(acc.empty.sem, 1)
                    att.scalar(act, i)
                    acc.wait_full(act, i, 2)
                    nc.scalar.activation(oT[:], shaped(acc.bank(2)[:], (KD, S)), ACT.Copy).then_inc(acc.empty.sem, 1)

            @block.vector
            def _(dve):
                start(pg, dve, n)
                body.out_taken.give(dve)
                o_scaled.give(dve)
                dve.wait_ge(kv_ready.sem, 1)
                for b in range(B):
                    for m in range(KD):
                        nc.vector.tensor_tensor(kblk[:, b, m, :, :],
                                                over(pg.bank[2][:, m * S + b * NK:m * S + (b + 1) * NK], 1, 8),
                                                over(pg.c("mask8"), 2, NK), ALU.mult)
                    last = nc.vector.tensor_tensor(vblk[:, b, :, :, :],
                                                   shaped(pg.bank[5 + b // 2][:, (b % 2) * D:(b % 2 + 1) * D], (8, 2, HD)),
                                                   over(over(pg.c("half2"), 1, 8), 3, HD), ALU.mult)
                last.then_inc(kv_spread.sem, 1)
                with dve.Fori(0, B) as i:
                    chain = Chain(body.vchain, dve, i)
                    att.vector(dve, i, chain)
                    dve.wait_ge(att.valued.sem, att.valued.at(i, len(units)))
                    nc.vector.tensor_tensor(shaped(o[:].rearrange("p t d -> p (t d)"), (T * NH, HD)), shaped(o_bank[:], (T * NH, HD)),
                                            over(att.rinv[:].rearrange("p u h -> p (u h)"), 2, HD), ALU.mult)\
                        .then_inc(o_scaled.sem, 1)
                    body.add_norm(dve, i, chain, y_bank)
                    chain.done()


def prefetch(pg, block, n, more=None):
    order, at = pg.order, pg.order.index(n)

    def load(sp, m):
        sp.dma_start(pg.arena[m % 2][:, 0:pg.where[m]["size"]], pg.dram[m]).then_inc(pg.loaded[m], 16)
        if m in pg.where["overflow"]:
            sp.dma_start(pg.overflow(m), pg.dram[f"overflow{m}"]).then_inc(pg.loaded[m], 16)

    @block.sync
    def _(sp):
        if at == 0:
            for b in range(2):
                sp.dma_start(pg.x[:, 2 * b:2 * b + 2, :, :],
                             pg.dram["x"][2 * b:2 * b + 2].rearrange("b (t p) d -> p b t d", p=P))\
                    .then_inc(pg.inputs_loaded, 16)
            load(sp, n)
            for half in range(2):
                cols = slice(half * NK, (half + 1) * NK)
                sp.dma_start(pg.ctxT[:, :, cols], pg.dram["ctxT"]).then_inc(pg.inputs_loaded, 16)
            sp.dma_start(pg.ctx2[:], pg.dram["ctx2"]).then_inc(pg.inputs_loaded, 16)
            sp.dma_start(pg.const[:], pg.dram["const"]).then_inc(pg.inputs_loaded, 16)
        if at + 1 < len(order):
            load(sp, order[at + 1])
        if more:
            more(sp)


BUILDERS = {1: small_xattn, 4: small_xattn, 0: head_attention, 7: lambda pg, n: latent_attention(pg, n, False),
            10: lambda pg, n: latent_attention(pg, n, True), 6: differential_attention, 3: decay_attention,
            8: modulated_ffn, 9: windowed_attention,
            2: lambda pg, n: weighted_experts(pg, n, 8, 2, True, 17), 5: top1_experts,
            11: lambda pg, n: weighted_experts(pg, n, 8, 2, False, 11)}


def decoder(nc, where, dram, out):
    with ExitStack() as ctx:
        pg = Program(nc, ctx, where, dram)
        for n in pg.order:
            BUILDERS[n](pg, n)
        with nc.Block() as block:
            @block.sync
            def _(sp):
                sp.dma_start(out.rearrange("b (t p) d -> p b t d", p=P), pg.x[:]).then_inc(pg.stored, 16)
                sp.wait_ge(pg.stored, 16)


def kernel(**inputs):
    import concourse.bacc as bacc
    from concourse.bass_utils import run_bass_kernel_spmd

    w = {k: np.asarray(v) for k, v in inputs.items()}
    consts, L, overflow = layouts(w)
    ctx = w["ctx_512"]
    arrays = {"x": w["x"], "ctxT": np.ascontiguousarray(ctx.transpose(2, 0, 1)),
              "ctx2": np.ascontiguousarray(np.concatenate([ctx.transpose(1, 0, 2)] * 2))}
    where = {"order": SUBLAYERS, "arena": [8, 8]}
    arrays["const"], where["const"] = pack(consts)
    where["const"]["size"] = arrays["const"].shape[1]
    for n in SUBLAYERS:
        arrays[n], where[n] = pack(L[n])
        where[n]["size"] = arrays[n].shape[1]
    for n in SUBLAYERS:
        where["arena"][n % 2] = max(where["arena"][n % 2], where[n]["size"])
        if n in SPARE:
            assert n + 1 not in where or where[n + 1]["size"] <= SPARE_AT[n]
            where["arena"][1 - n % 2] = max(where["arena"][1 - n % 2], SPARE_AT[n] + SPARE[n])
    where["overflow"] = {}
    for n, a in overflow.items():
        if n in SUBLAYERS:
            at = max(where[m]["size"] for m in (n - 1, n + 1) if m in where) if len(SUBLAYERS) > 1 else 0
            arrays[f"overflow{n}"], where["overflow"][n] = np.ascontiguousarray(a), (at, a.shape[1])
            where["arena"][1 - n % 2] = max(where["arena"][1 - n % 2], at + a.shape[1])
    nc = bacc.Bacc("TRN2", target_bir_lowering=False, num_devices=1)
    dram, given = {}, {}
    for name, a in arrays.items():
        label = f"in_{name}_dram" if isinstance(name, str) else f"in_weights_{name}_dram"
        given[label] = a
        dram[name] = nc.dram_tensor(label, a.shape, mybir.dt.from_np(a.dtype), kind="ExternalInput").ap()
    out = nc.dram_tensor("out_0_dram", (B, S, D), F32, kind="ExternalOutput").ap()
    decoder(nc, where, dram, out)
    r = run_bass_kernel_spmd(nc, [given], core_ids=[0])
    return r.results[0]["out_0_dram"]
```

```python
from contextlib import ExitStack

import numpy as np

import concourse.bass as bass
from concourse import mybir

F32 = mybir.dt.float32
ALU = mybir.AluOpType
ACT = mybir.ActivationFunctionType
AX = mybir.AxisListType.X

P = 128
B, S, D = 4, 256, 256
T = S // P
KD = D // P
NH, HD = 16, 16
NK = 64
LN_EPS, RMS_EPS = 1e-5, 1e-6
NEG = -1e30
HID = 176


class Scope(ExitStack):

    def __init__(self, nc, name):
        super().__init__()
        self.nc, self.name, self.sems = nc, name, []

    def semaphore(self, name):
        self.sems.append(self.nc.alloc_semaphore(f"{self.name}_{name}"))
        return self.sems[-1]

    def __exit__(self, *failure):
        if failure[0] is None:
            self.nc.clear_and_free_semaphores(self.sems)
            self.nc.all_engine_barrier()
        return super().__exit__(*failure)


class Signal:

    def __init__(self, ctx, nc, name, per, credit=0):
        self.sem = ctx.semaphore(name)
        self.name, self.per, self.credit = name, per, credit

    def at(self, i, k):
        return i * self.per + (k + self.credit)

    def give(self, eng):
        eng.sem_inc(self.sem, self.credit)


class Accumulators:

    def __init__(self, ctx, nc, banks, fills, elsewhere=()):
        self.banks, self.fills, self.elsewhere = banks, fills, elsewhere
        self.full = Signal(ctx, nc, "acc_full", fills - len(elsewhere))
        self.empty = Signal(ctx, nc, "acc_empty", fills, credit=len(banks))

    def bank(self, k):
        return self.banks[k % len(self.banks)]

    def wait_empty(self, pe, i, k):
        pe.wait_ge(self.empty.sem, self.empty.at(i, k + 1 - len(self.banks)))

    def wait_full(self, act, i, k):
        before = sum(1 for f in self.elsewhere if f < k)
        act.wait_ge(self.full.sem, self.full.at(i, k + 1 - before))

    def wait_emptied(self, eng, i, k):
        eng.wait_ge(self.empty.sem, self.empty.at(i, k + 1))


class Root:

    def __init__(self, pg, ctx, name, width):
        self.pg, self.width = pg, width
        self.t = ctx.enter_context(pg.nc.sbuf_tensor(f"{name}_t", [P, width], F32))
        self.wanted = Signal(ctx, pg.nc, f"{name}_wanted", 1)
        self.ready = Signal(ctx, pg.nc, f"{name}_ready", 1)

    def power(self, pool, i):
        pool.wait_ge(self.wanted.sem, self.wanted.at(i, 1))
        self.pg.nc.gpsimd.tensor_tensor(self.t[:], self.t[:], self.pg.c("minus_half")[:, 0:self.width], ALU.pow)\
            .then_inc(self.ready.sem, 1)

    def wait(self, eng, i):
        eng.wait_ge(self.ready.sem, self.ready.at(i, 1))


class Chain:

    def __init__(self, counter, eng, i):
        self.counter, self.eng, self.i, self.k = counter, eng, i, 0

    def step(self, instruction):
        self.k += 1
        instruction.then_inc(self.counter.sem, 1)
        self.eng.wait_ge(self.counter.sem, self.counter.at(self.i, self.k))

    def done(self):
        assert self.k == self.counter.per, (self.counter.name, self.k, self.counter.per)



def ptile(a):
    k = a.shape[0] // P
    return a.reshape(k, P, -1).transpose(1, 0, 2).reshape(P, -1)


def pack(pieces):
    at, where, cols = 0, {}, []
    for name, a in pieces:
        a = a.reshape(a.shape[0], -1)
        if a.shape[0] < P:
            a = np.concatenate([a, np.zeros((P - a.shape[0], a.shape[1]), np.float32)])
        where[name] = (at, a.shape[1])
        at += a.shape[1]
        cols.append(a)
    return np.ascontiguousarray(np.concatenate(cols, axis=1)), where


def hidden_tiles(w, width):
    w = np.concatenate([w, np.zeros((D, width - w.shape[1]), np.float32)], axis=1)
    return w.reshape(KD, P, width // P, P).transpose(1, 2, 0, 3)


def xattn_small(wq, wkv, wo):
    wkT, wvT = wkv[:D].T, wkv[D:].T
    return [("wq", ptile(wq.T)), ("wo", ptile(wo.T)), ("wk", wkT), ("wv", wvT)]


def xattn_latent(wq, w_kc_q, w_kc_kv, w_qr, w_kr, wo, rope_q):
    q = w_kc_q.transpose(1, 0, 2) if rope_q else w_kc_q.transpose(2, 0, 1).reshape(2, 96, 16, P).transpose(1, 0, 2, 3)
    return [("wq", wq.reshape(NH, P, D).transpose(1, 0, 2)),
            ("kcq", q),
            ("kckv", w_kc_kv.transpose(1, 0, 2)),
            ("qr", w_qr.transpose(2, 0, 1)),
            ("kr", w_kr.transpose(2, 0, 1)),
            ("wo", wo.T.reshape(NH, P, D).transpose(1, 0, 2))]


def moe_weights(gate, g, u, d, width):
    if d is None:
        return [("gate", ptile(gate)), ("g", hidden_tiles(g, width)), ("u", hidden_tiles(u, width))]
    return [("gate", ptile(gate)), ("g", hidden_tiles(g, width)), ("u", hidden_tiles(u, width)),
            ("d", ptile(np.concatenate([d, np.zeros((width - d.shape[0], D), np.float32)])))]


def rope_angles(length, dim):
    inv = (1.0 / np.float32(10000.0) ** (np.arange(0, dim, 2, dtype=np.float32) / np.float32(dim))).astype(np.float32)
    return np.arange(length, dtype=np.float32)[:, None] * inv[None, :]


def owners(tiles, edges):
    e = np.zeros((len(edges), tiles * P), np.float32)
    lo = 0
    for n, hi in enumerate(edges):
        e[n, lo:hi] = 1.0
        lo = hi
    return e


def constants():
    p = np.arange(P)
    f = np.float32
    ident = np.eye(P, dtype=f)
    mask8 = (p[:, None] // HD == np.arange(8)).astype(f)
    par2 = ((p[:, None] // HD) % 2 == np.arange(2)).astype(f)
    half2 = (p[:, None] // NK == np.arange(2)).astype(f)
    causal = np.where(p[:, None] >= p[None, :], 0.0, NEG).astype(f)
    near = np.where((causal == 0) & (p[:, None] - p[None, :] < 32), 0.0, NEG).astype(f)
    before = np.where(p[:, None] + P - p[None, :] < 32, 0.0, NEG).astype(f)
    dist = np.maximum(np.arange(S)[None, :] - p[:, None], 0).astype(f)
    valid = (np.arange(S)[None, :] >= p[:, None]).astype(f)
    tri = (np.arange(8)[None, :] < np.arange(8)[:, None]).astype(f).reshape(1, 64).repeat(P, 0)
    ang = rope_angles(S, HD)
    cos = np.concatenate([np.cos(ang)] * 2, -1).reshape(T, P, HD).transpose(1, 0, 2)
    sin = np.concatenate([-np.sin(ang), np.sin(ang)], -1).reshape(T, P, HD).transpose(1, 0, 2)
    a = np.repeat(rope_angles(NK, 64), 2, axis=-1)
    kcos = np.cos(a)
    ksin = np.sin(a) * np.where(np.arange(64) < 32, -1.0, 1.0)
    kcos, ksin = (np.concatenate([t, t]).astype(f) for t in (kcos, ksin))
    return [("ident", ident), ("mask8", mask8), ("par2", par2), ("half2", half2), ("causal", causal),
            ("near", near), ("before", before), ("tri", tri), ("cos", cos.astype(f)), ("sin", sin.astype(f)),
            ("minus_half", np.full((P, 64), -0.5, f)), ("kcos", kcos), ("ksin", ksin)], dist, valid


def layouts(w):
    consts, dist, valid = constants()
    qa = np.repeat(rope_angles(S, 192), 2, axis=-1).T.reshape(2, 96, S).transpose(1, 0, 2)
    sign = np.array([-1.0, 1.0], np.float32)[None, :, None]
    qcos, qsin = np.cos(qa).astype(np.float32), (np.sin(qa) * sign).astype(np.float32)
    L = {}
    rows = lambda v: np.broadcast_to(v.reshape(1, -1), (P, v.size))
    L[0] = [("w", ptile(w["L0_attn_w_qkv"].T)), ("wo", ptile(w["L0_attn_w_out"].T)),
            ("b", rows(w["L0_attn_b_qkv"])), ("bo", rows(w["L0_attn_b_out"]))]
    L[1] = xattn_small(w["L0_xattn_Wq"], w["L0_xattn_Wkv_expand"], w["L0_xattn_Wout"])
    cat = lambda a: np.concatenate(list(a), axis=-1)
    L[2] = moe_weights(np.concatenate([w["L0_ffn_gate_w"].T, w["L0_ffn_shared_gate_w"]], axis=1),
                       np.concatenate([cat(w["L0_ffn_w_gate"]), w["L0_ffn_sw_gate"]], axis=1),
                       np.concatenate([cat(w["L0_ffn_w_up"]), w["L0_ffn_sw_up"]], axis=1),
                       np.concatenate([w["L0_ffn_w_down"].reshape(-1, D), w["L0_ffn_sw_down"]]), 17 * P)
    L[2].append(("owner", owners(17, [HID * (e + 1) for e in range(8)] + [8 * HID + 704])))
    L[3] = [("w", ptile(w["L1_attn_W_qkvu"].T)), ("wo", ptile(w["L1_attn_W_out"].T)),
            ("slope", rows(w["L1_attn_slope_rate"])), ("dist", dist), ("valid", valid)]
    L[4] = xattn_small(w["L1_xattn_Wq"], w["L1_xattn_Wkv_expand"], w["L1_xattn_Wout"])
    L[5] = moe_weights(w["L1_ffn_Wr"], cat(w["L1_ffn_Wg"]), cat(w["L1_ffn_Wu"]),
                       None, 32 * P) + [("br", rows(w["L1_ffn_br"]))]
    L[6] = [(n, ptile(w[f"L2_attn_{n}_w"].T)) for n in ("q1", "k1", "q2", "k2", "v", "o")] \
        + [("lam", rows(w["L2_attn_lambda_param"]))]
    L[7] = xattn_latent(*[w[f"L2_xattn_{n}"] for n in ("Wq", "w_kc_q", "w_kc_kv", "W_qr", "W_kr", "Wo")], False)
    L[8] = [("q", ptile(w["L2_ffn_Wq"].T)), ("k", ptile(w["L2_ffn_Wk"].T)), ("v", ptile(w["L2_ffn_Wv"].T)),
            ("o", ptile(w["L2_ffn_Wo"].T)), ("A", ptile(w["L2_ffn_A"])), ("B", w["L2_ffn_B"]),
            ("ln1", w["L2_ffn_ln1_w"].reshape(KD, P).T), ("ln2", w["L2_ffn_ln2_w"].reshape(KD, P).T),
            ("g", hidden_tiles(w["L2_ffn_W_in_base"].T, 1024)), ("u", hidden_tiles(w["L2_ffn_W_up_base"].T, 1024)),
            ("d", ptile(w["L2_ffn_W_down"].T))]
    overflow = {5: ptile(w["L1_ffn_Wd"].reshape(-1, D))}
    wk, wv = w["L3_attn_Wkv"][:64], w["L3_attn_Wkv"][64:]
    L[9] = [("w", ptile(np.concatenate([w["L3_attn_Wq"].T, wk.T, wv.T], axis=1))),
            ("wo", ptile(w["L3_attn_Wo"].T)), ("temp", rows(w["L3_attn_qk_temp"]))]
    L[10] = xattn_latent(*[w[f"L3_xattn_{n}"] for n in ("Wq", "w_kc_q", "w_kc_kv", "W_qr", "W_kr", "Wo")], True) \
        + [("qcos", qcos), ("qsin", qsin)]
    rowcat = lambda a: a.reshape(-1, a.shape[-1])
    L[11] = moe_weights(w["L3_ffn_Wg"].T, rowcat(w["L3_ffn_W1"]).T, rowcat(w["L3_ffn_W2"]).T,
                        w["L3_ffn_W3"].transpose(0, 2, 1).reshape(-1, D), 11 * P)
    L[11].append(("owner", owners(11, [HID * (e + 1) for e in range(8)])))
    return consts, L, overflow


SUBLAYERS = list(range(12))
SPARE = {3: NH * (S + P) + NH, 7: 4096, 10: 4096}
SPARE_AT = {3: 1600, 7: 10000, 10: 9900}


class Program:

    INPUT_LOADS = 16 * 6

    def __init__(self, nc, ctx, where, dram):
        self.nc, self.where, self.dram, self.order = nc, where, dram, where["order"]
        self.x = ctx.enter_context(nc.sbuf_tensor("x_all", [P, B, T, D], F32))
        self.const = ctx.enter_context(nc.sbuf_tensor("const", [P, where["const"]["size"]], F32))
        self.arena = [ctx.enter_context(nc.sbuf_tensor(f"weights{n}", [P, where["arena"][n]], F32)) for n in range(2)]
        self.ctxT = ctx.enter_context(nc.sbuf_tensor("ctxT", [NK, B, P], F32))
        self.ctx2 = ctx.enter_context(nc.sbuf_tensor("ctx2", [P, B, NK], F32))
        self.inputs_loaded = ctx.enter_context(nc.semaphore("inputs_loaded"))
        self.loaded = {n: ctx.enter_context(nc.semaphore(f"weights_loaded_{n}")) for n in where["order"]}
        self.stored = ctx.enter_context(nc.semaphore("stored"))
        self.bank = [ctx.enter_context(nc.psum_tensor(f"bank{n}", [P, 512], F32)) for n in range(8)]

    def c(self, name, *dims):
        at, n = self.where["const"][name]
        return shaped(self.const[:, at:at + n], dims)

    def w(self, n, name, *dims, rows=P):
        at, size = self.where[n][name]
        return shaped(self.arena[n % 2][0:rows, at:at + size], dims)

    def overflow(self, n, *dims):
        at, size = self.where["overflow"][n]
        return shaped(self.arena[1 - n % 2][:, at:at + size], dims)

    def over_weights(self, n, name, at, *dims):
        at += self.where[n][name][0]
        size = int(np.prod(dims))
        return shaped(self.arena[n % 2][:, at:at + size], dims)

    def spare(self, n, at, *dims, rows=P):
        at += SPARE_AT[n]
        size = int(np.prod(dims))
        return shaped(self.arena[1 - n % 2][0:rows, at:at + size], dims)


def shaped(ap, dims):
    if len(dims) < 2:
        return ap
    names = "abcdef"[:len(dims)]
    return ap.rearrange(f"p ({' '.join(names)}) -> p {' '.join(names)}", **dict(zip(names[1:], dims[1:])))


def over(ap, axis, n):
    ap = ap.unsqueeze(axis)
    shape = list(ap.shape)
    shape[axis] = n
    return ap.broadcast_to(shape)


def start(pg, eng, n):
    eng.wait_ge(pg.inputs_loaded, pg.INPUT_LOADS)
    eng.wait_ge(pg.loaded[n], 32 if n in pg.where["overflow"] else 16)


class Body:

    def __init__(self, pg, ctx, fills, vector_steps, name, roots=(), elsewhere=()):
        nc = self.nc = pg.nc
        self.pg = pg
        sb = lambda n, dims: ctx.enter_context(nc.sbuf_tensor(f"{name}_{n}", [P, *dims], F32))
        self.acc = Accumulators(ctx, nc, pg.bank[0:2], fills, elsewhere)
        self.x_staged = Signal(ctx, nc, "x_staged", 1)
        self.out_ready = Signal(ctx, nc, "out_ready", 1)
        self.out_taken = Signal(ctx, nc, "out_taken", 1, credit=1)
        self.vchain = Signal(ctx, nc, "vector_chain", vector_steps + 5)
        self.root = [Root(pg, ctx, f"{name}_root{k}", wd) for k, wd in enumerate([*roots, T])]
        self.passed = Signal(ctx, nc, "passed", 2)
        self.xs = sb("xs", [T, D])
        self.xT = sb("xT", [KD, S])
        self.r = sb("r", [T, D])
        self.stats = sb("stats", [T, 6])
        self.mv = sb("mv", [T, 2])

    def stage(self, pool, i):
        self.nc.gpsimd.tensor_copy(self.xs[:], self.pg.x[:, i, :, :]).then_inc(self.x_staged.sem, 1)
        self.acc.wait_full(pool, i, 0)

    def stage_first(self, pool):
        self.nc.gpsimd.tensor_copy(self.xs[:], self.pg.x[:, 0, :, :]).then_inc(self.x_staged.sem, 1)

    def stage_next(self, pool, i):
        self.acc.wait_full(pool, i, 0)
        self.nc.gpsimd.tensor_copy(self.xs[:], self.pg.x[:, i + 1, :, :]).then_inc(self.x_staged.sem, 1)

    def roots(self, pool, i):
        for root in self.root:
            root.power(pool, i)

    def transpose_x(self, pe, i):
        pe.wait_ge(self.x_staged.sem, self.x_staged.at(i, 1))
        self.acc.wait_empty(pe, i, 0)
        transpose_tokens(self.nc, pe, self.acc.bank(0), self.xs, self.pg.c("ident")).then_inc(self.acc.full.sem, 1)

    def take_xT(self, act, i):
        self.acc.wait_full(act, i, 0)
        self.nc.scalar.activation(self.xT[:], shaped(self.acc.bank(0)[:], (KD, S)), ACT.Copy)\
            .then_inc(self.acc.empty.sem, 1)

    def project_out(self, pe, i, xT, w, bank, chunks, last_tile=None):
        pe.wait_ge(self.out_taken.sem, self.out_taken.at(i, 0))
        y = shaped(bank[:], (T, D))
        for t in range(T):
            for k in range(chunks):
                last = self.nc.tensor.matmul(y[:, t, :], xT[:, k, t * P:(t + 1) * P], w[:, k, :],
                                             start=(k == 0), stop=(k == chunks - 1))
        last.then_inc(self.out_ready.sem, 1)

    def add_norm(self, dve, i, chain, bank, x_times=1.0, wait_out=True, bias=None):
        nc = self.nc
        if wait_out:
            dve.wait_ge(self.out_ready.sem, self.out_ready.at(i, 1))
        nc.vector.scalar_tensor_tensor(out=self.r[:], in0=self.pg.x[:, i, :, :], scalar=float(x_times),
                                       in1=shaped(bank[:], (T, D)), op0=ALU.mult, op1=ALU.add)\
            .then_inc(self.out_taken.sem, 1)
        dve.wait_ge(self.out_taken.sem, self.out_taken.at(i, 1))
        if bias is not None:
            chain.step(nc.vector.tensor_tensor(self.r[:], self.r[:], over(bias, 1, T), ALU.add))
        self.norm(dve, i, chain)

    def norm(self, dve, i, chain):
        nc = self.nc
        for t in range(T):
            chain.step(nc.vector.bn_stats(self.stats[:, t, :], self.r[:, t, :]))
        dve.sem_inc(self.passed.sem, 1)
        for t in range(T):
            last_aggr = nc.vector.bn_aggr(self.mv[:, t, :], self.stats[:, t, :])
        chain.step(last_aggr)
        root = self.root[-1]
        nc.vector.tensor_scalar(root.t[:], self.mv[:, :, 1], LN_EPS, None, ALU.add).then_inc(root.wanted.sem, 1)
        root.wait(dve, i)
        for t in range(T):
            chain.step(nc.vector.tensor_scalar(self.pg.x[:, i, t, :], self.r[:, t, :], self.mv[:, t, 0:1],
                                               root.t[:, t:t + 1], ALU.subtract, ALU.mult))


def transpose_tokens(nc, pe, bank, src, ident, chunks=KD):
    for t in range(T):
        for k in range(chunks):
            last = nc.tensor.transpose(bank[:, k * S + t * P:k * S + (t + 1) * P],
                                       src[:, t, k * P:(k + 1) * P], ident)
    return last


def project_features(nc, bank, w, xT, tiles=KD):
    for m in range(tiles):
        for k in range(KD):
            last = nc.tensor.matmul(bank[:, m * S:(m + 1) * S], w[:, k, m * P:(m + 1) * P], xT[:, k, :],
                                    start=(k == 0), stop=(k == KD - 1))
    return last


def project_tokens(nc, out, w, xT, t):
    for k in range(KD):
        last = nc.tensor.matmul(out, xT[:, k, t * P:(t + 1) * P], w[:, k, :], start=(k == 0), stop=(k == KD - 1))
    return last


class Attention:
    PROBS, TURNED = 4, 3
    TURN_LAG, COPY_LAG, VALUE_LAG = 3, 4, 5

    def __init__(self, pg, ctx, name, units, few_keys, score_banks, difference=None, probs=4):
        nc = self.nc = pg.nc
        self.pg, self.units, self.few, self.minus_lambda = pg, units, few_keys, difference
        self.parts = 2 if difference is not None else 1
        self.PROBS = probs
        n, m = len(units), len(units) * self.parts
        sig = lambda s, per, credit=0: Signal(ctx, nc, s, per, credit)
        sb = lambda s, dims: ctx.enter_context(nc.sbuf_tensor(f"{name}_{s}", [P, *dims], F32))
        self.s_bank, self.t_bank = score_banks, pg.bank[5:7]
        self.scored = sig("scored", m)
        self.maxed = sig("maxed", m)
        self.exps_ready = sig("exps_ready", m, len(score_banks))
        self.inverted = sig("inverted", m)
        self.probs_ready = sig("probs_ready", n)
        self.combined = sig("combined", n)
        self.transposed = sig("transposed", n, self.PROBS)
        self.turned = sig("turned", n, len(self.t_bank))
        self.valued = sig("valued", n, self.TURNED)
        self.probs = sb("probs", [self.PROBS, self.parts, 512])
        self.probsT = sb("probsT", [self.TURNED, 512])
        heads = units[0]["heads"]
        self.nmax = sb("nmax", [m, heads])
        self.sums = sb("sums", [m, heads])

    def credits_scalar(self, act):
        self.exps_ready.give(act)
        if self.few:
            self.turned.give(act)

    def credits_tensor(self, pe):
        self.transposed.give(pe)
        self.valued.give(pe)

    def credits_vector(self, dve):
        if not self.few:
            self.turned.give(dve)

    @staticmethod
    def chunks(unit):
        return unit["heads"] * unit["keys"] // P

    def slot(self, u, part, heads=None):
        h, k = self.units[u]["heads"], self.units[u]["keys"]
        ap = self.probs[:, u % self.PROBS, part, 0:h * k]
        return shaped(ap, (h, k)) if heads else ap

    def tensor(self, pe, i, score, value, before_last_bank=None, before_values=None, pieces=()):
        n, pieces = len(self.units), list(pieces)
        for s in range(n + self.VALUE_LAG):
            if s < n:
                for part in range(self.parts):
                    k = s * self.parts + part
                    if k == len(self.s_bank) - 1 and before_last_bank:
                        before_last_bank()
                    pe.wait_ge(self.exps_ready.sem, self.exps_ready.at(i, k + 1 - len(self.s_bank)))
                    score(k, self.units[s], part, self.s_bank[k % len(self.s_bank)]).then_inc(self.scored.sem, 1)
            u = s - self.TURN_LAG
            if 0 <= u < n:
                if self.parts == 2:
                    pe.wait_ge(self.combined.sem, self.combined.at(i, u + 1))
                else:
                    pe.wait_ge(self.probs_ready.sem, self.probs_ready.at(i, u + 1))
                pe.wait_ge(self.turned.sem, self.turned.at(i, u + 1 - 2))
                for c in range(self.chunks(self.units[u])):
                    last = self.nc.tensor.transpose(self.t_bank[u % 2][:, c * P:(c + 1) * P],
                                                    self.slot(u, self.parts - 1)[:, c * P:(c + 1) * P], self.pg.c("ident"))
                last.then_inc(self.transposed.sem, 1)
            u = s - self.VALUE_LAG
            if 0 <= u < n:
                if u == 0 and before_values:
                    before_values()
                pe.wait_ge(self.turned.sem, self.turned.at(i, u + 1))
                value(u, self.units[u], self.probsT[:, u % self.TURNED, :]).then_inc(self.valued.sem, 1)
            if s >= n and pieces:
                pieces.pop(0)()
        for piece in pieces:
            piece()

    def scalar(self, act, i, pieces=(), after_turn=None):
        n, pieces = len(self.units), list(pieces)
        for s in range(n + self.VALUE_LAG + (1 if after_turn else 0)):
            if s < n:
                h, k = self.units[s]["heads"], self.units[s]["keys"]
                for part in range(self.parts):
                    m = s * self.parts + part
                    act.wait_ge(self.maxed.sem, self.maxed.at(i, m + 1))
                    act.wait_ge(self.transposed.sem, self.transposed.at(i, s + 1 - self.PROBS))
                    src, dst = self.s_bank[m % len(self.s_bank)], self.slot(s, part)
                    if self.few:
                        last = self.nc.scalar.activation(dst, src[:, 0:h * k], ACT.Exp)
                    else:
                        for j in range(h):
                            last = self.nc.scalar.activation(dst[:, j * k:(j + 1) * k], src[:, j * k:(j + 1) * k], ACT.Exp,
                                                             bias=self.nmax[:, m, j:j + 1],
                                                             accum_out=self.sums[:, m, j:j + 1])
                    last.then_inc(self.exps_ready.sem, 1)
            if self.few and 0 <= s - self.COPY_LAG < n:
                self.turn(act, i, s - self.COPY_LAG)
            if after_turn and s - self.VALUE_LAG - 1 >= 0:
                after_turn(s - self.VALUE_LAG - 1)
            if s >= n and pieces:
                pieces.pop(0)()
        for piece in pieces:
            piece()

    def turn(self, eng, i, u):
        size = self.chunks(self.units[u]) * P
        eng.wait_ge(self.transposed.sem, self.transposed.at(i, u + 1))
        eng.wait_ge(self.valued.sem, self.valued.at(i, u + 1 - self.TURNED))
        dst, src = self.probsT[:, u % self.TURNED, 0:size], self.t_bank[u % 2][:, 0:size]
        if self.few:
            self.nc.scalar.activation(dst, src, ACT.Copy).then_inc(self.turned.sem, 1)
        else:
            self.nc.vector.tensor_copy(dst, src).then_inc(self.turned.sem, 1)

    def gpsimd(self, pool, i):
        for u in range(len(self.units)):
            m = u * self.parts
            pool.wait_ge(self.inverted.sem, self.inverted.at(i, m + 1))
            p = self.slot(u, 0, heads=True)
            self.nc.gpsimd.tensor_tensor(p, p, over(self.sums[:, m, :], 2, self.units[u]["keys"]), ALU.mult)\
                .then_inc(self.probs_ready.sem, 1)

    def invert(self, dve, i, m, chain):
        nc, u, part = self.nc, m // self.parts, m % self.parts
        dve.wait_ge(self.exps_ready.sem, self.exps_ready.at(i, m + 1))
        sums = self.sums[:, m, :]
        if self.few:
            chain.step(nc.vector.tensor_reduce(sums, self.slot(u, 0, heads=True), AX, ALU.add))
        if self.parts == 2 and part == 0:
            chain.step(nc.vector.reciprocal(sums, sums))
            g = self.units[u]["g"]
            nc.vector.tensor_tensor(sums, sums, self.minus_lambda[:, 2 * g:2 * g + 2], ALU.mult).then_inc(self.inverted.sem, 1)
            return
        nc.vector.reciprocal(sums, sums).then_inc(self.inverted.sem, 1)

    def combine(self, dve, i, u):
        dve.wait_ge(self.inverted.sem, self.inverted.at(i, 2 * u + 2))
        dve.wait_ge(self.probs_ready.sem, self.probs_ready.at(i, u + 1))
        for j in range(2):
            first, second = (self.slot(u, part, heads=True)[:, j, :] for part in range(2))
            last = self.nc.vector.scalar_tensor_tensor(out=second, in0=second, scalar=self.sums[:, 2 * u + 1, j:j + 1],
                                                       in1=first, op0=ALU.mult, op1=ALU.add)
        last.then_inc(self.combined.sem, 1)

    def vector(self, dve, i, chain):
        n = len(self.units)
        nc = self.nc
        for s in range(n + self.COPY_LAG):
            for part in range(self.parts):
                m = s * self.parts + part
                if s < n:
                    unit = self.units[s]
                    h, k = unit["heads"], unit["keys"]
                    bank = shaped(self.s_bank[m % len(self.s_bank)][:, 0:h * k], (h, k))
                    dve.wait_ge(self.scored.sem, self.scored.at(i, m + 1))
                    for lo, hi, mask in unit["masks"]:
                        chain.step(nc.vector.tensor_tensor(bank[:, :, lo:hi], bank[:, :, lo:hi], over(mask, 1, h), ALU.add))
                    if self.few:
                        chain.step(nc.vector.tensor_reduce(self.nmax[:, m, :], bank, AX, ALU.max))
                        nc.vector.tensor_tensor(bank, bank, over(self.nmax[:, m, :], 2, k), ALU.subtract)\
                            .then_inc(self.maxed.sem, 1)
                    else:
                        nc.vector.tensor_reduce(self.nmax[:, m, :], bank, AX, ALU.max, negate=True)\
                            .then_inc(self.maxed.sem, 1)
                if 0 <= s - 1 < n:
                    self.invert(dve, i, m - self.parts, chain)
            if self.parts == 2 and 0 <= s - 2 < n:
                self.combine(dve, i, s - 2)
            if not self.few and 0 <= s - self.COPY_LAG < n:
                self.turn(dve, i, s - self.COPY_LAG)


def attention_steps(units, few):
    return sum(len(u["masks"]) for u in units) + (2 * len(units) if few else 0)


def pair_units(masks_of, keys_of):
    return [{"t": t, "g": g, "heads": 2, "keys": keys_of[t], "masks": masks_of[t]} for t in range(T) for g in range(8)]


def pair_scores(nc, u, qT, kblk, bank):
    r, m, keys = 32 * (u["g"] % 4), u["g"] // 4, u["keys"]
    return nc.tensor.matmul(bank[:, 0:2 * keys], qT[r:r + 32, m, u["t"] * P:(u["t"] + 1) * P],
                            kblk[r:r + 32, m, :, 0:keys], start=True, stop=True)


def pair_values(nc, u, probsT, out, value_of):
    tiles, r = u["keys"] // P, 32 * (u["g"] % 4)
    cols = (u["g"] // 4) * S + u["t"] * P
    for j in range(2):
        for c in range(tiles):
            at = (j * tiles + c) * P
            last = nc.tensor.matmul(out[r:r + 32, cols:cols + P], value_of(c, u["g"], j), probsT[:, at:at + P],
                                    start=(j == 0 and c == 0), stop=(j == 1 and c == tiles - 1))
    return last


def pad_values(nc, vpad, src):
    for j in range(2):
        for c in range(T):
            last = nc.scalar.activation(vpad[:, c, :, j, j * HD:(j + 1) * HD],
                                        src[:, c, :].rearrange("p (g j d) -> p g j d", j=2, d=HD)[:, :, j, :], ACT.Copy)
    return last


def batches(eng, head, tail):
    head(0)
    with eng.Fori(0, B - 1) as i:
        tail(i, True)
    tail(B - 1, False)


def spread_keys(nc, kblk, src, par2):
    for par in range(2):
        last = nc.scalar.activation(kblk[:, :, par, :], src, ACT.Copy, scale=par2[:, par:par + 1])
    return last


def flat(ap):
    names = "abcdef"[:len(ap.shape) - 1]
    return ap.rearrange(f"p {' '.join(names)} -> p ({' '.join(names)})")


def differential_attention(pg, n):
    nc = pg.nc
    with Scope(nc, f"s{n}") as ctx:
        units = pair_units([[], []], [S, S])
        body = Body(pg, ctx, 6, attention_steps(units, False) + len(units), f"s{n}")
        acc = body.acc
        sb = lambda s, dims: ctx.enter_context(nc.sbuf_tensor(f"s{n}_{s}", [P, *dims], F32))
        minus_lambda = sb("minus_lambda", [NH])
        att = Attention(pg, ctx, f"s{n}", units, False, pg.bank[2:5], difference=minus_lambda)
        qT = [sb(f"q{w}T", [KD, S]) for w in (1, 2)]
        kblk = [sb(f"k{w}", [KD, 2, S]) for w in (1, 2)]
        vpad, oT = sb("vpad", [T, 8, 2, 32]), sb("oT", [KD, S])
        o_taken = Signal(ctx, nc, "o_taken", 1, credit=1)
        ready = Signal(ctx, nc, "ready", 0)
        w = {k: pg.w(n, k, KD, D) for k in ("q1", "k1", "q2", "k2", "v", "o")}
        o_bank, y_bank = pg.bank[7], pg.bank[4]
        with nc.Block() as block:
            prefetch(pg, block, n)

            @block.gpsimd
            def _(pool):
                start(pg, pool, n)

                def tail(i, more):
                    if more:
                        body.stage_next(pool, i)
                    att.gpsimd(pool, i)
                    body.roots(pool, i)
                batches(pool, lambda i: body.stage_first(pool), tail)

            @block.tensor
            def _(pe):
                start(pg, pe, n)
                att.credits_tensor(pe)

                def projections(i):
                    def x():
                        body.transpose_x(pe, i)
                        acc.wait_emptied(pe, i, 0)

                    def features(k, name):
                        acc.wait_empty(pe, i, k)
                        project_features(nc, acc.bank(k), w[name], body.xT).then_inc(acc.full.sem, 1)

                    def values():
                        acc.wait_empty(pe, i, 5)
                        for t in range(T):
                            last = project_tokens(nc, acc.bank(5)[:, t * D:(t + 1) * D], w["v"], body.xT, t)
                        last.then_inc(acc.full.sem, 1)
                    return [x] + [lambda k=k, name=name: features(k + 1, name)
                                  for k, name in enumerate(("q1", "k1", "q2", "k2"))] + [values]

                def head(i):
                    for piece in projections(i):
                        piece()

                def tail(i, more):
                    acc.wait_emptied(pe, i, 5)
                    att.tensor(pe, i,
                               lambda k, u, part, bank: pair_scores(nc, u, qT[1 - part], kblk[1 - part], bank),
                               lambda s, u, probsT: pair_values(nc, u, probsT, o_bank, lambda c, g, j: vpad[:, c, g, j, :]),
                               before_last_bank=lambda: pe.wait_ge(body.out_taken.sem, body.out_taken.at(i, 0)),
                               before_values=lambda: pe.wait_ge(o_taken.sem, o_taken.at(i, 0)),
                               pieces=projections(i + 1) if more else ())
                    pe.wait_ge(o_taken.sem, o_taken.at(i, 1))
                    body.project_out(pe, i, oT, w["o"], y_bank, KD)
                batches(pe, head, tail)

            @block.scalar
            def _(act):
                start(pg, act, n)
                acc.empty.give(act)
                att.credits_scalar(act)
                o_taken.give(act)
                act.wait_ge(ready.sem, 1)
                view = lambda k: shaped(acc.bank(k)[:], (KD, S))

                def takes(i):
                    def queries(which, k):
                        acc.wait_full(act, i, k)
                        nc.scalar.activation(qT[which][:], view(k), ACT.Copy, scale=0.25).then_inc(acc.empty.sem, 1)

                    def keys(which, k):
                        acc.wait_full(act, i, k)
                        spread_keys(nc, kblk[which], view(k), pg.c("par2")).then_inc(acc.empty.sem, 1)
                    return [lambda: body.take_xT(act, i), lambda: queries(0, 1), lambda: keys(0, 2),
                            lambda: queries(1, 3), lambda: keys(1, 4)]

                def take_values(i):
                    acc.wait_full(act, i, 5)
                    pad_values(nc, vpad, view(5)).then_inc(acc.empty.sem, 1)

                def head(i):
                    for take in takes(i):
                        take()
                    take_values(i)

                def tail(i, more):
                    att.scalar(act, i, takes(i + 1) if more else ())
                    act.wait_ge(att.valued.sem, att.valued.at(i, len(units)))
                    nc.scalar.activation(oT[:], shaped(o_bank[:], (KD, S)), ACT.Copy).then_inc(o_taken.sem, 1)
                    if more:
                        take_values(i + 1)
                batches(act, head, tail)

            @block.vector
            def _(dve):
                start(pg, dve, n)
                body.out_taken.give(dve)
                att.credits_vector(dve)
                nc.vector.memset(vpad[:], 0.0)
                nc.vector.tensor_scalar(minus_lambda[:], pg.w(n, "lam"), -1.0, None, ALU.mult).then_inc(ready.sem, 1)
                dve.wait_ge(ready.sem, 1)

                def tail(i, more):
                    chain = Chain(body.vchain, dve, i)
                    att.vector(dve, i, chain)
                    body.add_norm(dve, i, chain, y_bank)
                    chain.done()
                batches(dve, lambda i: None, tail)


class GatedTiles:
    SLOTS = 3

    def __init__(self, pg, ctx, name, tiles, gu_banks, w_banks=()):
        self.nc, self.tiles, self.banks, self.w_banks = pg.nc, tiles, gu_banks, w_banks
        sig = lambda s, credit=0: Signal(ctx, pg.nc, s, tiles, credit)
        sb = lambda s, dims: ctx.enter_context(pg.nc.sbuf_tensor(f"{name}_{s}", [P, *dims], F32))
        self.gu_full = sig("gu_full")
        self.tanh_ready = sig("tanh_ready")
        self.half_done = sig("half_done")
        self.hidden_ready = sig("hidden_ready", len(gu_banks))
        self.down_done = sig("down_done", self.SLOTS)
        self.tanh, self.half = sb("tanh", [2, S]), sb("half", [2, S])
        self.hidden = sb("hidden", [self.SLOTS, S])
        if w_banks:
            self.w_full = sig("w_full")
            self.w_ready = sig("w_ready", 2)
            self.scaled_ready = sig("scaled_ready", self.SLOTS)
            self.wsb, self.scaled = sb("wsb", [2, S]), sb("scaled", [self.SLOTS, S])
        self.down_src = self.scaled if w_banks else self.hidden
        self.down_ready = self.scaled_ready if w_banks else self.hidden_ready

    def credits(self, pe=None, act=None, dve=None, pool=None):
        if pe:
            self.down_done.give(pe)
        if act and self.w_banks:
            self.w_ready.give(act)
        if dve:
            self.hidden_ready.give(dve)
        if pool and self.w_banks:
            self.scaled_ready.give(pool)

    def gate_up(self, pe, i, g, xT, wg, wu, extra=None):
        pe.wait_ge(self.hidden_ready.sem, self.hidden_ready.at(i, g + 1 - len(self.banks)))
        bank = self.banks[g % len(self.banks)]
        for half, w in enumerate((wg, wu)):
            out = bank[:, half * S:(half + 1) * S]
            for k in range(KD):
                more = extra if half == 0 else None
                last = self.nc.tensor.matmul(out, w[:, g, k, :], xT[:, k, :], start=(k == 0),
                                             stop=(k == KD - 1 and not more))
            if more:
                more(out, g)
        last.then_inc(self.gu_full.sem, 1)

    def spread_weights(self, pe, i, g, owner, combT):
        pe.wait_ge(self.w_ready.sem, self.w_ready.at(i, g + 1 - 2))
        self.nc.tensor.matmul(self.w_banks[g % 2][:, 0:S], owner[:, g * P:(g + 1) * P], combT, start=True, stop=True)\
            .then_inc(self.w_full.sem, 1)

    def down(self, pe, i, g, wd, bank, first, last_one):
        pe.wait_ge(self.down_ready.sem, self.down_ready.at(i, g + 1))
        y = shaped(bank[:], (T, D))
        for t in range(T):
            last = self.nc.tensor.matmul(y[:, t, :], self.down_src[:, g % self.SLOTS, t * P:(t + 1) * P], wd[:, g, :],
                                         start=(first and t == 0), stop=last_one, skip_group_check=True)
        last.then_inc(self.down_done.sem, 1)
        return last

    def scalar(self, act, i, g):
        act.wait_ge(self.gu_full.sem, self.gu_full.at(i, g + 1))
        act.wait_ge(self.hidden_ready.sem, self.hidden_ready.at(i, g + 1 - 2))
        self.nc.scalar.activation(self.tanh[:, g % 2, :], self.banks[g % len(self.banks)][:, 0:S], ACT.Tanh, scale=0.5)\
            .then_inc(self.tanh_ready.sem, 1)

    def scalar_weights(self, act, i, g):
        act.wait_ge(self.w_full.sem, self.w_full.at(i, g + 1))
        act.wait_ge(self.scaled_ready.sem, self.scaled_ready.at(i, g + 1 - 2))
        self.nc.scalar.activation(self.wsb[:, g % 2, :], self.w_banks[g % 2][:, 0:S], ACT.Copy).then_inc(self.w_ready.sem, 1)

    def vector(self, dve, i, g):
        bank = self.banks[g % len(self.banks)]
        dve.wait_ge(self.tanh_ready.sem, self.tanh_ready.at(i, g + 1))
        self.nc.vector.scalar_tensor_tensor(out=self.half[:, g % 2, :], in0=self.tanh[:, g % 2, :], scalar=1.0,
                                            in1=bank[:, 0:S], op0=ALU.add, op1=ALU.mult).then_inc(self.half_done.sem, 1)
        dve.wait_ge(self.half_done.sem, self.half_done.at(i, g + 1))
        freed = self.scaled_ready if self.w_banks else self.down_done
        dve.wait_ge(freed.sem, freed.at(i, g + 1 - self.SLOTS))
        self.nc.vector.scalar_tensor_tensor(out=self.hidden[:, g % self.SLOTS, :], in0=self.half[:, g % 2, :], scalar=0.5,
                                            in1=bank[:, S:2 * S], op0=ALU.mult, op1=ALU.mult)\
            .then_inc(self.hidden_ready.sem, 1)

    def pool(self, pool, i, g):
        pool.wait_ge(self.w_ready.sem, self.w_ready.at(i, g + 1))
        pool.wait_ge(self.hidden_ready.sem, self.hidden_ready.at(i, g + 1))
        pool.wait_ge(self.down_done.sem, self.down_done.at(i, g + 1 - self.SLOTS))
        self.nc.gpsimd.tensor_tensor(self.scaled[:, g % self.SLOTS, :], self.hidden[:, g % self.SLOTS, :],
                                     self.wsb[:, g % 2, :], ALU.mult).then_inc(self.scaled_ready.sem, 1)


class Routing:

    def __init__(self, pg, ctx, name, experts, top, shared, over_all, bias=None):
        nc = self.nc = pg.nc
        self.pg, self.E, self.top, self.shared, self.over_all, self.bias = pg, experts, top, shared, over_all, bias
        self.cols = experts + (1 if shared else 0)
        sb = lambda s, dims: ctx.enter_context(nc.sbuf_tensor(f"{name}_{s}", [P, *dims], F32))
        E = experts
        self.logits, self.comb = sb("logits", [T, self.cols]), sb("comb", [T, self.cols])
        self.beats, self.ties = sb("beats", [T, E, E]), sb("ties", [T, E, E])
        self.rank, self.top1, self.shifted = sb("rank", [T, E]), sb("top1", [T]), sb("shifted", [T, self.cols])
        self.exps, self.total = sb("exps", [T, self.cols]), sb("total", [T])
        self.shifted_ready = Signal(ctx, nc, "shifted_ready", 1)
        self.exps_ready = Signal(ctx, nc, "exps_ready", 1)
        self.comb_ready = Signal(ctx, nc, "comb_ready", 1)
        self.steps = 9 + (1 if bias is not None else 0) + (2 if shared else 0)

    def project(self, pe, i, acc, k, xT, gate):
        for t in range(T):
            last = project_tokens(self.nc, acc.bank(k)[:, t * self.cols:(t + 1) * self.cols], gate, xT, t)
        last.then_inc(acc.full.sem, 1)

    def take_logits(self, act, i, acc, k):
        acc.wait_full(act, i, k)
        self.nc.scalar.activation(self.logits[:], shaped(acc.bank(k)[:, 0:T * self.cols], (T, self.cols)), ACT.Copy)\
            .then_inc(acc.empty.sem, 1)

    def scalar(self, act, i):
        act.wait_ge(self.shifted_ready.sem, self.shifted_ready.at(i, 1))
        self.nc.scalar.activation(self.exps[:], self.shifted[:], ACT.Exp).then_inc(self.exps_ready.sem, 1)

    def vector(self, dve, i, chain, acc, k):
        nc, E = self.nc, self.E
        acc.wait_emptied(dve, i, k)
        l = self.logits[:, :, 0:E]
        if self.bias is not None:
            chain.step(nc.vector.tensor_tensor(l, l, over(self.bias, 1, T), ALU.add))
        for t in range(T):
            mine, other = over(l[:, t, :], 2, E), over(l[:, t, :], 1, E)
            nc.vector.tensor_tensor(self.beats[:, t, :, :], other, mine, ALU.is_gt)
            last = nc.vector.tensor_tensor(self.ties[:, t, :, :], other, mine, ALU.is_equal)
        chain.step(last)
        tri = shaped(self.pg.c("tri"), (8, 8))[:, 0:E, 0:E]
        chain.step(nc.vector.tensor_tensor(self.ties[:], self.ties[:], over(tri, 1, T), ALU.mult))
        chain.step(nc.vector.tensor_tensor(self.beats[:], self.beats[:], self.ties[:], ALU.add))
        chain.step(nc.vector.tensor_reduce(self.rank[:], self.beats[:], AX, ALU.add))
        chain.step(nc.vector.tensor_reduce(self.top1[:], l, AX, ALU.max))
        if self.shared:
            chain.step(nc.vector.tensor_scalar(self.shifted[:, :, E:E + 1], self.logits[:, :, E:E + 1], -1.0, None, ALU.mult))
        nc.vector.tensor_tensor(self.shifted[:, :, 0:E], l, over(self.top1[:], 2, E), ALU.subtract)\
            .then_inc(self.shifted_ready.sem, 1)
        chain.step(nc.vector.tensor_scalar(self.rank[:], self.rank[:], float(self.top), None, ALU.is_lt))
        dve.wait_ge(self.exps_ready.sem, self.exps_ready.at(i, 1))
        e, c = self.exps[:, :, 0:E], self.comb[:, :, 0:E]
        chain.step(nc.vector.tensor_tensor(c, e, self.rank[:], ALU.mult))
        chain.step(nc.vector.tensor_reduce(self.total[:], e if self.over_all else c, AX, ALU.add))
        chain.step(nc.vector.reciprocal(self.total[:], self.total[:]))
        if self.shared:
            z = self.comb[:, :, E:E + 1]
            chain.step(nc.vector.tensor_scalar(z, self.exps[:, :, E:E + 1], 1.0, None, ALU.add))
            nc.vector.reciprocal(z, z)
        nc.vector.tensor_tensor(c, c, over(self.total[:], 2, E), ALU.mult).then_inc(self.comb_ready.sem, 1)


def weighted_experts(pg, n, experts, top, shared, tiles):
    nc = pg.nc
    with Scope(nc, f"s{n}") as ctx:
        route = Routing(pg, ctx, f"s{n}", experts, top, shared, over_all=False)
        body = Body(pg, ctx, 3, route.steps, f"s{n}")
        acc = body.acc
        ff = GatedTiles(pg, ctx, f"s{n}", tiles, [pg.bank[2], pg.bank[3], pg.bank[7]], pg.bank[5:7])
        cols = route.cols
        combT = ctx.enter_context(nc.sbuf_tensor(f"s{n}_combT", [cols, S], F32))
        gate = pg.w(n, "gate", KD, cols)
        wg, wu, wd = pg.w(n, "g", tiles, KD, P), pg.w(n, "u", tiles, KD, P), pg.w(n, "d", tiles, D)
        owner, y_bank = pg.w(n, "owner", rows=cols), pg.bank[4]
        with nc.Block() as block:
            prefetch(pg, block, n)

            @block.gpsimd
            def _(pool):
                start(pg, pool, n)
                ff.credits(pool=pool)
                with pool.Fori(0, B) as i:
                    body.stage(pool, i)
                    for g in range(tiles):
                        ff.pool(pool, i, g)
                    body.roots(pool, i)

            @block.tensor
            def _(pe):
                start(pg, pe, n)
                ff.credits(pe=pe)
                with pe.Fori(0, B) as i:
                    body.transpose_x(pe, i)
                    acc.wait_emptied(pe, i, 0)
                    acc.wait_empty(pe, i, 1)
                    route.project(pe, i, acc, 1, body.xT, gate)
                    for s in range(tiles + 3):
                        if s < tiles:
                            ff.gate_up(pe, i, s, body.xT, wg, wu)
                        if s == 2:
                            pe.wait_ge(route.comb_ready.sem, route.comb_ready.at(i, 1))
                            acc.wait_empty(pe, i, 2)
                            for t in range(T):
                                last = nc.tensor.transpose(acc.bank(2)[0:cols, t * P:(t + 1) * P], route.comb[:, t, :],
                                                           pg.c("ident"))
                            last.then_inc(acc.full.sem, 1)
                            acc.wait_emptied(pe, i, 2)
                        if 0 <= s - 2 < tiles:
                            ff.spread_weights(pe, i, s - 2, owner, combT[:])
                        if s == 3:
                            pe.wait_ge(body.out_taken.sem, body.out_taken.at(i, 0))
                        if 0 <= s - 3 < tiles:
                            ff.down(pe, i, s - 3, wd, y_bank, first=(s == 3), last_one=(s - 3 == tiles - 1))

            @block.scalar
            def _(act):
                start(pg, act, n)
                acc.empty.give(act)
                ff.credits(act=act)
                with act.Fori(0, B) as i:
                    body.take_xT(act, i)
                    route.take_logits(act, i, acc, 1)
                    ff.scalar(act, i, 0)
                    route.scalar(act, i)
                    acc.wait_full(act, i, 2)
                    nc.scalar.activation(combT[:], acc.bank(2)[0:cols, 0:S], ACT.Copy).then_inc(acc.empty.sem, 1)
                    for g in range(tiles):
                        if g:
                            ff.scalar(act, i, g)
                        ff.scalar_weights(act, i, g)

            @block.vector
            def _(dve):
                start(pg, dve, n)
                body.out_taken.give(dve)
                ff.credits(dve=dve)
                with dve.Fori(0, B) as i:
                    chain = Chain(body.vchain, dve, i)
                    route.vector(dve, i, chain, acc, 1)
                    for g in range(tiles):
                        ff.vector(dve, i, g)
                    dve.wait_ge(ff.down_done.sem, ff.down_done.at(i, tiles))
                    body.add_norm(dve, i, chain, y_bank, wait_out=False)
                    chain.done()


def top1_experts(pg, n):
    nc = pg.nc
    E, per, tiles = 4, 8, 32
    with Scope(nc, f"s{n}") as ctx:
        route = Routing(pg, ctx, f"s{n}", E, 1, False, over_all=True, bias=pg.w(n, "br"))
        body = Body(pg, ctx, 2, route.steps, f"s{n}")
        acc = body.acc
        ff = GatedTiles(pg, ctx, f"s{n}", tiles, [pg.bank[2], pg.bank[3], pg.bank[5]])
        gate = pg.w(n, "gate", KD, E)
        wg, wu, wd = pg.w(n, "g", tiles, KD, P), pg.w(n, "u", tiles, KD, P), pg.overflow(n, tiles, D)
        y_banks = [pg.bank[4], pg.bank[7]]
        expert_taken = Signal(ctx, nc, "expert_taken", E, credit=2)
        with nc.Block() as block:
            prefetch(pg, block, n)

            @block.gpsimd
            def _(pool):
                start(pg, pool, n)
                with pool.Fori(0, B) as i:
                    body.stage(pool, i)
                    body.roots(pool, i)

            @block.tensor
            def _(pe):
                start(pg, pe, n)
                ff.credits(pe=pe)
                with pe.Fori(0, B) as i:
                    body.transpose_x(pe, i)
                    acc.wait_emptied(pe, i, 0)
                    acc.wait_empty(pe, i, 1)
                    route.project(pe, i, acc, 1, body.xT, gate)
                    for s in range(tiles + 2):
                        if s < tiles:
                            ff.gate_up(pe, i, s, body.xT, wg, wu)
                        g = s - 2
                        if 0 <= g < tiles:
                            e = g // per
                            if g % per == 0:
                                pe.wait_ge(expert_taken.sem, expert_taken.at(i, e + 1 - 2))
                            ff.down(pe, i, g, wd, y_banks[e % 2], first=(g % per == 0), last_one=(g % per == per - 1))

            @block.scalar
            def _(act):
                start(pg, act, n)
                acc.empty.give(act)
                with act.Fori(0, B) as i:
                    body.take_xT(act, i)
                    route.take_logits(act, i, acc, 1)
                    ff.scalar(act, i, 0)
                    route.scalar(act, i)
                    for g in range(1, tiles):
                        ff.scalar(act, i, g)

            @block.vector
            def _(dve):
                start(pg, dve, n)
                expert_taken.give(dve)
                ff.credits(dve=dve)
                with dve.Fori(0, B) as i:
                    chain = Chain(body.vchain, dve, i)
                    route.vector(dve, i, chain, acc, 1)

                    def take(e):
                        dve.wait_ge(ff.down_done.sem, ff.down_done.at(i, (e + 1) * per))
                        y = shaped(y_banks[e % 2][:], (T, D))
                        for t in range(T):
                            before = pg.x[:, i, t, :] if e == 0 else body.r[:, t, :]
                            last = nc.vector.scalar_tensor_tensor(out=body.r[:, t, :], in0=y[:, t, :],
                                                                  scalar=route.comb[:, t, e:e + 1], in1=before,
                                                                  op0=ALU.mult, op1=ALU.add)
                        last.then_inc(expert_taken.sem, 1)
                        dve.wait_ge(expert_taken.sem, expert_taken.at(i, e + 1))
                    dve.wait_ge(route.comb_ready.sem, route.comb_ready.at(i, 1))
                    for g in range(tiles):
                        ff.vector(dve, i, g)
                        if g % per == 3 and g > per:
                            take(g // per - 1)
                    take(E - 1)
                    body.norm(dve, i, chain)
                    chain.done()


def modulated_ffn(pg, n):
    nc = pg.nc
    R, tiles = 16, 8
    with Scope(nc, f"s{n}") as ctx:
        causal = pg.c("causal")
        units = pair_units([[(0, P, causal)], [(P, S, causal)]], [P, S])
        body = Body(pg, ctx, 6, attention_steps(units, False), f"s{n}", roots=(T,))
        att = Attention(pg, ctx, f"s{n}", units, False, pg.bank[2:5])
        ff = GatedTiles(pg, ctx, f"s{n}", tiles, pg.bank[2:4])
        acc = body.acc
        sb = lambda s, dims, p=P: ctx.enter_context(nc.sbuf_tensor(f"s{n}_{s}", [p, *dims], F32))
        x_rms, h1T, h2T = sb("x_rms", [T, D]), sb("h1T", [KD, S]), sb("h2T", [KD, S])
        squares, sumsq = sb("squares", [T, D]), sb("sumsq", [T])
        qT, kblk, vpad = sb("qT", [KD, S]), sb("kblk", [KD, 2, S]), sb("vpad", [T, 8, 2, 32])
        oT, attnT = sb("oT", [KD, S]), sb("attnT", [KD, S])
        mod, hA, prod = sb("mod", [S], R), sb("hA", [S], R), sb("prod", [S], R)
        o_taken = Signal(ctx, nc, "o_taken", 1, credit=1)
        padded = Signal(ctx, nc, "padded", 0)
        summed = Signal(ctx, nc, "summed", 1)
        rms_ready = Signal(ctx, nc, "rms_ready", 1)
        mod_ready = Signal(ctx, nc, "mod_ready", 1)
        w = {k: pg.w(n, k, KD, D) for k in ("q", "k", "v", "o")}
        A, Bw = pg.w(n, "A", KD, R), pg.w(n, "B", rows=R)
        wg, wu, wd = pg.w(n, "g", tiles, KD, P), pg.w(n, "u", tiles, KD, P), pg.w(n, "d", tiles, D)
        o_bank, y_bank = pg.bank[7], pg.bank[4]
        with nc.Block() as block:
            prefetch(pg, block, n)

            @block.gpsimd
            def _(pool):
                start(pg, pool, n)

                def head(i):
                    body.stage_first(pool)
                    body.root[0].power(pool, i)

                def tail(i, more):
                    if more:
                        pool.wait_ge(rms_ready.sem, rms_ready.at(i, 1))
                        nc.gpsimd.tensor_copy(body.xs[:], pg.x[:, i + 1, :, :]).then_inc(body.x_staged.sem, 1)
                    att.gpsimd(pool, i)
                    if more:
                        body.root[0].power(pool, i + 1)
                    body.root[1].power(pool, i)
                batches(pool, head, tail)

            @block.tensor
            def _(pe):
                start(pg, pe, n)
                att.credits_tensor(pe)
                ff.credits(pe=pe)

                def projections(i):
                    def x():
                        pe.wait_ge(rms_ready.sem, rms_ready.at(i, 1))
                        acc.wait_empty(pe, i, 0)
                        transpose_tokens(nc, pe, acc.bank(0), x_rms, pg.c("ident")).then_inc(acc.full.sem, 1)
                        acc.wait_emptied(pe, i, 0)

                    def features(k, name):
                        acc.wait_empty(pe, i, k)
                        project_features(nc, acc.bank(k), w[name], h1T).then_inc(acc.full.sem, 1)

                    def values():
                        acc.wait_empty(pe, i, 3)
                        for t in range(T):
                            last = project_tokens(nc, acc.bank(3)[:, t * D:(t + 1) * D], w["v"], h1T, t)
                        last.then_inc(acc.full.sem, 1)
                    return [x, lambda: features(1, "q"), lambda: features(2, "k"), values]

                def head(i):
                    for piece in projections(i):
                        piece()

                def modulate(i, out, g):
                    if g == 0:
                        pe.wait_ge(mod_ready.sem, mod_ready.at(i, 1))
                    return nc.tensor.matmul(out, Bw[:, g * P:(g + 1) * P], prod[:], start=False, stop=True)

                def tail(i, more):
                    acc.wait_emptied(pe, i, 3)
                    att.tensor(pe, i, lambda k, u, part, bank: pair_scores(nc, u, qT, kblk, bank),
                               lambda s, u, probsT: pair_values(nc, u, probsT, o_bank, lambda c, g, j: vpad[:, c, g, j, :]),
                               before_last_bank=lambda: pe.wait_ge(body.out_taken.sem, body.out_taken.at(i, 0)),
                               before_values=lambda: pe.wait_ge(o_taken.sem, o_taken.at(i, 0)))
                    pe.wait_ge(o_taken.sem, o_taken.at(i, 1))
                    acc.wait_empty(pe, i, 4)
                    project_features(nc, acc.bank(4), w["o"], oT).then_inc(acc.full.sem, 1)
                    acc.wait_emptied(pe, i, 4)
                    acc.wait_empty(pe, i, 5)
                    for half, src in enumerate((attnT, h2T)):
                        for k in range(KD):
                            last = nc.tensor.matmul(acc.bank(5)[0:R, half * S:(half + 1) * S], A[:, k, :], src[:, k, :],
                                                    start=(k == 0), stop=(k == KD - 1))
                    last.then_inc(acc.full.sem, 1)
                    for s in range(tiles + 2):
                        if s < tiles:
                            ff.gate_up(pe, i, s, h2T, wg, wu, extra=lambda out, g: modulate(i, out, g))
                        if s == 2:
                            pe.wait_ge(body.out_taken.sem, body.out_taken.at(i, 0))
                        if s >= 2:
                            ff.down(pe, i, s - 2, wd, y_bank, first=(s == 2), last_one=(s == tiles + 1))
                    if more:
                        head(i + 1)
                batches(pe, head, tail)

            @block.scalar
            def _(act):
                start(pg, act, n)
                acc.empty.give(act)
                att.credits_scalar(act)
                o_taken.give(act)
                act.wait_ge(padded.sem, 1)
                view = lambda k: shaped(acc.bank(k)[:], (KD, S))

                def sum_squares(i):
                    act.wait_ge(body.x_staged.sem, body.x_staged.at(i, 1))
                    for t in range(T):
                        last = nc.scalar.activation(squares[:, t, :], body.xs[:, t, :], ACT.Square,
                                                    accum_out=sumsq[:, t:t + 1])
                    last.then_inc(summed.sem, 1)

                def takes(i):
                    acc.wait_full(act, i, 0)
                    for name, dst in (("ln1", h1T), ("ln2", h2T)):
                        for k in range(KD):
                            last = nc.scalar.activation(dst[:, k, :], acc.bank(0)[:, k * S:(k + 1) * S], ACT.Copy,
                                                        scale=pg.w(n, name)[:, k:k + 1])
                    last.then_inc(acc.empty.sem, 1)
                    acc.wait_full(act, i, 1)
                    nc.scalar.activation(qT[:], view(1), ACT.Copy, scale=0.25).then_inc(acc.empty.sem, 1)
                    acc.wait_full(act, i, 2)
                    spread_keys(nc, kblk, view(2), pg.c("par2")).then_inc(acc.empty.sem, 1)
                    acc.wait_full(act, i, 3)
                    pad_values(nc, vpad, view(3)).then_inc(acc.empty.sem, 1)

                def head(i):
                    sum_squares(i)
                    takes(i)

                def tail(i, more):
                    att.scalar(act, i)
                    act.wait_ge(att.valued.sem, att.valued.at(i, len(units)))
                    nc.scalar.activation(oT[:], shaped(o_bank[:], (KD, S)), ACT.Copy).then_inc(o_taken.sem, 1)
                    acc.wait_full(act, i, 4)
                    nc.scalar.activation(attnT[:], view(4), ACT.Copy).then_inc(acc.empty.sem, 1)
                    acc.wait_full(act, i, 5)
                    nc.scalar.activation(mod[:], acc.bank(5)[0:R, 0:S], ACT.Tanh)
                    nc.scalar.activation(hA[:], acc.bank(5)[0:R, S:2 * S], ACT.Copy).then_inc(acc.empty.sem, 1)
                    if more:
                        sum_squares(i + 1)
                    for g in range(tiles):
                        ff.scalar(act, i, g)
                    if more:
                        takes(i + 1)
                batches(act, head, tail)

            @block.vector
            def _(dve):
                start(pg, dve, n)
                body.out_taken.give(dve)
                nc.vector.memset(vpad[:], 0.0).then_inc(padded.sem, 1)
                att.credits_vector(dve)
                ff.credits(dve=dve)

                def head(i):
                    dve.wait_ge(summed.sem, summed.at(i, 1))
                    nc.vector.tensor_scalar(body.root[0].t[:], sumsq[:], 1.0 / D, RMS_EPS, ALU.mult, ALU.add)\
                        .then_inc(body.root[0].wanted.sem, 1)
                    body.root[0].wait(dve, i)
                    nc.vector.tensor_tensor(x_rms[:], body.xs[:], over(body.root[0].t[:], 2, D), ALU.mult)\
                        .then_inc(rms_ready.sem, 1)

                def tail(i, more):
                    chain = Chain(body.vchain, dve, i)
                    att.vector(dve, i, chain)
                    acc.wait_emptied(dve, i, 5)
                    nc.vector.scalar_tensor_tensor(out=prod[:], in0=mod[:], scalar=0.1, in1=hA[:],
                                                   op0=ALU.mult, op1=ALU.mult).then_inc(mod_ready.sem, 1)
                    for g in range(tiles):
                        ff.vector(dve, i, g)
                    if more:
                        head(i + 1)
                    dve.wait_ge(ff.down_done.sem, ff.down_done.at(i, tiles))
                    body.add_norm(dve, i, chain, y_bank, x_times=2.0, wait_out=False)
                    chain.done()
                batches(dve, head, tail)


def windowed_attention(pg, n):
    nc = pg.nc
    HK = 4
    H = NH + HK
    with Scope(nc, f"s{n}") as ctx:
        near, before = pg.c("near"), pg.c("before")
        units = pair_units([[(0, P, near)], [(0, P, before), (P, S, near)]], [P, S])
        body = Body(pg, ctx, 5, attention_steps(units, False), f"s{n}", roots=(T * H,))
        att = Attention(pg, ctx, f"s{n}", units, False, pg.bank[2:5])
        acc = body.acc
        sb = lambda s, dims: ctx.enter_context(nc.sbuf_tensor(f"s{n}_{s}", [P, *dims], F32))
        qk, turned, v = sb("qk", [T, H, HD]), sb("turned", [T, H, HD]), sb("v", [T, HK, HD])
        sumsq, krep = sb("sumsq", [T, H]), sb("krep", [T, NH, HD])
        qT, kblk, oT, vpad = sb("qT", [KD, S]), sb("kblk", [KD, 2, S]), sb("oT", [KD, S]), sb("vpad", [T, HK, 2, 32])
        o_taken = Signal(ctx, nc, "o_taken", 1, credit=1)
        padded = Signal(ctx, nc, "padded", 0)
        v_ready = Signal(ctx, nc, "v_ready", 1)
        unit_steps = Signal(ctx, nc, "unit_steps", 7)
        unit_ready = Signal(ctx, nc, "unit_ready", 1)
        w, wo = pg.w(n, "w", KD, D + 2 * HK * HD), pg.w(n, "wo", KD, D)
        o_bank, y_bank = pg.bank[7], pg.bank[4]
        with nc.Block() as block:
            prefetch(pg, block, n)

            @block.gpsimd
            def _(pool):
                start(pg, pool, n)

                def head(i):
                    body.root[0].power(pool, i)

                def tail(i, more):
                    if more:
                        body.stage_next(pool, i)
                    att.gpsimd(pool, i)
                    if more:
                        head(i + 1)
                    body.root[1].power(pool, i)
                batches(pool, lambda i: (body.stage_first(pool), head(i)), tail)

            @block.tensor
            def _(pe):
                start(pg, pe, n)
                att.credits_tensor(pe)

                def projections(i):
                    def x():
                        body.transpose_x(pe, i)
                        acc.wait_emptied(pe, i, 0)

                    def tokens(k, lo, hi):
                        acc.wait_empty(pe, i, k)
                        for t in range(T):
                            last = project_tokens(nc, acc.bank(k)[:, t * (hi - lo):(t + 1) * (hi - lo)],
                                                  w[:, :, lo:hi], body.xT, t)
                        last.then_inc(acc.full.sem, 1)
                    return [x, lambda: tokens(1, 0, D), lambda: tokens(2, D, D + 2 * HK * HD)]

                def turn(i):
                    pe.wait_ge(unit_ready.sem, unit_ready.at(i, 1))
                    for fill, src in ((3, qk), (4, krep)):
                        acc.wait_empty(pe, i, fill)
                        for t in range(T):
                            for k in range(KD):
                                last = nc.tensor.transpose(acc.bank(fill)[:, k * S + t * P:k * S + (t + 1) * P],
                                                           src[:, t, k * 8:(k + 1) * 8, :].rearrange("p h d -> p (h d)"),
                                                           pg.c("ident"))
                        last.then_inc(acc.full.sem, 1)

                def head(i):
                    for piece in projections(i):
                        piece()
                    turn(i)

                def before_values(i):
                    pe.wait_ge(o_taken.sem, o_taken.at(i, 0))
                    pe.wait_ge(v_ready.sem, v_ready.at(i, 1))

                def tail(i, more):
                    acc.wait_emptied(pe, i, 4)
                    att.tensor(pe, i, lambda k, u, part, bank: pair_scores(nc, u, qT, kblk, bank),
                               lambda s, u, probsT: pair_values(nc, u, probsT, o_bank,
                                                                lambda c, g, j: vpad[:, c, g // 2, j, :]),
                               before_last_bank=lambda: pe.wait_ge(body.out_taken.sem, body.out_taken.at(i, 0)),
                               before_values=lambda: before_values(i), pieces=projections(i + 1) if more else ())
                    pe.wait_ge(o_taken.sem, o_taken.at(i, 1))
                    body.project_out(pe, i, oT, wo, y_bank, KD)
                    if more:
                        turn(i + 1)
                batches(pe, head, tail)

            @block.scalar
            def _(act):
                start(pg, act, n)
                acc.empty.give(act)
                att.credits_scalar(act)
                o_taken.give(act)
                act.wait_ge(padded.sem, 1)

                def takes(i):
                    def queries():
                        acc.wait_full(act, i, 1)
                        nc.scalar.activation(qk[:, :, 0:NH, :].rearrange("p t h d -> p t (h d)"),
                                             shaped(acc.bank(1)[:], (T, D)), ACT.Copy).then_inc(acc.empty.sem, 1)

                    def keys_values():
                        acc.wait_full(act, i, 2)
                        kv = shaped(acc.bank(2)[:, 0:T * 2 * HK * HD], (T, 2, HK * HD))
                        nc.scalar.activation(qk[:, :, NH:H, :].rearrange("p t h d -> p t (h d)"), kv[:, :, 0, :], ACT.Copy)
                        nc.scalar.activation(v[:].rearrange("p t h d -> p t (h d)"), kv[:, :, 1, :], ACT.Copy)\
                            .then_inc(acc.empty.sem, 1)
                    return [lambda: body.take_xT(act, i), queries, keys_values]

                def turned_ones(i):
                    acc.wait_emptied(act, i, 2)
                    for j in range(2):
                        last = nc.scalar.activation(vpad[:, :, :, j, j * HD:(j + 1) * HD].rearrange("p t g d -> p (t g) d"),
                                                    v[:].rearrange("p t g d -> p (t g) d"), ACT.Copy)
                    last.then_inc(v_ready.sem, 1)
                    acc.wait_full(act, i, 3)
                    nc.scalar.activation(qT[:], shaped(acc.bank(3)[:], (KD, S)), ACT.Copy).then_inc(acc.empty.sem, 1)
                    acc.wait_full(act, i, 4)
                    spread_keys(nc, kblk, shaped(acc.bank(4)[:], (KD, S)), pg.c("par2")).then_inc(acc.empty.sem, 1)

                def head(i):
                    for take in takes(i):
                        take()
                    turned_ones(i)

                def tail(i, more):
                    att.scalar(act, i, takes(i + 1) if more else ())
                    act.wait_ge(att.valued.sem, att.valued.at(i, len(units)))
                    nc.scalar.activation(oT[:], shaped(o_bank[:], (KD, S)), ACT.Copy).then_inc(o_taken.sem, 1)
                    if more:
                        turned_ones(i + 1)
                batches(act, head, tail)

            @block.vector
            def _(dve):
                start(pg, dve, n)
                body.out_taken.give(dve)
                nc.vector.memset(vpad[:], 0.0).then_inc(padded.sem, 1)
                att.credits_vector(dve)
                cos, sin = (over(shaped(pg.c(k), (T, HD)), 2, H) for k in ("cos", "sin"))
                half = HD // 2

                def head(i):
                    chain = Chain(unit_steps, dve, i)
                    acc.wait_emptied(dve, i, 2)
                    nc.vector.tensor_tensor(turned[:, :, :, 0:half], qk[:, :, :, half:HD], sin[:, :, :, 0:half], ALU.mult)
                    chain.step(nc.vector.tensor_tensor(turned[:, :, :, half:HD], qk[:, :, :, 0:half],
                                                       sin[:, :, :, half:HD], ALU.mult))
                    chain.step(nc.vector.tensor_tensor(qk[:], qk[:], cos, ALU.mult))
                    chain.step(nc.vector.tensor_tensor(qk[:], qk[:], turned[:], ALU.add))
                    chain.step(nc.vector.tensor_tensor(turned[:], qk[:], qk[:], ALU.mult))
                    chain.step(nc.vector.tensor_reduce(sumsq[:], turned[:], AX, ALU.add))
                    nc.vector.tensor_scalar(body.root[0].t[:], flat(sumsq[:]), 1e-24, None, ALU.max)\
                        .then_inc(body.root[0].wanted.sem, 1)
                    body.root[0].wait(dve, i)
                    rt = shaped(body.root[0].t[:], (T, H))
                    chain.step(nc.vector.tensor_tensor(rt[:, :, 0:NH], rt[:, :, 0:NH], over(pg.w(n, "temp"), 1, T), ALU.mult))
                    chain.step(nc.vector.tensor_tensor(qk[:], qk[:], over(rt, 3, HD), ALU.mult))
                    for t in range(T):
                        last = nc.vector.tensor_copy(krep[:, t, :, :].rearrange("p (g r) d -> p g r d", g=HK),
                                                     over(qk[:, t, NH:H, :], 2, NH // HK))
                    last.then_inc(unit_ready.sem, 1)
                    chain.done()

                def tail(i, more):
                    chain = Chain(body.vchain, dve, i)
                    att.vector(dve, i, chain)
                    if more:
                        head(i + 1)
                    body.add_norm(dve, i, chain, y_bank)
                    chain.done()
                batches(dve, head, tail)


def decay_attention(pg, n):
    nc = pg.nc
    W = S + P
    with Scope(nc, f"s{n}") as ctx:
        body = Body(pg, ctx, 6, 3, f"s{n}", roots=(T,))
        acc = body.acc
        sb = lambda s, dims: ctx.enter_context(nc.sbuf_tensor(f"s{n}_{s}", [P, *dims], F32))
        sig = lambda s, per, credit=0: Signal(ctx, nc, s, per, credit)
        raw, th = sb("raw", [2, KD, S]), sb("th", [2, KD, S])
        q2T, k2T, kblk, v, u = sb("q2T", [KD, S]), sb("k2T", [KD, S]), sb("kblk", [KD, 2, S]), sb("v", [T, D]), sb("u", [T, D])
        o, oT, squares, sumsq = sb("o", [T, D]), sb("oT", [KD, S]), sb("squares", [T, D]), sb("sumsq", [T])
        weighted = sb("weighted", [3, W])
        decay = pg.spare(n, 0, NH, W)
        minus_slope = pg.spare(n, NH * W, NH)
        slope_ready, exps_done, decay_ready = sig("slope_ready", 1), sig("exps_done", 1), sig("decay_ready", 1)
        keys_ready = sig("keys_ready", 1)
        scored = sig("scored", NH)
        s_banks = [pg.bank[2], pg.bank[3], pg.bank[5], pg.bank[6]]
        weighted_ready = sig("weighted_ready", NH, len(s_banks))
        valued = sig("valued", NH, 3)
        o_taken = sig("o_taken", 1, 1)
        o_ready = sig("o_ready", 1)
        w, wo = pg.w(n, "w", KD, 4 * D), pg.w(n, "wo", KD, D)
        o_bank, y_bank = pg.bank[7], pg.bank[4]
        with nc.Block() as block:
            prefetch(pg, block, n)

            @block.gpsimd
            def _(pool):
                start(pg, pool, n)
                with pool.Fori(0, B) as i:
                    body.stage(pool, i)
                    body.roots(pool, i)

            @block.tensor
            def _(pe):
                start(pg, pe, n)
                valued.give(pe)
                with pe.Fori(0, B) as i:
                    body.transpose_x(pe, i)
                    acc.wait_emptied(pe, i, 0)
                    for k in range(2):
                        acc.wait_empty(pe, i, 1 + k)
                        project_features(nc, acc.bank(1 + k), w[:, :, k * D:(k + 1) * D], body.xT).then_inc(acc.full.sem, 1)
                    for k in range(2, 4):
                        acc.wait_empty(pe, i, 1 + k)
                        for t in range(T):
                            last = project_tokens(nc, acc.bank(1 + k)[:, t * D:(t + 1) * D], w[:, :, k * D:(k + 1) * D],
                                                  body.xT, t)
                        last.then_inc(acc.full.sem, 1)
                    pe.wait_ge(keys_ready.sem, keys_ready.at(i, 1))
                    acc.wait_emptied(pe, i, 3)
                    for s in range(NH + 2):
                        if s < NH:
                            pe.wait_ge(weighted_ready.sem, weighted_ready.at(i, s + 1 - len(s_banks)))
                            r, m, j = 32 * (s % 8 // 2), s // 8, s % 2
                            for c in range(T):
                                last = nc.tensor.matmul(s_banks[s % 4][:, c * S:c * S + S - c * P],
                                                        kblk[r:r + 32, m, j, c * P:(c + 1) * P],
                                                        q2T[r:r + 32, m, c * P:S], start=True, stop=True)
                            last.then_inc(scored.sem, 1)
                        h = s - 2
                        if h == 0:
                            pe.wait_ge(o_taken.sem, o_taken.at(i, 0))
                        if h >= 0:
                            pe.wait_ge(weighted_ready.sem, weighted_ready.at(i, h + 1))
                            p = weighted[:, h % 3, :]
                            cols = slice(h * HD, (h + 1) * HD)
                            nc.tensor.matmul(o_bank[:, cols], p[:, 0:P], v[:, 0, cols], start=True, stop=True)
                            late = o_bank[:, D + h * HD:D + (h + 1) * HD]
                            nc.tensor.matmul(late, p[:, P:S], v[:, 0, cols], start=True, stop=False)
                            nc.tensor.matmul(late, p[:, S:W], v[:, 1, cols], start=False, stop=True)\
                                .then_inc(valued.sem, 1)
                    pe.wait_ge(o_ready.sem, o_ready.at(i, 1))
                    acc.wait_empty(pe, i, 5)
                    transpose_tokens(nc, pe, acc.bank(5), o, pg.c("ident")).then_inc(acc.full.sem, 1)
                    acc.wait_emptied(pe, i, 5)
                    body.project_out(pe, i, oT, wo, y_bank, KD)

            @block.scalar
            def _(act):
                start(pg, act, n)
                acc.empty.give(act)
                act.wait_ge(slope_ready.sem, 1)
                for h in range(NH):
                    last = nc.scalar.activation(decay[:, h, 0:S], pg.w(n, "dist"), ACT.Exp, scale=minus_slope[:, h:h + 1])
                last.then_inc(exps_done.sem, 1)
                with act.Fori(0, B) as i:
                    body.take_xT(act, i)
                    for k in range(2):
                        acc.wait_full(act, i, 1 + k)
                        view = shaped(acc.bank(1 + k)[:], (KD, S))
                        nc.scalar.activation(raw[:, k, :, :], view, ACT.Copy)
                        nc.scalar.activation(th[:, k, :, :], view, ACT.Tanh, scale=0.5).then_inc(acc.empty.sem, 1)
                    for k, dst in ((3, v), (4, u), (5, oT)):
                        acc.wait_full(act, i, k)
                        nc.scalar.activation(dst[:], shaped(acc.bank(k)[:], (KD, S)), ACT.Copy).then_inc(acc.empty.sem, 1)

            @block.vector
            def _(dve):
                start(pg, dve, n)
                body.out_taken.give(dve)
                weighted_ready.give(dve)
                o_taken.give(dve)
                nc.vector.tensor_scalar(minus_slope, pg.w(n, "slope"), -1.0, None, ALU.mult).then_inc(slope_ready.sem, 1)
                dve.wait_ge(exps_done.sem, 1)
                for h in range(NH):
                    last = nc.vector.scalar_tensor_tensor(out=decay[:, h, 0:S], in0=decay[:, h, 0:S], scalar=0.25,
                                                          in1=pg.w(n, "valid"), op0=ALU.mult, op1=ALU.mult)
                last.then_inc(decay_ready.sem, 1)
                dve.wait_ge(decay_ready.sem, 1)
                nc.vector.tensor_copy(decay[:, :, S:W], decay[:, :, 0:P]).then_inc(decay_ready.sem, 1)
                dve.wait_ge(decay_ready.sem, 2)
                with dve.Fori(0, B) as i:
                    chain = Chain(body.vchain, dve, i)
                    acc.wait_emptied(dve, i, 2)
                    for k, dst in ((0, q2T), (1, k2T)):
                        last = nc.vector.scalar_tensor_tensor(out=dst[:], in0=th[:, k, :, :], scalar=1.0,
                                                              in1=raw[:, k, :, :], op0=ALU.add, op1=ALU.mult)
                    chain.step(last)
                    for par in range(2):
                        last = nc.vector.tensor_scalar(kblk[:, :, par, :], k2T[:], pg.c("par2")[:, par:par + 1], None,
                                                       ALU.mult)
                    last.then_inc(keys_ready.sem, 1)
                    for h in range(NH):
                        dve.wait_ge(scored.sem, scored.at(i, h + 1))
                        dve.wait_ge(valued.sem, valued.at(i, h + 1 - 3))
                        nc.vector.tensor_tensor(weighted[:, h % 3, :], s_banks[h % 4][:, 0:W], decay[:, h, :], ALU.mult)\
                            .then_inc(weighted_ready.sem, 1)
                    dve.wait_ge(valued.sem, valued.at(i, NH))
                    nc.vector.tensor_copy(o[:], shaped(o_bank[:], (T, D))).then_inc(o_taken.sem, 1)
                    dve.wait_ge(o_taken.sem, o_taken.at(i, 1))
                    chain.step(nc.vector.tensor_tensor(squares[:], o[:], o[:], ALU.mult))
                    chain.step(nc.vector.tensor_reduce(sumsq[:], squares[:], AX, ALU.add))
                    nc.vector.tensor_scalar(body.root[0].t[:], sumsq[:], 1.0 / D, RMS_EPS, ALU.mult, ALU.add)\
                        .then_inc(body.root[0].wanted.sem, 1)
                    body.root[0].wait(dve, i)
                    acc.wait_emptied(dve, i, 4)
                    for t in range(T):
                        last = nc.vector.scalar_tensor_tensor(out=o[:, t, :], in0=o[:, t, :],
                                                              scalar=body.root[0].t[:, t:t + 1], in1=u[:, t, :],
                                                              op0=ALU.mult, op1=ALU.mult)
                    last.then_inc(o_ready.sem, 1)
                    body.add_norm(dve, i, chain, y_bank)
                    chain.done()


def head_attention(pg, n):
    nc = pg.nc
    HG = 8
    units = [(t, g) for t in range(T) for g in range(NH // HG)]
    U = len(units)
    with Scope(nc, f"s{n}") as ctx:
        body = Body(pg, ctx, 5, 4, f"s{n}")
        acc = body.acc
        sb = lambda s, dims: ctx.enter_context(nc.sbuf_tensor(f"s{n}_{s}", [P, *dims], F32))
        sig = lambda s, per, credit=0: Signal(ctx, nc, s, per, credit)
        raw, qkv = sb("raw", [T, 3, D]), sb("qkv", [T, 3, D])
        products = sb("products", [2, HG, NH, HD])
        scores, top, sums = sb("scores", [T, NH, NH]), sb("top", [T, NH]), sb("sums", [T, NH])
        o, regrouped, oT = sb("o", [T, NH, HD]), sb("regrouped", [T, D]), sb("oT", [KD, S])
        regroup = nc.dram_tensor(f"regroup{n}", [B, NH, S, HD], F32, kind="Internal").ap()
        biased = sig("biased", 1)
        product_ready = sig("product_ready", 2 * U)
        product_used = sig("product_used", 2 * U, 2)
        shifted_ready, exps_ready, probs_ready = sig("shifted_ready", 1), sig("exps_ready", 1), sig("probs_ready", 1)
        written = sig("written", 16 * T)
        read_back = sig("read_back", 16)
        w, wo = pg.w(n, "w", KD, 3 * D), pg.w(n, "wo", KD, D)
        y_bank = pg.bank[4]

        def regroup_rows(sp):
            with sp.Fori(0, B) as i:
                sp.wait_ge(product_used.sem, product_used.at(i, 2 * U))
                for t in range(T):
                    sp.dma_start(regroup[i, :, t * P:(t + 1) * P, :].rearrange("h p d -> p h d"), o[:, t, :, :])\
                        .then_inc(written.sem, 16)
                sp.wait_ge(written.sem, written.at(i, 16 * T))
                sp.dma_start(regrouped[:], regroup[i].rearrange("h (r c) d -> (h r) (c d)", c=NH)
                             .rearrange("(t p) d -> p t d", p=P)).then_inc(read_back.sem, 16)
        with nc.Block() as block:
            prefetch(pg, block, n, regroup_rows)

            @block.gpsimd
            def _(pool):
                start(pg, pool, n)
                with pool.Fori(0, B) as i:
                    body.stage(pool, i)
                    acc.wait_emptied(pool, i, 3)
                    nc.gpsimd.tensor_tensor(qkv[:].rearrange("p t a d -> p t (a d)"), raw[:].rearrange("p t a d -> p t (a d)"),
                                            over(pg.w(n, "b"), 1, T), ALU.add).then_inc(biased.sem, 1)
                    pool.wait_ge(biased.sem, biased.at(i, 1))
                    head = lambda t, a: shaped(qkv[:, t, a, :], (NH, HD))
                    for k in range(2 * U):
                        t, g = units[k % U]
                        mine = slice(g * HG, (g + 1) * HG)
                        if k < U:
                            in0, in1 = over(head(t, 0)[:, mine, :], 2, NH), over(head(t, 1), 1, HG)
                        else:
                            if k == U:
                                pool.wait_ge(probs_ready.sem, probs_ready.at(i, 1))
                            in0 = over(scores[:, t, mine, :], 2, HD)
                            in1 = over(head(t, 2).rearrange("p g d -> p d g"), 1, HG)
                        pool.wait_ge(product_used.sem, product_used.at(i, k + 1 - 2))
                        nc.gpsimd.tensor_tensor(products[:, k % 2, :, :, :], in0, in1, ALU.mult)\
                            .then_inc(product_ready.sem, 1)
                    body.roots(pool, i)

            @block.tensor
            def _(pe):
                start(pg, pe, n)
                with pe.Fori(0, B) as i:
                    body.transpose_x(pe, i)
                    acc.wait_emptied(pe, i, 0)
                    acc.wait_empty(pe, i, 1)
                    project_tokens(nc, acc.bank(1)[:], w[:, :, 0:2 * D], body.xT, 0).then_inc(acc.full.sem, 1)
                    acc.wait_empty(pe, i, 2)
                    for t in range(T):
                        last = project_tokens(nc, acc.bank(2)[:, t * D:(t + 1) * D], w[:, :, 2 * D:3 * D], body.xT, t)
                    last.then_inc(acc.full.sem, 1)
                    acc.wait_empty(pe, i, 3)
                    project_tokens(nc, acc.bank(3)[:], w[:, :, 0:2 * D], body.xT, 1).then_inc(acc.full.sem, 1)
                    pe.wait_ge(read_back.sem, read_back.at(i, 16))
                    acc.wait_empty(pe, i, 4)
                    transpose_tokens(nc, pe, acc.bank(4), regrouped, pg.c("ident")).then_inc(acc.full.sem, 1)
                    acc.wait_emptied(pe, i, 4)
                    body.project_out(pe, i, oT, wo, y_bank, KD)

            @block.scalar
            def _(act):
                start(pg, act, n)
                acc.empty.give(act)
                with act.Fori(0, B) as i:
                    body.take_xT(act, i)
                    for k, dst in ((1, raw[:, 0, 0:2, :]), (2, raw[:, :, 2, :]), (3, raw[:, 1, 0:2, :])):
                        acc.wait_full(act, i, k)
                        nc.scalar.activation(dst, shaped(acc.bank(k)[:], (2, D)), ACT.Copy).then_inc(acc.empty.sem, 1)
                    act.wait_ge(shifted_ready.sem, shifted_ready.at(i, 1))
                    nc.scalar.activation(scores[:], scores[:], ACT.Exp, scale=1.0 / 16).then_inc(exps_ready.sem, 1)
                    acc.wait_full(act, i, 4)
                    nc.scalar.activation(oT[:], shaped(acc.bank(4)[:], (KD, S)), ACT.Copy).then_inc(acc.empty.sem, 1)

            @block.vector
            def _(dve):
                start(pg, dve, n)
                body.out_taken.give(dve)
                product_used.give(dve)
                rows = lambda ap: ap.rearrange("p t h g -> p (t h) g")
                with dve.Fori(0, B) as i:
                    chain = Chain(body.vchain, dve, i)
                    for k in range(2 * U):
                        t, g = units[k % U]
                        if k == U:
                            dve.wait_ge(product_used.sem, product_used.at(i, U))
                            chain.step(nc.vector.tensor_reduce(flat(top[:]), rows(scores[:]), AX, ALU.max))
                            nc.vector.tensor_tensor(rows(scores[:]), rows(scores[:]), over(flat(top[:]), 2, NH), ALU.subtract)\
                                .then_inc(shifted_ready.sem, 1)
                            dve.wait_ge(exps_ready.sem, exps_ready.at(i, 1))
                            chain.step(nc.vector.tensor_reduce(flat(sums[:]), rows(scores[:]), AX, ALU.add))
                            chain.step(nc.vector.reciprocal(sums[:], sums[:]))
                            nc.vector.tensor_tensor(rows(scores[:]), rows(scores[:]), over(flat(sums[:]), 2, NH), ALU.mult)\
                                .then_inc(probs_ready.sem, 1)
                        dst = (scores if k < U else o)[:, t, g * HG:(g + 1) * HG, :]
                        dve.wait_ge(product_ready.sem, product_ready.at(i, k + 1))
                        nc.vector.tensor_reduce(dst, products[:, k % 2, :, :, :], AX, ALU.add).then_inc(product_used.sem, 1)
                    body.add_norm(dve, i, chain, y_bank, bias=pg.w(n, "bo"))
                    chain.done()


def latent_attention(pg, n, rotate_queries):
    nc = pg.nc
    CQ, DC, PAIRS = 96, 64, NH // 2
    with Scope(nc, f"s{n}") as ctx:
        units = [{"t": t, "g": g, "heads": 8, "keys": NK, "masks": []} for t in range(T) for g in range(2)]
        U = len(units)
        fills = 1 + 4
        body = Body(pg, ctx, fills, attention_steps(units, True), f"s{n}",
                    elsewhere=range(1, 5) if rotate_queries else ())
        att = Attention(pg, ctx, f"s{n}", units, True, pg.bank[2:4])
        acc = body.acc
        sb = lambda s, dims, p=P: ctx.enter_context(nc.sbuf_tensor(f"s{n}_{s}", [p, *dims], F32))
        sig = lambda s, per, credit=0: Signal(ctx, nc, s, per, credit)
        wq, kckv = pg.w(n, "wq", NH, D), pg.w(n, "kckv", NH, DC)
        qr, kr, wo = pg.w(n, "qr", NH, 2 * CQ, rows=DC), pg.w(n, "kr", NH, DC, rows=DC), pg.w(n, "wo", NH, D)
        QR = pg.spare(n, 0, NH, 2, DC, rows=CQ)
        OUT = pg.spare(n, 2048, PAIRS, D)
        if rotate_queries:
            kcq = pg.w(n, "kcq", NH, 2 * CQ)
            BIG = pg.over_weights(n, "kckv", 0, NH, KD, 2 * CQ)
            qcos, qsin = pg.w(n, "qcos", 2, S, rows=CQ), pg.w(n, "qsin", 2, S, rows=CQ)
        else:
            kcq = pg.w(n, "kcq", 2, NH, P, rows=CQ)
            MID = pg.over_weights(n, "kckv", 0, NH, DC)
            Q = pg.over_weights(n, "kckv", NH * DC, KD, NH, DC)
        kv, swapped = sb("kv", [B, DC]), sb("swapped", [B, DC])
        vblk, kblk = sb("vblk", [B, P]), sb("kblk", [B, P])
        v = sb("v", [P])
        qT, oT = sb("qT", [PAIRS, S]), sb("oT", [PAIRS, S])
        v_bank = [pg.bank[7], pg.bank[4]]
        y_bank = pg.bank[4]
        kv_steps = sig("kv_steps", 0)
        kv_spread = sig("kv_spread", 1)
        fold_full, fold_empty = sig("fold_full", 0), sig("fold_empty", 0)
        v_staged = sig("v_staged", 1)
        o_taken = sig("o_taken", U, 2)
        ring = [pg.bank[2], pg.bank[3], pg.bank[5], pg.bank[6]]

        folds, stage_starts = [], []

        def qr_fold(q):
            def mm(bank):
                for h in range(4 * q, 4 * q + 4):
                    for half in range(2):
                        at = ((h % 4) * 2 + half) * DC
                        last = nc.tensor.matmul(bank[0:CQ, at:at + DC], qr[:, h, half * CQ:(half + 1) * CQ], kr[:, h, :],
                                                start=True, stop=True)
                return last
            return mm, flat(QR[:, 4 * q:4 * q + 4, :, :]), slice(0, CQ), 512

        def out_fold(q):
            def mm(bank):
                for pair in (2 * q, 2 * q + 1):
                    for j in range(2):
                        last = nc.tensor.matmul(bank[j * DC:(j + 1) * DC, (pair % 2) * D:(pair % 2 + 1) * D],
                                                kckv[:, 2 * pair + j, :], wo[:, 2 * pair + j, :], start=True, stop=True)
                return last
            return mm, flat(OUT[:, 2 * q:2 * q + 2, :]), slice(0, P), 512

        def big_fold(h):
            def mm(bank):
                for m in range(KD):
                    last = nc.tensor.matmul(bank[:, m * 2 * CQ:(m + 1) * 2 * CQ], wq[:, h, m * P:(m + 1) * P], kcq[:, h, :],
                                            start=True, stop=True)
                return last
            return mm, flat(BIG[:, h, :, :]), slice(0, P), KD * 2 * CQ

        def mid_fold(q):
            def mm(bank):
                for h in range(8 * q, 8 * q + 8):
                    for half in range(2):
                        last = nc.tensor.matmul(bank[:, (h % 8) * DC:(h % 8 + 1) * DC], kcq[:, half, h, :], QR[:, h, half, :],
                                                start=(half == 0), stop=(half == 1))
                return last
            return mm, flat(MID[:, 8 * q:8 * q + 8, :]), slice(0, P), 512

        def q_fold(q):
            m, quarter = q // 2, q % 2
            def mm(bank):
                for h in range(8 * quarter, 8 * quarter + 8):
                    last = nc.tensor.matmul(bank[:, (h % 8) * DC:(h % 8 + 1) * DC], wq[:, h, m * P:(m + 1) * P], MID[:, h, :],
                                            start=True, stop=True)
                return last
            return mm, flat(Q[:, m, 8 * quarter:8 * quarter + 8, :]), slice(0, P), 512

        stages = [[qr_fold(q) for q in range(4)] + [out_fold(q) for q in range(4)]]
        stages += [[big_fold(h) for h in range(NH)]] if rotate_queries else \
            [[mid_fold(q) for q in range(2)], [q_fold(q) for q in range(4)]]

        if rotate_queries:
            big_full = sig("big_full", NH)
            products_ready = sig("products_ready", NH, len(ring))
            rotated_ready = sig("rotated_ready", NH, 2)
            rotated_used = sig("rotated_used", NH, 3)
            rotated, crossed = sb("rotated", [3, 2, S], CQ), sb("crossed", [2, 2, S], CQ)
        with nc.Block() as block:
            prefetch(pg, block, n)

            @block.gpsimd
            def _(pool):
                start(pg, pool, n)
                if rotate_queries:
                    rotated_ready.give(pool)
                pool.wait_ge(kv_spread.sem, 1)

                def rotate(i):
                    for h in range(NH):
                        pool.wait_ge(products_ready.sem, products_ready.at(i, h + 1))
                        nc.gpsimd.tensor_tensor(rotated[:, h % 3, :, :], rotated[:, h % 3, :, :], crossed[:, h % 2, :, :],
                                                ALU.add).then_inc(rotated_ready.sem, 1)

                def head(i):
                    body.stage_first(pool)
                    if rotate_queries:
                        rotate(i)

                def tail(i, more):
                    if more:
                        body.stage_next(pool, i)
                    pool.wait_ge(att.valued.sem, att.valued.at(i, 0))
                    nc.gpsimd.tensor_copy(v[:], vblk[:, i, :]).then_inc(v_staged.sem, 1)
                    att.gpsimd(pool, i)
                    if more and rotate_queries:
                        rotate(i + 1)
                    body.roots(pool, i)
                batches(pool, head, tail)

            @block.tensor
            def _(pe):
                start(pg, pe, n)
                k = 0
                for stage in stages:
                    if k:
                        pe.wait_ge(fold_empty.sem, k)
                    for mm, _, _, _ in stage:
                        if k >= len(ring):
                            pe.wait_ge(fold_empty.sem, k + 1 - len(ring))
                        mm(ring[k % len(ring)]).then_inc(fold_full.sem, 1)
                        k += 1
                pe.wait_ge(fold_empty.sem, k)
                pe.wait_ge(kv_spread.sem, 1)
                for b in range(B):
                    last = nc.tensor.transpose(ring[0][:, b * P:(b + 1) * P], vblk[:, b, :], pg.c("ident"))
                last.then_inc(fold_full.sem, 1)
                pe.wait_ge(fold_empty.sem, k + 1)
                att.credits_tensor(pe)
                if rotate_queries:
                    rotated_used.give(pe)

                def x(i):
                    body.transpose_x(pe, i)
                    acc.wait_emptied(pe, i, 0)

                def rotated_queries(i, s):
                    if s < NH:
                        pe.wait_ge(products_ready.sem, products_ready.at(i, s + 1 - len(ring)))
                        for half in range(2):
                            for m in range(KD):
                                last = nc.tensor.matmul(ring[s % 4][0:CQ, half * S:(half + 1) * S],
                                                        BIG[:, s, m, half * CQ:(half + 1) * CQ], body.xT[:, m, :],
                                                        start=(m == 0), stop=(m == KD - 1))
                        last.then_inc(big_full.sem, 1)
                    h = s - 2
                    if h >= 0:
                        fill, at = 1 + h // 4, (h // 2 % 2) * S
                        if h % 4 == 0:
                            acc.wait_empty(pe, i, fill)
                        pe.wait_ge(rotated_ready.sem, rotated_ready.at(i, h + 1))
                        out = acc.bank(fill)[(h % 2) * DC:(h % 2 + 1) * DC, at:at + S]
                        for half in range(2):
                            last = nc.tensor.matmul(out, QR[:, h, half, :], rotated[:, h % 3, half, :],
                                                    start=(half == 0), stop=(half == 1))
                        last.then_inc(rotated_used.sem, 1)

                def queries(i, f):
                    acc.wait_empty(pe, i, 1 + f)
                    for pair in (2 * f, 2 * f + 1):
                        for m in range(KD):
                            last = nc.tensor.matmul(acc.bank(1 + f)[:, (pair % 2) * S:(pair % 2 + 1) * S],
                                                    flat(Q[:, m, 2 * pair:2 * pair + 2, :]), body.xT[:, m, :],
                                                    start=(m == 0), stop=(m == KD - 1))
                    last.then_inc(acc.full.sem, 1)

                def projections(i):
                    if rotate_queries:
                        return [lambda: x(i)]
                    return [lambda: x(i)] + [lambda f=f: queries(i, f) for f in range(4)]

                def rotation(i):
                    if rotate_queries:
                        for s in range(NH + 2):
                            rotated_queries(i, s)

                def head(i):
                    for piece in projections(i):
                        piece()
                    rotation(i)

                def score(i, u, bank):
                    for c in range(4):
                        last = nc.tensor.matmul(bank[:, c * P:(c + 1) * P], qT[:, 4 * u["g"] + c, u["t"] * P:(u["t"] + 1) * P],
                                                kblk[:, i, :], start=True, stop=True)
                    return last

                def value(i, s, probsT):
                    pe.wait_ge(o_taken.sem, o_taken.at(i, s + 1 - 2))
                    return nc.tensor.matmul(v_bank[s % 2][:], v[:], probsT, start=True, stop=True)

                def before_values(i):
                    pe.wait_ge(v_staged.sem, v_staged.at(i, 1))
                    pe.wait_ge(body.out_taken.sem, body.out_taken.at(i, 0))

                def tail(i, more):
                    acc.wait_emptied(pe, i, 4)
                    att.tensor(pe, i, lambda k, u, part, bank: score(i, u, bank), lambda s, u, probsT: value(i, s, probsT),
                               before_values=lambda: before_values(i), pieces=projections(i + 1) if more else ())
                    pe.wait_ge(o_taken.sem, o_taken.at(i, U))
                    body.project_out(pe, i, oT, OUT, y_bank, PAIRS)
                    if more:
                        rotation(i + 1)
                batches(pe, head, tail)

            @block.scalar
            def _(act):
                start(pg, act, n)
                acc.empty.give(act)
                att.credits_scalar(act)
                o_taken.give(act)

                def queries(i, f):
                    if rotate_queries:
                        act.wait_ge(rotated_used.sem, rotated_used.at(i, 4 * f + 4))
                    else:
                        acc.wait_full(act, i, 1 + f)
                    nc.scalar.activation(qT[:, 2 * f:2 * f + 2, :], shaped(acc.bank(1 + f)[:], (2, S)), ACT.Copy)\
                        .then_inc(acc.empty.sem, 1)

                def takes(i):
                    return [lambda: body.take_xT(act, i)] + [lambda f=f: queries(i, f) for f in range(0 if rotate_queries else 4)]

                def rotation(i):
                    if rotate_queries:
                        for f in range(4):
                            queries(i, f)

                def head(i):
                    for take in takes(i):
                        take()
                    rotation(i)

                def take_output(i, s):
                    u = units[s]
                    act.wait_ge(att.valued.sem, att.valued.at(i, s + 1))
                    nc.scalar.activation(oT[:, 4 * u["g"]:4 * u["g"] + 4, u["t"] * P:(u["t"] + 1) * P],
                                         shaped(v_bank[s % 2][:], (4, P)), ACT.Copy).then_inc(o_taken.sem, 1)

                def tail(i, more):
                    att.scalar(act, i, takes(i + 1) if more else (), after_turn=lambda s: take_output(i, s))
                    if more:
                        rotation(i + 1)
                batches(act, head, tail)

            @block.vector
            def _(dve):
                start(pg, dve, n)
                body.out_taken.give(dve)
                if rotate_queries:
                    products_ready.give(dve)
                cos, sin = over(pg.c("kcos"), 1, B), over(pg.c("ksin"), 1, B)
                h = DC // 2
                nc.vector.tensor_tensor(swapped[:, :, 0:h], pg.ctx2[:, :, h:DC], sin[:, :, 0:h], ALU.mult)
                nc.vector.tensor_tensor(swapped[:, :, h:DC], pg.ctx2[:, :, 0:h], sin[:, :, h:DC], ALU.mult)
                nc.vector.tensor_tensor(kv[:], pg.ctx2[:], cos, ALU.mult)
                nc.vector.memset(vblk[:], 0.0).then_inc(kv_steps.sem, 1)
                dve.wait_ge(kv_steps.sem, 1)
                nc.vector.tensor_tensor(kv[:], kv[:], swapped[:], ALU.add).then_inc(kv_steps.sem, 1)
                dve.wait_ge(kv_steps.sem, 2)
                nc.vector.tensor_copy(vblk[0:NK, :, 0:DC], kv[0:NK, :, :])
                nc.vector.tensor_copy(vblk[NK:P, :, DC:P], kv[NK:P, :, :]).then_inc(kv_spread.sem, 1)
                k = 0
                for stage in stages:
                    for _, dst, rows, size in stage:
                        dve.wait_ge(fold_full.sem, k + 1)
                        nc.vector.tensor_copy(dst, ring[k % len(ring)][rows, 0:size]).then_inc(fold_empty.sem, 1)
                        k += 1
                dve.wait_ge(fold_full.sem, k + 1)
                nc.vector.tensor_copy(kblk[:], shaped(ring[0][:], (B, P))).then_inc(fold_empty.sem, 1)

                def rotation(i):
                    for h in range(NH if rotate_queries else 0):
                        src = shaped(ring[h % 4][0:CQ, :], (2, S))
                        dve.wait_ge(big_full.sem, big_full.at(i, h + 1))
                        dve.wait_ge(rotated_ready.sem, rotated_ready.at(i, h + 1 - 2))
                        dve.wait_ge(rotated_used.sem, rotated_used.at(i, h + 1 - 3))
                        nc.vector.tensor_tensor(rotated[:, h % 3, :, :], src, qcos, ALU.mult)
                        for half in range(2):
                            last = nc.vector.tensor_tensor(crossed[:, h % 2, half, :], src[:, 1 - half, :],
                                                           qsin[:, half, :], ALU.mult)
                        last.then_inc(products_ready.sem, 1)

                def tail(i, more):
                    chain = Chain(body.vchain, dve, i)
                    att.vector(dve, i, chain)
                    if more:
                        rotation(i + 1)
                    body.add_norm(dve, i, chain, y_bank)
                    chain.done()
                batches(dve, rotation, tail)


def small_xattn(pg, n):
    nc = pg.nc
    with Scope(nc, f"s{n}") as ctx:
        units = [{"t": t, "g": g, "heads": 8, "keys": NK, "masks": [(0, NK, pg.c("causal")[:, 0:NK])] if t == 0 else []}
                 for t in range(T) for g in range(KD)]
        body = Body(pg, ctx, 2, attention_steps(units, True), f"s{n}")
        att = Attention(pg, ctx, f"s{n}", units, True, pg.bank[2:5])
        acc = body.acc
        sb = lambda s, dims: ctx.enter_context(nc.sbuf_tensor(f"s{n}_{s}", [P, *dims], F32))
        qT, oT = sb("qT", [KD, S]), sb("oT", [KD, S])
        kblk, vblk = sb("kblk", [B, KD, 8, NK]), sb("vblk", [B, 8, 2, HD])
        v = sb("v", [8, 2, HD])
        kv_ready = Signal(ctx, nc, "kv_ready", 1)
        kv_spread = Signal(ctx, nc, "kv_spread", 1)
        v_staged = Signal(ctx, nc, "v_staged", 1)
        o_taken = Signal(ctx, nc, "o_taken", 1, credit=1)
        ctxT = pg.ctxT
        wq, wo = pg.w(n, "wq", KD, D), pg.w(n, "wo", KD, D)
        wk, wv = pg.w(n, "wk", rows=NK), pg.w(n, "wv", rows=NK)
        o_bank, y_bank = pg.bank[7], pg.bank[4]
        with nc.Block() as block:
            prefetch(pg, block, n)

            @block.gpsimd
            def _(pool):
                start(pg, pool, n)
                pool.wait_ge(kv_spread.sem, 1)

                def tail(i, more):
                    if more:
                        body.stage_next(pool, i)
                    pool.wait_ge(att.valued.sem, att.valued.at(i, 0))
                    nc.gpsimd.tensor_copy(v[:], vblk[:, i, :, :, :]).then_inc(v_staged.sem, 1)
                    att.gpsimd(pool, i)
                    body.roots(pool, i)
                batches(pool, lambda i: body.stage_first(pool), tail)

            @block.tensor
            def _(pe):
                start(pg, pe, n)
                for m in range(KD):
                    nc.tensor.matmul(pg.bank[2][:, m * S:(m + 1) * S], wk[:, m * P:(m + 1) * P], ctxT[:, :, 0:NK],
                                     start=True, stop=True)
                for b in range(B):
                    last = nc.tensor.matmul(pg.bank[5 + b // 2][:, (b % 2) * D:(b % 2 + 1) * D], ctxT[:, b, :], wv,
                                            start=True, stop=True)
                last.then_inc(kv_ready.sem, 1)
                att.credits_tensor(pe)
                pe.wait_ge(kv_spread.sem, 1)

                def projections(i):
                    def x():
                        body.transpose_x(pe, i)
                        acc.wait_emptied(pe, i, 0)

                    def queries():
                        acc.wait_empty(pe, i, 1)
                        project_features(nc, acc.bank(1), wq, body.xT).then_inc(acc.full.sem, 1)
                    return [x, queries]

                def head(i):
                    for piece in projections(i):
                        piece()

                def score(i, u, bank):
                    return nc.tensor.matmul(bank[:], qT[:, u["g"], u["t"] * P:(u["t"] + 1) * P],
                                            kblk[:, i, u["g"], :, :], start=True, stop=True)

                def value(u, probsT):
                    for c in range(4):
                        at = u["g"] * S + u["t"] * P
                        last = nc.tensor.matmul(o_bank[c * 32:(c + 1) * 32, at:at + P], v[:, 4 * u["g"] + c, :, :],
                                                probsT[:, c * P:(c + 1) * P], start=True, stop=True)
                    return last

                def before_values(i):
                    pe.wait_ge(o_taken.sem, o_taken.at(i, 0))
                    pe.wait_ge(v_staged.sem, v_staged.at(i, 1))

                def tail(i, more):
                    acc.wait_emptied(pe, i, 1)
                    att.tensor(pe, i, lambda k, u, part, bank: score(i, u, bank), lambda s, u, probsT: value(u, probsT),
                               before_last_bank=lambda: pe.wait_ge(body.out_taken.sem, body.out_taken.at(i, 0)),
                               before_values=lambda: before_values(i), pieces=projections(i + 1) if more else ())
                    pe.wait_ge(o_taken.sem, o_taken.at(i, 1))
                    body.project_out(pe, i, oT, wo, y_bank, KD)
                batches(pe, head, tail)

            @block.scalar
            def _(act):
                start(pg, act, n)
                acc.empty.give(act)
                att.credits_scalar(act)
                o_taken.give(act)

                def takes(i):
                    def queries():
                        acc.wait_full(act, i, 1)
                        nc.scalar.activation(qT[:], shaped(acc.bank(1)[:], (KD, S)), ACT.Copy, scale=0.25)\
                            .then_inc(acc.empty.sem, 1)
                    return [lambda: body.take_xT(act, i), queries]

                def head(i):
                    for take in takes(i):
                        take()

                def tail(i, more):
                    att.scalar(act, i, takes(i + 1) if more else ())
                    act.wait_ge(att.valued.sem, att.valued.at(i, len(units)))
                    nc.scalar.activation(oT[:], shaped(o_bank[:], (KD, S)), ACT.Copy).then_inc(o_taken.sem, 1)
                batches(act, head, tail)

            @block.vector
            def _(dve):
                start(pg, dve, n)
                body.out_taken.give(dve)
                dve.wait_ge(kv_ready.sem, 1)
                for b in range(B):
                    for m in range(KD):
                        nc.vector.tensor_tensor(kblk[:, b, m, :, :],
                                                over(pg.bank[2][:, m * S + b * NK:m * S + (b + 1) * NK], 1, 8),
                                                over(pg.c("mask8"), 2, NK), ALU.mult)
                    last = nc.vector.tensor_tensor(vblk[:, b, :, :, :],
                                                   shaped(pg.bank[5 + b // 2][:, (b % 2) * D:(b % 2 + 1) * D], (8, 2, HD)),
                                                   over(over(pg.c("half2"), 1, 8), 3, HD), ALU.mult)
                last.then_inc(kv_spread.sem, 1)

                def tail(i, more):
                    chain = Chain(body.vchain, dve, i)
                    att.vector(dve, i, chain)
                    body.add_norm(dve, i, chain, y_bank)
                    chain.done()
                batches(dve, lambda i: None, tail)


def prefetch(pg, block, n, more=None):
    order, at = pg.order, pg.order.index(n)

    def load(sp, m):
        sp.dma_start(pg.arena[m % 2][:, 0:pg.where[m]["size"]], pg.dram[m]).then_inc(pg.loaded[m], 16)
        if m in pg.where["overflow"]:
            sp.dma_start(pg.overflow(m), pg.dram[f"overflow{m}"]).then_inc(pg.loaded[m], 16)

    @block.sync
    def _(sp):
        if at == 0:
            for b in range(2):
                sp.dma_start(pg.x[:, 2 * b:2 * b + 2, :, :],
                             pg.dram["x"][2 * b:2 * b + 2].rearrange("b (t p) d -> p b t d", p=P))\
                    .then_inc(pg.inputs_loaded, 16)
            load(sp, n)
            for half in range(2):
                cols = slice(half * NK, (half + 1) * NK)
                sp.dma_start(pg.ctxT[:, :, cols], pg.dram["ctxT"]).then_inc(pg.inputs_loaded, 16)
            sp.dma_start(pg.ctx2[:], pg.dram["ctx2"]).then_inc(pg.inputs_loaded, 16)
            sp.dma_start(pg.const[:], pg.dram["const"]).then_inc(pg.inputs_loaded, 16)
        if at + 1 < len(order):
            load(sp, order[at + 1])
        if more:
            more(sp)


BUILDERS = {1: small_xattn, 4: small_xattn, 0: head_attention, 7: lambda pg, n: latent_attention(pg, n, False),
            10: lambda pg, n: latent_attention(pg, n, True), 6: differential_attention, 3: decay_attention,
            8: modulated_ffn, 9: windowed_attention,
            2: lambda pg, n: weighted_experts(pg, n, 8, 2, True, 17), 5: top1_experts,
            11: lambda pg, n: weighted_experts(pg, n, 8, 2, False, 11)}


def decoder(nc, where, dram, out):
    with ExitStack() as ctx:
        pg = Program(nc, ctx, where, dram)
        for n in pg.order:
            BUILDERS[n](pg, n)
        with nc.Block() as block:
            @block.sync
            def _(sp):
                sp.dma_start(out.rearrange("b (t p) d -> p b t d", p=P), pg.x[:]).then_inc(pg.stored, 16)
                sp.wait_ge(pg.stored, 16)


def kernel(**inputs):
    import concourse.bacc as bacc
    from concourse.bass_utils import run_bass_kernel_spmd

    w = {k: np.asarray(v) for k, v in inputs.items()}
    consts, L, overflow = layouts(w)
    ctx = w["ctx_512"]
    arrays = {"x": w["x"], "ctxT": np.ascontiguousarray(ctx.transpose(2, 0, 1)),
              "ctx2": np.ascontiguousarray(np.concatenate([ctx.transpose(1, 0, 2)] * 2))}
    where = {"order": SUBLAYERS, "arena": [8, 8]}
    arrays["const"], where["const"] = pack(consts)
    where["const"]["size"] = arrays["const"].shape[1]
    for n in SUBLAYERS:
        arrays[n], where[n] = pack(L[n])
        where[n]["size"] = arrays[n].shape[1]
    for n in SUBLAYERS:
        where["arena"][n % 2] = max(where["arena"][n % 2], where[n]["size"])
        if n in SPARE:
            assert n + 1 not in where or where[n + 1]["size"] <= SPARE_AT[n]
            where["arena"][1 - n % 2] = max(where["arena"][1 - n % 2], SPARE_AT[n] + SPARE[n])
    where["overflow"] = {}
    for n, a in overflow.items():
        if n in SUBLAYERS:
            at = max(where[m]["size"] for m in (n - 1, n + 1) if m in where) if len(SUBLAYERS) > 1 else 0
            arrays[f"overflow{n}"], where["overflow"][n] = np.ascontiguousarray(a), (at, a.shape[1])
            where["arena"][1 - n % 2] = max(where["arena"][1 - n % 2], at + a.shape[1])
    nc = bacc.Bacc("TRN2", target_bir_lowering=False, num_devices=1)
    dram, given = {}, {}
    for name, a in arrays.items():
        label = f"in_{name}_dram" if isinstance(name, str) else f"in_weights_{name}_dram"
        given[label] = a
        dram[name] = nc.dram_tensor(label, a.shape, mybir.dt.from_np(a.dtype), kind="ExternalInput").ap()
    out = nc.dram_tensor("out_0_dram", (B, S, D), F32, kind="ExternalOutput").ap()
    decoder(nc, where, dram, out)
    r = run_bass_kernel_spmd(nc, [given], core_ids=[0])
    return r.results[0]["out_0_dram"]
```

```python
from contextlib import ExitStack

import numpy as np

import concourse.bass as bass
from concourse import mybir

F32 = mybir.dt.float32
ALU = mybir.AluOpType
ACT = mybir.ActivationFunctionType
AX = mybir.AxisListType.X

P = 128
B, S, D = 4, 256, 256
T = S // P
KD = D // P
NH, HD = 16, 16
NK = 64
LN_EPS, RMS_EPS = 1e-5, 1e-6
NEG = -1e30
HID = 176


class Scope(ExitStack):

    def __init__(self, nc, name):
        super().__init__()
        self.nc, self.name, self.sems = nc, name, []

    def semaphore(self, name):
        self.sems.append(self.nc.alloc_semaphore(f"{self.name}_{name}"))
        return self.sems[-1]

    def __exit__(self, *failure):
        if failure[0] is None:
            self.nc.clear_and_free_semaphores(self.sems)
            self.nc.all_engine_barrier()
        return super().__exit__(*failure)


class Signal:

    def __init__(self, ctx, nc, name, per, credit=0):
        self.sem = ctx.semaphore(name)
        self.name, self.per, self.credit = name, per, credit

    def at(self, i, k):
        return i * self.per + (k + self.credit)

    def give(self, eng):
        eng.sem_inc(self.sem, self.credit)


class Accumulators:

    def __init__(self, ctx, nc, banks, fills, elsewhere=()):
        self.banks, self.fills, self.elsewhere = banks, fills, elsewhere
        self.full = Signal(ctx, nc, "acc_full", fills - len(elsewhere))
        self.empty = Signal(ctx, nc, "acc_empty", fills, credit=len(banks))

    def bank(self, k):
        return self.banks[k % len(self.banks)]

    def wait_empty(self, pe, i, k):
        pe.wait_ge(self.empty.sem, self.empty.at(i, k + 1 - len(self.banks)))

    def wait_full(self, act, i, k):
        before = sum(1 for f in self.elsewhere if f < k)
        act.wait_ge(self.full.sem, self.full.at(i, k + 1 - before))

    def wait_emptied(self, eng, i, k):
        eng.wait_ge(self.empty.sem, self.empty.at(i, k + 1))


class Root:

    def __init__(self, pg, ctx, name, width):
        self.pg, self.width = pg, width
        self.t = ctx.enter_context(pg.nc.sbuf_tensor(f"{name}_t", [P, width], F32))
        self.wanted = Signal(ctx, pg.nc, f"{name}_wanted", 1)
        self.ready = Signal(ctx, pg.nc, f"{name}_ready", 1)

    def power(self, pool, i):
        pool.wait_ge(self.wanted.sem, self.wanted.at(i, 1))
        self.pg.nc.gpsimd.tensor_tensor(self.t[:], self.t[:], self.pg.c("minus_half")[:, 0:self.width], ALU.pow)\
            .then_inc(self.ready.sem, 1)

    def wait(self, eng, i):
        eng.wait_ge(self.ready.sem, self.ready.at(i, 1))


class Chain:

    def __init__(self, counter, eng, i):
        self.counter, self.eng, self.i, self.k = counter, eng, i, 0

    def step(self, instruction):
        self.k += 1
        instruction.then_inc(self.counter.sem, 1)
        self.eng.wait_ge(self.counter.sem, self.counter.at(self.i, self.k))

    def done(self):
        assert self.k == self.counter.per, (self.counter.name, self.k, self.counter.per)



def ptile(a):
    k = a.shape[0] // P
    return a.reshape(k, P, -1).transpose(1, 0, 2).reshape(P, -1)


def rolled(a, yes):
    return np.roll(a.reshape(-1, KD, P), 32, axis=2).reshape(a.shape) if yes else a


def pack(pieces):
    at, where, cols = 0, {}, []
    for name, a in pieces:
        a = a.reshape(a.shape[0], -1)
        if a.shape[0] < P:
            a = np.concatenate([a, np.zeros((P - a.shape[0], a.shape[1]), np.float32)])
        where[name] = (at, a.shape[1])
        at += a.shape[1]
        cols.append(a)
    return np.ascontiguousarray(np.concatenate(cols, axis=1)), where


def hidden_tiles(w, width):
    w = np.concatenate([w, np.zeros((D, width - w.shape[1]), np.float32)], axis=1)
    return w.reshape(KD, P, width // P, P).transpose(1, 2, 0, 3)


def xattn_small(wq, wkv, wo):
    wkT, wvT = wkv[:D].T, wkv[D:].T
    return [("wq", ptile(wq.T)), ("wo", ptile(wo.T)), ("wk", wkT), ("wv", wvT)]


def xattn_latent(wq, w_kc_q, w_kc_kv, w_qr, w_kr, wo, rope_q):
    q = w_kc_q.transpose(1, 0, 2) if rope_q else w_kc_q.transpose(2, 0, 1).reshape(2, 96, 16, P).transpose(1, 0, 2, 3)
    return [("wq", wq.reshape(NH, P, D).transpose(1, 0, 2)),
            ("kcq", q),
            ("kckv", w_kc_kv.transpose(1, 0, 2)),
            ("qr", w_qr.transpose(2, 0, 1)),
            ("kr", w_kr.transpose(2, 0, 1)),
            ("wo", wo.T.reshape(NH, P, D).transpose(1, 0, 2))]


def moe_weights(gate, g, u, d, width):
    if d is None:
        return [("gate", ptile(gate)), ("g", hidden_tiles(g, width)), ("u", hidden_tiles(u, width))]
    return [("gate", ptile(gate)), ("g", hidden_tiles(g, width)), ("u", hidden_tiles(u, width)),
            ("d", ptile(np.concatenate([d, np.zeros((width - d.shape[0], D), np.float32)])))]


def rope_angles(length, dim):
    inv = (1.0 / np.float32(10000.0) ** (np.arange(0, dim, 2, dtype=np.float32) / np.float32(dim))).astype(np.float32)
    return np.arange(length, dtype=np.float32)[:, None] * inv[None, :]


def owners(tiles, edges):
    e = np.zeros((len(edges), tiles * P), np.float32)
    lo = 0
    for n, hi in enumerate(edges):
        e[n, lo:hi] = 1.0
        lo = hi
    return e


def constants():
    p = np.arange(P)
    f = np.float32
    ident = np.eye(P, dtype=f)
    mask8 = (p[:, None] // HD == np.arange(8)).astype(f)
    par2 = ((p[:, None] // HD) % 2 == np.arange(2)).astype(f)
    half2 = (p[:, None] // NK == np.arange(2)).astype(f)
    causal = np.where(p[:, None] >= p[None, :], 0.0, NEG).astype(f)
    near = np.where((causal == 0) & (p[:, None] - p[None, :] < 32), 0.0, NEG).astype(f)
    before = np.where(p[:, None] + P - p[None, :] < 32, 0.0, NEG).astype(f)
    dist = np.maximum(np.arange(S)[None, :] - p[:, None], 0).astype(f)
    valid = (np.arange(S)[None, :] >= p[:, None]).astype(f)
    tri = (np.arange(8)[None, :] < np.arange(8)[:, None]).astype(f).reshape(1, 64).repeat(P, 0)
    ang = rope_angles(S, HD)
    cos = np.concatenate([np.cos(ang)] * 2, -1).reshape(T, P, HD).transpose(1, 0, 2)
    sin = np.concatenate([-np.sin(ang), np.sin(ang)], -1).reshape(T, P, HD).transpose(1, 0, 2)
    a = np.repeat(rope_angles(NK, 64), 2, axis=-1)
    kcos = np.cos(a)
    ksin = np.sin(a) * np.where(np.arange(64) < 32, -1.0, 1.0)
    kcos, ksin = (np.concatenate([t, t]).astype(f) for t in (kcos, ksin))
    return [("ident", ident), ("mask8", mask8), ("par2", par2), ("half2", half2), ("causal", causal),
            ("window", np.concatenate([before, near], 1)), ("near", near), ("tri", tri), ("cos", cos.astype(f)), ("sin", sin.astype(f)),
            ("minus_half", np.full((P, 64), -0.5, f)), ("kcos", kcos), ("ksin", ksin)], dist, valid


def layouts(w):
    consts, dist, valid = constants()
    qa = np.repeat(rope_angles(S, 192), 2, axis=-1).T.reshape(2, 96, S).transpose(1, 0, 2)
    sign = np.array([-1.0, 1.0], np.float32)[None, :, None]
    qcos, qsin = np.cos(qa).astype(np.float32), (np.sin(qa) * sign).astype(np.float32)
    L = {}
    rows = lambda v: np.broadcast_to(v.reshape(1, -1), (P, v.size))
    L[0] = [("w", ptile(w["L0_attn_w_qkv"].T)), ("wo", ptile(w["L0_attn_w_out"].T)),
            ("b", rows(w["L0_attn_b_qkv"])), ("bo", rows(w["L0_attn_b_out"])),
            ("first", (np.arange(P)[:, None] == np.zeros((1, P))).astype(np.float32))]
    L[1] = xattn_small(w["L0_xattn_Wq"], w["L0_xattn_Wkv_expand"], w["L0_xattn_Wout"])
    cat = lambda a: np.concatenate(list(a), axis=-1)
    L[2] = moe_weights(np.concatenate([w["L0_ffn_gate_w"].T, w["L0_ffn_shared_gate_w"]], axis=1),
                       np.concatenate([cat(w["L0_ffn_w_gate"]), w["L0_ffn_sw_gate"]], axis=1),
                       np.concatenate([cat(w["L0_ffn_w_up"]), w["L0_ffn_sw_up"]], axis=1),
                       np.concatenate([w["L0_ffn_w_down"].reshape(-1, D), w["L0_ffn_sw_down"]]), 17 * P)
    L[2].append(("owner", owners(17, [HID * (e + 1) for e in range(8)] + [8 * HID + 704])))
    L[3] = [("w", ptile(w["L1_attn_W_qkvu"].T)), ("wo", ptile(w["L1_attn_W_out"].T)),
            ("slope", rows(w["L1_attn_slope_rate"])), ("dist", dist), ("valid", valid),
            ("one", np.ones((P, 1), np.float32))]
    L[4] = xattn_small(w["L1_xattn_Wq"], w["L1_xattn_Wkv_expand"], w["L1_xattn_Wout"])
    L[5] = moe_weights(w["L1_ffn_Wr"], cat(w["L1_ffn_Wg"]), cat(w["L1_ffn_Wu"]),
                       None, 32 * P) + [("br", rows(w["L1_ffn_br"]))]
    L[6] = [(n, ptile(rolled(w[f"L2_attn_{n}_w"].T, n in ("q2", "k2")))) for n in ("q1", "k1", "q2", "k2", "v", "o")] \
        + [("lam", rows(w["L2_attn_lambda_param"]))]
    L[7] = xattn_latent(*[w[f"L2_xattn_{n}"] for n in ("Wq", "w_kc_q", "w_kc_kv", "W_qr", "W_kr", "Wo")], False)
    L[8] = [("q", ptile(w["L2_ffn_Wq"].T)), ("k", ptile(w["L2_ffn_Wk"].T)), ("v", ptile(w["L2_ffn_Wv"].T)),
            ("o", ptile(w["L2_ffn_Wo"].T)), ("A", ptile(w["L2_ffn_A"])), ("B", w["L2_ffn_B"]),
            ("ln1", w["L2_ffn_ln1_w"].reshape(KD, P).T), ("ln2", w["L2_ffn_ln2_w"].reshape(KD, P).T),
            ("g", hidden_tiles(w["L2_ffn_W_in_base"].T, 1024)), ("u", hidden_tiles(w["L2_ffn_W_up_base"].T, 1024)),
            ("d", ptile(w["L2_ffn_W_down"].T))]
    overflow = {5: ptile(w["L1_ffn_Wd"].reshape(-1, D))}
    wk, wv = w["L3_attn_Wkv"][:64], w["L3_attn_Wkv"][64:]
    L[9] = [("w", ptile(np.concatenate([w["L3_attn_Wq"].T, wk.T, wv.T], axis=1))),
            ("wo", ptile(w["L3_attn_Wo"].T)), ("temp", rows(w["L3_attn_qk_temp"]))]
    L[10] = xattn_latent(*[w[f"L3_xattn_{n}"] for n in ("Wq", "w_kc_q", "w_kc_kv", "W_qr", "W_kr", "Wo")], True) \
        + [("qcos", qcos), ("qsin", qsin)]
    rowcat = lambda a: a.reshape(-1, a.shape[-1])
    L[11] = moe_weights(w["L3_ffn_Wg"].T, rowcat(w["L3_ffn_W1"]).T, rowcat(w["L3_ffn_W2"]).T,
                        w["L3_ffn_W3"].transpose(0, 2, 1).reshape(-1, D), 11 * P)
    L[11].append(("owner", owners(11, [HID * (e + 1) for e in range(8)])))
    return consts, L, overflow


SUBLAYERS = list(range(12))
SPARE = {3: NH * (S + P) + NH, 7: 4096, 10: 4096}
SPARE_AT = {3: 1600, 7: 10000, 10: 9900}


class Program:

    INPUT_LOADS = 16 * 6

    def __init__(self, nc, ctx, where, dram):
        self.nc, self.where, self.dram, self.order = nc, where, dram, where["order"]
        self.x = ctx.enter_context(nc.sbuf_tensor("x_all", [P, B, T, D], F32))
        self.const = ctx.enter_context(nc.sbuf_tensor("const", [P, where["const"]["size"]], F32))
        self.arena = [ctx.enter_context(nc.sbuf_tensor(f"weights{n}", [P, where["arena"][n]], F32)) for n in range(2)]
        self.ctxT = ctx.enter_context(nc.sbuf_tensor("ctxT", [NK, B, P], F32))
        self.ctx2 = ctx.enter_context(nc.sbuf_tensor("ctx2", [P, B, NK], F32))
        self.inputs_loaded = ctx.enter_context(nc.semaphore("inputs_loaded"))
        self.loaded = {n: ctx.enter_context(nc.semaphore(f"weights_loaded_{n}")) for n in where["order"]}
        self.stored = ctx.enter_context(nc.semaphore("stored"))
        self.bank = [ctx.enter_context(nc.psum_tensor(f"bank{n}", [P, 512], F32)) for n in range(8)]

    def c(self, name, *dims):
        at, n = self.where["const"][name]
        return shaped(self.const[:, at:at + n], dims)

    def w(self, n, name, *dims, rows=P):
        at, size = self.where[n][name]
        return shaped(self.arena[n % 2][0:rows, at:at + size], dims)

    def overflow(self, n, *dims):
        at, size = self.where["overflow"][n]
        return shaped(self.arena[1 - n % 2][:, at:at + size], dims)

    def over_weights(self, n, name, at, *dims):
        at += self.where[n][name][0]
        size = int(np.prod(dims))
        return shaped(self.arena[n % 2][:, at:at + size], dims)

    def spare(self, n, at, *dims, rows=P):
        at += SPARE_AT[n]
        size = int(np.prod(dims))
        return shaped(self.arena[1 - n % 2][0:rows, at:at + size], dims)


def shaped(ap, dims):
    if len(dims) < 2:
        return ap
    names = "abcdef"[:len(dims)]
    return ap.rearrange(f"p ({' '.join(names)}) -> p {' '.join(names)}", **dict(zip(names[1:], dims[1:])))


def over(ap, axis, n):
    ap = ap.unsqueeze(axis)
    shape = list(ap.shape)
    shape[axis] = n
    return ap.broadcast_to(shape)


def start(pg, eng, n):
    eng.wait_ge(pg.inputs_loaded, pg.INPUT_LOADS)
    eng.wait_ge(pg.loaded[n], 32 if n in pg.where["overflow"] else 16)


class Ending:

    def __init__(self, pg, ctx, name, bias=None):
        nc = self.nc = pg.nc
        self.pg, self.bias = pg, bias
        sb = lambda n, dims: ctx.enter_context(nc.sbuf_tensor(f"{name}_{n}", [P, *dims], F32))
        self.out_ready = Signal(ctx, nc, "out_ready", 1)
        self.out_taken = Signal(ctx, nc, "out_taken", 1, credit=1)
        self.norm_steps = Signal(ctx, nc, "norm_steps", 3 + (bias is not None))
        self.passed = Signal(ctx, nc, "passed", 2)
        self.norm_root = Root(pg, ctx, f"{name}_norm_root", T)
        self.r, self.stats, self.mv = sb("r", [T, D]), sb("stats", [T, 6]), sb("mv", [T, 2])

    def step(self, dve, i, k, instruction):
        instruction.then_inc(self.norm_steps.sem, 1)
        dve.wait_ge(self.norm_steps.sem, self.norm_steps.at(i, k + 1))

    def add(self, dve, i, bank, x_times=1.0, wait_out=True):
        nc = self.nc
        if wait_out:
            dve.wait_ge(self.out_ready.sem, self.out_ready.at(i, 1))
        nc.vector.scalar_tensor_tensor(out=self.r[:], in0=self.pg.x[:, i, :, :], scalar=float(x_times),
                                       in1=shaped(bank[:], (T, D)), op0=ALU.mult, op1=ALU.add)\
            .then_inc(self.out_taken.sem, 1)
        dve.wait_ge(self.out_taken.sem, self.out_taken.at(i, 1))
        if self.bias is not None:
            self.step(dve, i, 0, nc.vector.tensor_tensor(self.r[:], self.r[:], over(self.bias, 1, T), ALU.add))

    def norm_pieces(self, dve, i):
        nc, root, first = self.nc, self.norm_root, self.norm_steps.per - 3

        def statistics():
            for t in range(T):
                last = nc.vector.bn_stats(self.stats[:, t, :], self.r[:, t, :])
            self.step(dve, i, first, last)

        def moments():
            dve.sem_inc(self.passed.sem, 1)
            for t in range(T):
                last = nc.vector.bn_aggr(self.mv[:, t, :], self.stats[:, t, :])
            self.step(dve, i, first + 1, last)
            nc.vector.tensor_scalar(root.t[:], self.mv[:, :, 1], LN_EPS, None, ALU.add).then_inc(root.wanted.sem, 1)

        def result():
            root.wait(dve, i)
            for t in range(T):
                last = nc.vector.tensor_scalar(self.pg.x[:, i, t, :], self.r[:, t, :], self.mv[:, t, 0:1],
                                               root.t[:, t:t + 1], ALU.subtract, ALU.mult)
            self.step(dve, i, first + 2, last)
        return [lambda: (statistics(), moments()), None, None, result]

    def norm(self, dve, i):
        for piece in self.norm_pieces(dve, i):
            if piece:
                piece()

    def add_norm(self, dve, i, bank, **how):
        self.add(dve, i, bank, **how)
        self.norm(dve, i)


class Body(Ending):

    def __init__(self, pg, ctx, fills, vector_steps, name, roots=(), elsewhere=(), bias=None):
        super().__init__(pg, ctx, name, bias)
        nc = pg.nc
        sb = lambda n, dims: ctx.enter_context(nc.sbuf_tensor(f"{name}_{n}", [P, *dims], F32))
        self.acc = Accumulators(ctx, nc, pg.bank[0:2], fills, elsewhere)
        self.x_staged = Signal(ctx, nc, "x_staged", 1)
        self.vchain = Signal(ctx, nc, "vector_chain", vector_steps)
        self.root = [Root(pg, ctx, f"{name}_root{k}", wd) for k, wd in enumerate(roots)] + [self.norm_root]
        self.xs = sb("xs", [T, D])
        self.xT = sb("xT", [KD, S])

    def stage_first(self, pool):
        self.nc.gpsimd.tensor_copy(self.xs[:], self.pg.x[:, 0, :, :]).then_inc(self.x_staged.sem, 1)

    def stage_next(self, pool, i):
        self.acc.wait_full(pool, i, 0)
        self.nc.gpsimd.tensor_copy(self.xs[:], self.pg.x[:, i + 1, :, :]).then_inc(self.x_staged.sem, 1)

    def roots(self, pool, i):
        for root in self.root:
            root.power(pool, i)

    def transpose_x(self, pe, i):
        pe.wait_ge(self.x_staged.sem, self.x_staged.at(i, 1))
        self.acc.wait_empty(pe, i, 0)
        transpose_tokens(self.nc, pe, self.acc.bank(0), self.xs, self.pg.c("ident")).then_inc(self.acc.full.sem, 1)

    def take_xT(self, act, i):
        self.acc.wait_full(act, i, 0)
        self.nc.scalar.activation(self.xT[:], shaped(self.acc.bank(0)[:], (KD, S)), ACT.Copy)\
            .then_inc(self.acc.empty.sem, 1)

    def project_out(self, pe, i, xT, w, bank, chunks, last_tile=None):
        pe.wait_ge(self.out_taken.sem, self.out_taken.at(i, 0))
        y = shaped(bank[:], (T, D))
        for t in range(T):
            for k in range(chunks):
                last = self.nc.tensor.matmul(y[:, t, :], xT[:, k, t * P:(t + 1) * P], w[:, k, :],
                                             start=(k == 0), stop=(k == chunks - 1))
        last.then_inc(self.out_ready.sem, 1)


def transpose_tokens(nc, pe, bank, src, ident, chunks=KD):
    for t in range(T):
        for k in range(chunks):
            last = nc.tensor.transpose(bank[:, k * S + t * P:k * S + (t + 1) * P],
                                       src[:, t, k * P:(k + 1) * P], ident)
    return last


def project_features(nc, bank, w, xT, tiles=KD):
    for m in range(tiles):
        for k in range(KD):
            last = nc.tensor.matmul(bank[:, m * S:(m + 1) * S], w[:, k, m * P:(m + 1) * P], xT[:, k, :],
                                    start=(k == 0), stop=(k == KD - 1))
    return last


def project_tokens(nc, out, w, xT, t):
    for k in range(KD):
        last = nc.tensor.matmul(out, xT[:, k, t * P:(t + 1) * P], w[:, k, :], start=(k == 0), stop=(k == KD - 1))
    return last


class Attention:
    DEPTHS = {"PROBS": 6, "TURNED": 4, "TURN_LAG": 4, "COPY_LAG": 5, "VALUE_LAG": 7}
    FEW_DEPTHS = {"PROBS": 4, "TURNED": 3, "TURN_LAG": 3, "COPY_LAG": 4, "VALUE_LAG": 5}

    def __init__(self, pg, ctx, name, units, few_keys, score_banks, difference=None):
        nc = self.nc = pg.nc
        self.pg, self.units, self.few, self.minus_lambda = pg, units, few_keys, difference
        self.parts = 2 if difference is not None else 1
        depths = self.FEW_DEPTHS if few_keys else self.DEPTHS
        self.PROBS, self.TURNED = depths["PROBS"], depths["TURNED"]
        self.TURN_LAG, self.COPY_LAG, self.VALUE_LAG = depths["TURN_LAG"], depths["COPY_LAG"], depths["VALUE_LAG"]
        n, m = len(units), len(units) * self.parts
        sig = lambda s, per, credit=0: Signal(ctx, nc, s, per, credit)
        sb = lambda s, dims: ctx.enter_context(nc.sbuf_tensor(f"{name}_{s}", [P, *dims], F32))
        self.s_bank, self.t_bank = score_banks, pg.bank[5:7]
        self.scored = sig("scored", m)
        self.maxed = sig("maxed", m)
        self.exps_ready = sig("exps_ready", m, len(score_banks))
        self.inverted = sig("inverted", m)
        self.probs_ready = sig("probs_ready", n)
        self.combined = sig("combined", n)
        self.transposed = sig("transposed", n, self.PROBS)
        self.turned = sig("turned", n, len(self.t_bank))
        self.valued = sig("valued", n, self.TURNED)
        self.probs = sb("probs", [self.PROBS, self.parts, 512])
        self.probsT = sb("probsT", [self.TURNED, 512])
        heads = units[0]["heads"]
        self.nmax = sb("nmax", [m, heads])
        self.sums = sb("sums", [m, heads])

    def credits_scalar(self, act):
        self.exps_ready.give(act)
        if self.few:
            self.turned.give(act)

    def credits_tensor(self, pe):
        self.transposed.give(pe)
        self.valued.give(pe)

    def credits_vector(self, dve):
        if not self.few:
            self.turned.give(dve)

    @staticmethod
    def chunks(unit):
        return unit["heads"] * unit["keys"] // P

    def turned_slot(self, u):
        return u % self.TURNED

    def slot(self, u, part, heads=None):
        h, k = self.units[u]["heads"], self.units[u]["keys"]
        ap = self.probs[:, u % self.PROBS, part, 0:h * k]
        return shaped(ap, (h, k)) if heads else ap

    def tensor(self, pe, i, score, value, before_last_bank=None, before_values=None, pieces=(), early={}):
        n, pieces = len(self.units), list(pieces)
        for s in range(n + self.VALUE_LAG):
            if s < n:
                for part in range(self.parts):
                    k = s * self.parts + part
                    if k == len(self.s_bank) - 1 and before_last_bank:
                        before_last_bank()
                    pe.wait_ge(self.exps_ready.sem, self.exps_ready.at(i, k + 1 - len(self.s_bank)))
                    score(k, self.units[s], part, self.s_bank[k % len(self.s_bank)]).then_inc(self.scored.sem, 1)
            u = s - self.TURN_LAG
            if 0 <= u < n:
                if self.parts == 2:
                    pe.wait_ge(self.combined.sem, self.combined.at(i, u + 1))
                else:
                    pe.wait_ge(self.probs_ready.sem, self.probs_ready.at(i, u + 1))
                pe.wait_ge(self.turned.sem, self.turned.at(i, u + 1 - 2))
                for c in range(self.chunks(self.units[u])):
                    last = self.nc.tensor.transpose(self.t_bank[u % 2][:, c * P:(c + 1) * P],
                                                    self.slot(u, self.parts - 1)[:, c * P:(c + 1) * P], self.pg.c("ident"))
                last.then_inc(self.transposed.sem, 1)
            u = s - self.VALUE_LAG
            if 0 <= u < n:
                if u == 0 and before_values:
                    before_values()
                pe.wait_ge(self.turned.sem, self.turned.at(i, u + 1))
                value(u, self.units[u], self.probsT[:, self.turned_slot(u), :]).then_inc(self.valued.sem, 1)
            if s in early:
                early[s]()
            piece = pieces.pop(0) if s >= n and pieces else None
            if piece:
                piece()
        for piece in pieces:
            piece()

    def score_unit(self, pe, i, u, score):
        pe.wait_ge(self.exps_ready.sem, self.exps_ready.at(i, u + 1 - len(self.s_bank)))
        score(u, self.units[u], 0, self.s_bank[u % len(self.s_bank)]).then_inc(self.scored.sem, 1)

    def turn_unit(self, pe, i, u):
        pe.wait_ge(self.probs_ready.sem, self.probs_ready.at(i, u + 1))
        pe.wait_ge(self.turned.sem, self.turned.at(i, u + 1 - 2))
        for c in range(self.chunks(self.units[u])):
            last = self.nc.tensor.transpose(self.t_bank[u % 2][:, c * P:(c + 1) * P],
                                            self.slot(u, 0)[:, c * P:(c + 1) * P], self.pg.c("ident"))
        last.then_inc(self.transposed.sem, 1)

    def value_unit(self, pe, i, u, value):
        pe.wait_ge(self.turned.sem, self.turned.at(i, u + 1))
        value(u, self.units[u], self.probsT[:, self.turned_slot(u), :]).then_inc(self.valued.sem, 1)

    def exp_unit(self, act, i, u):
        act.wait_ge(self.maxed.sem, self.maxed.at(i, u + 1))
        act.wait_ge(self.transposed.sem, self.transposed.at(i, u + 1 - self.PROBS))
        h, k = self.units[u]["heads"], self.units[u]["keys"]
        self.nc.scalar.activation(self.slot(u, 0), self.s_bank[u % len(self.s_bank)][:, 0:h * k], ACT.Exp)\
            .then_inc(self.exps_ready.sem, 1)

    def scalar(self, act, i, pieces=(), after_turn=None, early={}):
        n, pieces = len(self.units), list(pieces)
        for s in range(n + self.VALUE_LAG + (1 if after_turn else 0)):
            if s < n:
                h, k = self.units[s]["heads"], self.units[s]["keys"]
                for part in range(self.parts):
                    m = s * self.parts + part
                    act.wait_ge(self.maxed.sem, self.maxed.at(i, m + 1))
                    act.wait_ge(self.transposed.sem, self.transposed.at(i, s + 1 - self.PROBS))
                    src, dst = self.s_bank[m % len(self.s_bank)], self.slot(s, part)
                    if self.few:
                        last = self.nc.scalar.activation(dst, src[:, 0:h * k], ACT.Exp)
                    else:
                        for j in range(h):
                            last = self.nc.scalar.activation(dst[:, j * k:(j + 1) * k], src[:, j * k:(j + 1) * k], ACT.Exp,
                                                             bias=self.nmax[:, m, j:j + 1],
                                                             accum_out=self.sums[:, m, j:j + 1])
                    last.then_inc(self.exps_ready.sem, 1)
            if self.few and 0 <= s - self.COPY_LAG < n:
                self.turn(act, i, s - self.COPY_LAG)
            if after_turn and s - self.VALUE_LAG - 1 >= 0:
                after_turn(s - self.VALUE_LAG - 1)
            if s in early:
                early[s]()
            piece = pieces.pop(0) if s >= n and pieces else None
            if piece:
                piece()
        for piece in pieces:
            piece()

    def turn(self, eng, i, u):
        size = self.chunks(self.units[u]) * P
        eng.wait_ge(self.transposed.sem, self.transposed.at(i, u + 1))
        eng.wait_ge(self.valued.sem, self.valued.at(i, u + 1 - self.TURNED))
        dst, src = self.probsT[:, self.turned_slot(u), 0:size], self.t_bank[u % 2][:, 0:size]
        if self.few:
            self.nc.scalar.activation(dst, src, ACT.Copy).then_inc(self.turned.sem, 1)
        else:
            self.nc.vector.tensor_copy(dst, src).then_inc(self.turned.sem, 1)

    def gpsimd(self, pool, i, between=None, early={}):
        for u in range(len(self.units)):
            m = u * self.parts
            pool.wait_ge(self.inverted.sem, self.inverted.at(i, m + 1))
            p = self.slot(u, 0, heads=True)
            self.nc.gpsimd.tensor_tensor(p, p, over(self.sums[:, m, :], 2, self.units[u]["keys"]), ALU.mult)\
                .then_inc(self.probs_ready.sem, 1)
            if u == 1 and between:
                between()
            if u in early:
                early[u]()

    def invert(self, dve, i, m, chain):
        nc, u, part = self.nc, m // self.parts, m % self.parts
        dve.wait_ge(self.exps_ready.sem, self.exps_ready.at(i, m + 1))
        sums = self.sums[:, m, :]
        if self.few:
            chain.step(nc.vector.tensor_reduce(sums, self.slot(u, 0, heads=True), AX, ALU.add))
        if self.parts == 2 and part == 0:
            chain.step(nc.vector.reciprocal(sums, sums))
            g = self.units[u]["g"]
            nc.vector.tensor_tensor(sums, sums, self.minus_lambda[:, 2 * g:2 * g + 2], ALU.mult).then_inc(self.inverted.sem, 1)
            return
        nc.vector.reciprocal(sums, sums).then_inc(self.inverted.sem, 1)

    def combine(self, dve, i, u):
        dve.wait_ge(self.inverted.sem, self.inverted.at(i, 2 * u + 2))
        dve.wait_ge(self.probs_ready.sem, self.probs_ready.at(i, u + 1))
        for j in range(2):
            first, second = (self.slot(u, part, heads=True)[:, j, :] for part in range(2))
            last = self.nc.vector.scalar_tensor_tensor(out=second, in0=second, scalar=self.sums[:, 2 * u + 1, j:j + 1],
                                                       in1=first, op0=ALU.mult, op1=ALU.add)
        last.then_inc(self.combined.sem, 1)

    def vector(self, dve, i, chain, pieces=(), early={}):
        n, pieces = len(self.units), list(pieces)
        nc = self.nc
        for s in range(n + self.COPY_LAG):
            for part in range(self.parts):
                m = s * self.parts + part
                if s < n:
                    unit = self.units[s]
                    h, k = unit["heads"], unit["keys"]
                    bank = shaped(self.s_bank[m % len(self.s_bank)][:, 0:h * k], (h, k))
                    dve.wait_ge(self.scored.sem, self.scored.at(i, m + 1))
                    for lo, hi, mask in unit["masks"]:
                        chain.step(nc.vector.tensor_tensor(bank[:, :, lo:hi], bank[:, :, lo:hi], over(mask, 1, h), ALU.add))
                    if self.few:
                        chain.step(nc.vector.tensor_reduce(self.nmax[:, m, :], bank, AX, ALU.max))
                        nc.vector.tensor_tensor(bank, bank, over(self.nmax[:, m, :], 2, k), ALU.subtract)\
                            .then_inc(self.maxed.sem, 1)
                    else:
                        nc.vector.tensor_reduce(self.nmax[:, m, :], bank, AX, ALU.max, negate=True)\
                            .then_inc(self.maxed.sem, 1)
                if 0 <= s - 1 < n:
                    self.invert(dve, i, m - self.parts, chain)
            if self.parts == 2 and 0 <= s - 2 < n:
                self.combine(dve, i, s - 2)
            if not self.few and 0 <= s - self.COPY_LAG < n:
                self.turn(dve, i, s - self.COPY_LAG)
            piece = pieces.pop(0) if s >= 1 and pieces else None
            if piece:
                piece()
            if s in early:
                early[s]()


def attention_steps(units, few):
    return sum(len(u["masks"]) for u in units) + (2 * len(units) if few else 0)


def pair_units(masks_of, keys_of):
    return [{"t": t, "g": g, "heads": 2, "keys": keys_of[t], "masks": masks_of[t]} for t in range(T) for g in range(8)]


def pair_scores(nc, u, qT, kblk, bank, place=0):
    r, m, keys = 32 * ((u["g"] + place) % 4), u["g"] // 4, u["keys"]
    return nc.tensor.matmul(bank[:, 0:2 * keys], qT[r:r + 32, m, u["t"] * P:(u["t"] + 1) * P],
                            kblk[r:r + 32, m, :, 0:keys], start=True, stop=True)


def pair_values(nc, u, probsT, out, value_of):
    tiles, r = u["keys"] // P, 32 * (u["g"] % 4)
    cols = (u["g"] // 4) * S + u["t"] * P
    for j in range(2):
        for c in range(tiles):
            at = (j * tiles + c) * P
            last = nc.tensor.matmul(out[r:r + 32, cols:cols + P], value_of(c, u["g"], j), probsT[:, at:at + P],
                                    start=(j == 0 and c == 0), stop=(j == 1 and c == tiles - 1))
    return last


def pad_values(nc, vpad, src):
    for j in range(2):
        for c in range(T):
            last = nc.scalar.activation(vpad[:, c, :, j, j * HD:(j + 1) * HD],
                                        src[:, c, :].rearrange("p (g j d) -> p g j d", j=2, d=HD)[:, :, j, :], ACT.Copy)
    return last


def batches(eng, head, tail, finish=None):
    head(0)
    if finish is None:
        with eng.Fori(0, B - 1) as i:
            tail(i, True)
        tail(B - 1, False)
        return
    tail(0, True, False)
    with eng.Fori(1, B - 1) as i:
        tail(i, True, True)
    tail(B - 1, False, True)
    finish(B - 1)


def spread_keys(nc, kblk, src, par2):
    for par in range(2):
        last = nc.scalar.activation(kblk[:, :, par, :], src, ACT.Copy, scale=par2[:, par:par + 1])
    return last


def flat(ap):
    names = "abcdef"[:len(ap.shape) - 1]
    return ap.rearrange(f"p {' '.join(names)} -> p ({' '.join(names)})")


def differential_attention(pg, n):
    nc = pg.nc
    with Scope(nc, f"s{n}") as ctx:
        units = pair_units([[], []], [S, S])
        body = Body(pg, ctx, 6, attention_steps(units, False) + len(units), f"s{n}")
        acc = body.acc
        sb = lambda s, dims: ctx.enter_context(nc.sbuf_tensor(f"s{n}_{s}", [P, *dims], F32))
        minus_lambda = sb("minus_lambda", [NH])
        att = Attention(pg, ctx, f"s{n}", units, False, pg.bank[2:5], difference=minus_lambda)
        qT = [sb(f"q{w}T", [KD, S]) for w in (1, 2)]
        kblk = [sb(f"k{w}", [KD, 2, S]) for w in (1, 2)]
        vpad, oT = sb("vpad", [T, 8, 2, 32]), sb("oT", [KD, S])
        o_taken = Signal(ctx, nc, "o_taken", 1, credit=1)
        ready = Signal(ctx, nc, "ready", 0)
        w = {k: pg.w(n, k, KD, D) for k in ("q1", "k1", "q2", "k2", "v", "o")}
        o_bank, y_bank = pg.bank[7], pg.bank[4]
        with nc.Block() as block:
            prefetch(pg, block, n)

            @block.gpsimd
            def _(pool):
                start(pg, pool, n)

                def tail(i, more, before):
                    if more:
                        body.stage_next(pool, i)
                    att.gpsimd(pool, i, (lambda: body.roots(pool, i - 1)) if before else None)
                batches(pool, lambda i: body.stage_first(pool), tail, lambda i: body.roots(pool, i))

            @block.tensor
            def _(pe):
                start(pg, pe, n)
                att.credits_tensor(pe)

                def projections(i):
                    def features(k, name):
                        if k == 1:
                            acc.wait_emptied(pe, i, 0)
                        acc.wait_empty(pe, i, k)
                        project_features(nc, acc.bank(k), w[name], body.xT).then_inc(acc.full.sem, 1)

                    def values():
                        acc.wait_empty(pe, i, 5)
                        for t in range(T):
                            last = project_tokens(nc, acc.bank(5)[:, t * D:(t + 1) * D], w["v"], body.xT, t)
                        last.then_inc(acc.full.sem, 1)
                    return [lambda k=k, name=name: features(k + 1, name)
                                  for k, name in enumerate(("q1", "k1", "q2", "k2"))] + [values]

                def head(i):
                    body.transpose_x(pe, i)
                    for piece in projections(i):
                        piece()

                def tail(i, more):
                    acc.wait_emptied(pe, i, 5)
                    att.tensor(pe, i,
                               lambda k, u, part, bank: pair_scores(nc, u, qT[1 - part], kblk[1 - part], bank,
                                                                    place=1 - part),
                               lambda s, u, probsT: pair_values(nc, u, probsT, o_bank, lambda c, g, j: vpad[:, c, g, j, :]),
                               before_last_bank=lambda: pe.wait_ge(body.out_taken.sem, body.out_taken.at(i, 0)),
                               before_values=lambda: pe.wait_ge(o_taken.sem, o_taken.at(i, 0)),
                               pieces=projections(i + 1) if more else (),
                               early={8: lambda: body.transpose_x(pe, i + 1)} if more else {})
                    pe.wait_ge(o_taken.sem, o_taken.at(i, 1))
                    body.project_out(pe, i, oT, w["o"], y_bank, KD)
                batches(pe, head, tail)

            @block.scalar
            def _(act):
                start(pg, act, n)
                acc.empty.give(act)
                att.credits_scalar(act)
                o_taken.give(act)
                act.wait_ge(ready.sem, 1)
                view = lambda k: shaped(acc.bank(k)[:], (KD, S))

                def takes(i):
                    def queries(which, k):
                        acc.wait_full(act, i, k)
                        nc.scalar.activation(qT[which][:], view(k), ACT.Copy, scale=0.25).then_inc(acc.empty.sem, 1)

                    def keys(which, k):
                        acc.wait_full(act, i, k)
                        spread_keys(nc, kblk[which], view(k), pg.c("par2")).then_inc(acc.empty.sem, 1)
                    return [lambda: queries(0, 1), lambda: keys(0, 2),
                            lambda: queries(1, 3), lambda: keys(1, 4)]

                def take_values(i):
                    acc.wait_full(act, i, 5)
                    pad_values(nc, vpad, view(5)).then_inc(acc.empty.sem, 1)

                def head(i):
                    body.take_xT(act, i)
                    for take in takes(i):
                        take()
                    take_values(i)

                def tail(i, more):
                    att.scalar(act, i, takes(i + 1) if more else (),
                               early={9: lambda: body.take_xT(act, i + 1)} if more else {})
                    act.wait_ge(att.valued.sem, att.valued.at(i, len(units)))
                    nc.scalar.activation(oT[:], shaped(o_bank[:], (KD, S)), ACT.Copy).then_inc(o_taken.sem, 1)
                    if more:
                        take_values(i + 1)
                batches(act, head, tail)

            @block.vector
            def _(dve):
                start(pg, dve, n)
                body.out_taken.give(dve)
                att.credits_vector(dve)
                nc.vector.memset(vpad[:], 0.0)
                nc.vector.tensor_scalar(minus_lambda[:], pg.w(n, "lam"), -1.0, None, ALU.mult).then_inc(ready.sem, 1)
                dve.wait_ge(ready.sem, 1)

                def tail(i, more, before):
                    chain = Chain(body.vchain, dve, i)
                    att.vector(dve, i, chain, body.norm_pieces(dve, i - 1) if before else ())
                    body.add(dve, i, y_bank)
                    chain.done()
                batches(dve, lambda i: None, tail, lambda i: body.norm(dve, i))


class GatedTiles:
    SLOTS = 3

    def __init__(self, pg, ctx, name, tiles, gu_banks, w_banks=()):
        self.nc, self.tiles, self.banks, self.w_banks = pg.nc, tiles, gu_banks, w_banks
        sig = lambda s, credit=0: Signal(ctx, pg.nc, s, tiles, credit)
        sb = lambda s, dims: ctx.enter_context(pg.nc.sbuf_tensor(f"{name}_{s}", [P, *dims], F32))
        self.gu_full = sig("gu_full")
        self.tanh_ready = sig("tanh_ready")
        self.half_done = sig("half_done")
        self.hidden_ready = sig("hidden_ready", len(gu_banks))
        self.down_done = sig("down_done", self.SLOTS)
        self.tanh, self.half = sb("tanh", [2, S]), sb("half", [2, S])
        self.hidden = sb("hidden", [self.SLOTS, S])
        if w_banks:
            self.w_full = sig("w_full")
            self.w_ready = sig("w_ready", 2)
            self.scaled_ready = sig("scaled_ready", self.SLOTS)
            self.wsb, self.scaled = sb("wsb", [2, S]), sb("scaled", [self.SLOTS, S])
        self.down_src = self.scaled if w_banks else self.hidden
        self.down_ready = self.scaled_ready if w_banks else self.hidden_ready

    def credits(self, pe=None, act=None, dve=None, pool=None):
        if pe:
            self.down_done.give(pe)
        if act and self.w_banks:
            self.w_ready.give(act)
        if dve:
            self.hidden_ready.give(dve)
        if pool and self.w_banks:
            self.scaled_ready.give(pool)

    def gate_up(self, pe, i, g, xT, wg, wu, extra=None):
        pe.wait_ge(self.hidden_ready.sem, self.hidden_ready.at(i, g + 1 - len(self.banks)))
        bank = self.banks[g % len(self.banks)]
        for half, w in enumerate((wg, wu)):
            out = bank[:, half * S:(half + 1) * S]
            for k in range(KD):
                more = extra if half == 0 else None
                last = self.nc.tensor.matmul(out, w[:, g, k, :], xT[:, k, :], start=(k == 0),
                                             stop=(k == KD - 1 and not more))
            if more:
                more(out, g)
        last.then_inc(self.gu_full.sem, 1)

    def spread_weights(self, pe, i, g, owner, combT):
        pe.wait_ge(self.w_ready.sem, self.w_ready.at(i, g + 1 - 2))
        self.nc.tensor.matmul(self.w_banks[g % 2][:, 0:S], owner[:, g * P:(g + 1) * P], combT, start=True, stop=True)\
            .then_inc(self.w_full.sem, 1)

    def down(self, pe, i, g, wd, bank, first, last_one):
        pe.wait_ge(self.down_ready.sem, self.down_ready.at(i, g + 1))
        y = shaped(bank[:], (T, D))
        for t in range(T):
            last = self.nc.tensor.matmul(y[:, t, :], self.down_src[:, g % self.SLOTS, t * P:(t + 1) * P], wd[:, g, :],
                                         start=(first and t == 0), stop=last_one, skip_group_check=True)
        last.then_inc(self.down_done.sem, 1)
        return last

    def scalar(self, act, i, g):
        act.wait_ge(self.gu_full.sem, self.gu_full.at(i, g + 1))
        act.wait_ge(self.hidden_ready.sem, self.hidden_ready.at(i, g + 1 - 2))
        self.nc.scalar.activation(self.tanh[:, g % 2, :], self.banks[g % len(self.banks)][:, 0:S], ACT.Tanh, scale=0.5)\
            .then_inc(self.tanh_ready.sem, 1)

    def scalar_weights(self, act, i, g):
        act.wait_ge(self.w_full.sem, self.w_full.at(i, g + 1))
        act.wait_ge(self.scaled_ready.sem, self.scaled_ready.at(i, g + 1 - 2))
        self.nc.scalar.activation(self.wsb[:, g % 2, :], self.w_banks[g % 2][:, 0:S], ACT.Copy).then_inc(self.w_ready.sem, 1)

    def vector(self, dve, i, g):
        bank = self.banks[g % len(self.banks)]
        dve.wait_ge(self.tanh_ready.sem, self.tanh_ready.at(i, g + 1))
        self.nc.vector.scalar_tensor_tensor(out=self.half[:, g % 2, :], in0=self.tanh[:, g % 2, :], scalar=1.0,
                                            in1=bank[:, 0:S], op0=ALU.add, op1=ALU.mult).then_inc(self.half_done.sem, 1)
        dve.wait_ge(self.half_done.sem, self.half_done.at(i, g + 1))
        freed = self.scaled_ready if self.w_banks else self.down_done
        dve.wait_ge(freed.sem, freed.at(i, g + 1 - self.SLOTS))
        self.nc.vector.scalar_tensor_tensor(out=self.hidden[:, g % self.SLOTS, :], in0=self.half[:, g % 2, :], scalar=0.5,
                                            in1=bank[:, S:2 * S], op0=ALU.mult, op1=ALU.mult)\
            .then_inc(self.hidden_ready.sem, 1)

    def pool(self, pool, i, g):
        pool.wait_ge(self.w_ready.sem, self.w_ready.at(i, g + 1))
        pool.wait_ge(self.hidden_ready.sem, self.hidden_ready.at(i, g + 1))
        pool.wait_ge(self.down_done.sem, self.down_done.at(i, g + 1 - self.SLOTS))
        self.nc.gpsimd.tensor_tensor(self.scaled[:, g % self.SLOTS, :], self.hidden[:, g % self.SLOTS, :],
                                     self.wsb[:, g % 2, :], ALU.mult).then_inc(self.scaled_ready.sem, 1)


class Tokens(Ending):

    def __init__(self, pg, ctx, name):
        super().__init__(pg, ctx, name)
        self.xT = ctx.enter_context(pg.nc.sbuf_tensor(f"{name}_xT", [P, B, KD, S], F32))
        self.turned = Signal(ctx, pg.nc, "turned", 0)
        self.taken = Signal(ctx, pg.nc, "taken", 0)

    def tensor(self, pe):
        for b in range(B):
            if b >= 2:
                pe.wait_ge(self.taken.sem, b - 1)
            transpose_tokens(self.nc, pe, self.pg.bank[b % 2], self.pg.x[:, b, :, :], self.pg.c("ident"))\
                .then_inc(self.turned.sem, 1)

    def scalar(self, act):
        for b in range(B):
            act.wait_ge(self.turned.sem, b + 1)
            self.nc.scalar.activation(self.xT[:, b, :, :], shaped(self.pg.bank[b % 2][:], (KD, S)), ACT.Copy)\
                .then_inc(self.taken.sem, 1)


class Routing:

    def __init__(self, pg, ctx, name, experts, top, shared, over_all, bias=None):
        nc = self.nc = pg.nc
        self.pg, self.E, self.top, self.shared, self.over_all, self.bias = pg, experts, top, shared, over_all, bias
        self.cols = experts + (1 if shared else 0)
        sb = lambda s, dims, p=P: ctx.enter_context(nc.sbuf_tensor(f"{name}_{s}", [p, *dims], F32))
        R, E = B * T, experts
        self.logits, self.comb = sb("logits", [R, self.cols]), sb("comb", [R, self.cols])
        self.combT = sb("combT", [B, S], self.cols)
        self.beats, self.ties = sb("beats", [R, E, E]), sb("ties", [R, E, E])
        self.rank, self.top1, self.shifted = sb("rank", [R, E]), sb("top1", [R]), sb("shifted", [R, self.cols])
        self.exps, self.total = sb("exps", [R, self.cols]), sb("total", [R])
        sig = lambda s: Signal(ctx, nc, s, 0)
        self.logits_full, self.logits_taken, self.route_steps = sig("logits_full"), sig("logits_taken"), sig("route_steps")
        self.shifted_ready, self.exps_ready, self.comb_ready = sig("shifted_ready"), sig("exps_ready"), sig("comb_ready")
        self.comb_turned, self.combT_ready = sig("comb_turned"), sig("combT_ready")

    def tensor(self, pe, tokens, gate):
        pe.wait_ge(tokens.taken.sem, B)
        for b in range(B):
            for t in range(T):
                at = (b * T + t) * self.cols
                last = project_tokens(self.nc, self.pg.bank[0][:, at:at + self.cols], gate, tokens.xT[:, b, :, :], t)
        last.then_inc(self.logits_full.sem, 1)

    def turn(self, pe):
        pe.wait_ge(self.comb_ready.sem, 1)
        for b in range(B):
            for t in range(T):
                at = (b % 2) * S + t * P
                last = self.nc.tensor.transpose(self.pg.bank[b // 2][0:self.cols, at:at + P], self.comb[:, b * T + t, :],
                                                self.pg.c("ident"))
        last.then_inc(self.comb_turned.sem, 1)

    def scalar(self, act):
        act.wait_ge(self.logits_full.sem, 1)
        self.nc.scalar.activation(flat(self.logits[:]), self.pg.bank[0][:, 0:B * T * self.cols], ACT.Copy)\
            .then_inc(self.logits_taken.sem, 1)
        act.wait_ge(self.shifted_ready.sem, 1)
        self.nc.scalar.activation(self.exps[:], self.shifted[:], ACT.Exp).then_inc(self.exps_ready.sem, 1)

    def take_turned(self, act):
        act.wait_ge(self.comb_turned.sem, 1)
        for half in range(B // 2):
            self.nc.scalar.activation(self.combT[:, 2 * half:2 * half + 2, :],
                                      shaped(self.pg.bank[half][0:self.cols, :], (2, S)), ACT.Copy)\
                .then_inc(self.combT_ready.sem, 1)

    def vector(self, dve):
        nc, E, R = self.nc, self.E, B * T
        chain = Chain(self.route_steps, dve, 0)
        dve.wait_ge(self.logits_taken.sem, 1)
        l = self.logits[:, :, 0:E]
        if self.bias is not None:
            chain.step(nc.vector.tensor_tensor(l, l, over(self.bias, 1, R), ALU.add))
        mine, other = over(l, 3, E), over(l, 2, E)
        nc.vector.tensor_tensor(self.beats[:], other, mine, ALU.is_gt)
        chain.step(nc.vector.tensor_tensor(self.ties[:], other, mine, ALU.is_equal))
        tri = shaped(self.pg.c("tri"), (8, 8))[:, 0:E, 0:E]
        chain.step(nc.vector.tensor_tensor(self.ties[:], self.ties[:], over(tri, 1, R), ALU.mult))
        chain.step(nc.vector.tensor_tensor(self.beats[:], self.beats[:], self.ties[:], ALU.add))
        chain.step(nc.vector.tensor_reduce(self.rank[:], self.beats[:], AX, ALU.add))
        chain.step(nc.vector.tensor_reduce(self.top1[:], l, AX, ALU.max))
        if self.shared:
            chain.step(nc.vector.tensor_scalar(self.shifted[:, :, E:E + 1], self.logits[:, :, E:E + 1], -1.0, None, ALU.mult))
        nc.vector.tensor_tensor(self.shifted[:, :, 0:E], l, over(self.top1[:], 2, E), ALU.subtract)\
            .then_inc(self.shifted_ready.sem, 1)
        chain.step(nc.vector.tensor_scalar(self.rank[:], self.rank[:], float(self.top), None, ALU.is_lt))
        dve.wait_ge(self.exps_ready.sem, 1)
        e, c = self.exps[:, :, 0:E], self.comb[:, :, 0:E]
        chain.step(nc.vector.tensor_tensor(c, e, self.rank[:], ALU.mult))
        chain.step(nc.vector.tensor_reduce(self.total[:], e if self.over_all else c, AX, ALU.add))
        chain.step(nc.vector.reciprocal(self.total[:], self.total[:]))
        if self.shared:
            z = self.comb[:, :, E:E + 1]
            chain.step(nc.vector.tensor_scalar(z, self.exps[:, :, E:E + 1], 1.0, None, ALU.add))
            nc.vector.reciprocal(z, z)
        nc.vector.tensor_tensor(c, c, over(self.total[:], 2, E), ALU.mult).then_inc(self.comb_ready.sem, 1)
        dve.wait_ge(self.comb_ready.sem, 1)


def weighted_experts(pg, n, experts, top, shared, tiles):
    nc = pg.nc
    with Scope(nc, f"s{n}") as ctx:
        route = Routing(pg, ctx, f"s{n}", experts, top, shared, over_all=False)
        tokens = Tokens(pg, ctx, f"s{n}")
        ff = GatedTiles(pg, ctx, f"s{n}", tiles, [pg.bank[2], pg.bank[3], pg.bank[7]], pg.bank[5:7])
        cols = route.cols
        combT = ctx.enter_context(nc.sbuf_tensor(f"s{n}_combT_now", [cols, S], F32))
        combT_staged = Signal(ctx, nc, "combT_staged", 1)
        gate = pg.w(n, "gate", KD, cols)
        wg, wu, wd = pg.w(n, "g", tiles, KD, P), pg.w(n, "u", tiles, KD, P), pg.w(n, "d", tiles, D)
        owner, y_bank = pg.w(n, "owner", rows=cols), pg.bank[4]
        with nc.Block() as block:
            prefetch(pg, block, n)

            @block.gpsimd
            def _(pool):
                start(pg, pool, n)
                ff.credits(pool=pool)
                pool.wait_ge(route.combT_ready.sem, B // 2)
                with pool.Fori(0, B) as i:
                    nc.gpsimd.tensor_copy(combT[:], route.combT[:, i, :]).then_inc(combT_staged.sem, 1)
                    for g in range(tiles):
                        ff.pool(pool, i, g)
                    tokens.norm_root.power(pool, i)

            @block.tensor
            def _(pe):
                start(pg, pe, n)
                ff.credits(pe=pe)
                tokens.tensor(pe)
                route.tensor(pe, tokens, gate)
                route.turn(pe)
                with pe.Fori(0, B) as i:
                    for s in range(tiles + 3):
                        if s < tiles:
                            ff.gate_up(pe, i, s, tokens.xT[:, i, :, :], wg, wu)
                        if s == 2:
                            pe.wait_ge(combT_staged.sem, combT_staged.at(i, 1))
                        if 0 <= s - 2 < tiles:
                            ff.spread_weights(pe, i, s - 2, owner, combT[:])
                        if s == 3:
                            pe.wait_ge(tokens.out_taken.sem, tokens.out_taken.at(i, 0))
                        if 0 <= s - 3 < tiles:
                            ff.down(pe, i, s - 3, wd, y_bank, first=(s == 3), last_one=(s - 3 == tiles - 1))

            @block.scalar
            def _(act):
                start(pg, act, n)
                ff.credits(act=act)
                tokens.scalar(act)
                route.scalar(act)
                route.take_turned(act)
                with act.Fori(0, B) as i:
                    for g in range(tiles):
                        ff.scalar(act, i, g)
                        ff.scalar_weights(act, i, g)

            @block.vector
            def _(dve):
                start(pg, dve, n)
                tokens.out_taken.give(dve)
                ff.credits(dve=dve)
                route.vector(dve)
                with dve.Fori(0, B) as i:
                    for g in range(tiles):
                        ff.vector(dve, i, g)
                    dve.wait_ge(ff.down_done.sem, ff.down_done.at(i, tiles))
                    tokens.add_norm(dve, i, y_bank, wait_out=False)


def top1_experts(pg, n):
    nc = pg.nc
    E, per, tiles = 4, 8, 32
    with Scope(nc, f"s{n}") as ctx:
        route = Routing(pg, ctx, f"s{n}", E, 1, False, over_all=True, bias=pg.w(n, "br"))
        tokens = Tokens(pg, ctx, f"s{n}")
        ff = GatedTiles(pg, ctx, f"s{n}", tiles, [pg.bank[2], pg.bank[3], pg.bank[5]])
        gate = pg.w(n, "gate", KD, E)
        wg, wu, wd = pg.w(n, "g", tiles, KD, P), pg.w(n, "u", tiles, KD, P), pg.overflow(n, tiles, D)
        weight = ctx.enter_context(nc.sbuf_tensor(f"s{n}_weight", [P, T, E], F32))
        y_banks = [pg.bank[4], pg.bank[7]]
        expert_taken = Signal(ctx, nc, "expert_taken", E, credit=2)
        weight_ready = Signal(ctx, nc, "weight_ready", 1)
        with nc.Block() as block:
            prefetch(pg, block, n)

            @block.gpsimd
            def _(pool):
                start(pg, pool, n)
                pool.wait_ge(route.comb_ready.sem, 1)
                with pool.Fori(0, B) as i:
                    nc.gpsimd.tensor_copy(weight[:], shaped(flat(route.comb[:]), (B, T, E))[:, i, :, :]).then_inc(weight_ready.sem, 1)
                    tokens.norm_root.power(pool, i)

            @block.tensor
            def _(pe):
                start(pg, pe, n)
                ff.credits(pe=pe)
                tokens.tensor(pe)
                route.tensor(pe, tokens, gate)
                with pe.Fori(0, B) as i:
                    for s in range(tiles + 2):
                        if s < tiles:
                            ff.gate_up(pe, i, s, tokens.xT[:, i, :, :], wg, wu)
                        g = s - 2
                        if 0 <= g < tiles:
                            e = g // per
                            if g % per == 0:
                                pe.wait_ge(expert_taken.sem, expert_taken.at(i, e + 1 - 2))
                            ff.down(pe, i, g, wd, y_banks[e % 2], first=(g % per == 0), last_one=(g % per == per - 1))

            @block.scalar
            def _(act):
                start(pg, act, n)
                tokens.scalar(act)
                route.scalar(act)
                with act.Fori(0, B) as i:
                    for g in range(tiles):
                        ff.scalar(act, i, g)

            @block.vector
            def _(dve):
                start(pg, dve, n)
                expert_taken.give(dve)
                ff.credits(dve=dve)
                route.vector(dve)
                with dve.Fori(0, B) as i:

                    def take(e):
                        dve.wait_ge(ff.down_done.sem, ff.down_done.at(i, (e + 1) * per))
                        y = shaped(y_banks[e % 2][:], (T, D))
                        for t in range(T):
                            before = pg.x[:, i, t, :] if e == 0 else tokens.r[:, t, :]
                            last = nc.vector.scalar_tensor_tensor(out=tokens.r[:, t, :], in0=y[:, t, :],
                                                                  scalar=weight[:, t, e:e + 1], in1=before,
                                                                  op0=ALU.mult, op1=ALU.add)
                        last.then_inc(expert_taken.sem, 1)
                        dve.wait_ge(expert_taken.sem, expert_taken.at(i, e + 1))
                    for g in range(tiles):
                        ff.vector(dve, i, g)
                        if g == per + 3:
                            dve.wait_ge(weight_ready.sem, weight_ready.at(i, 1))
                        if g % per == 3 and g > per:
                            take(g // per - 1)
                    take(E - 1)
                    tokens.norm(dve, i)


def modulated_ffn(pg, n):
    nc = pg.nc
    R, tiles = 16, 8
    with Scope(nc, f"s{n}") as ctx:
        causal = pg.c("causal")
        units = pair_units([[(0, P, causal)], [(P, S, causal)]], [P, S])
        body = Body(pg, ctx, 6, attention_steps(units, False), f"s{n}", roots=(T,))
        att = Attention(pg, ctx, f"s{n}", units, False, pg.bank[2:5])
        ff = GatedTiles(pg, ctx, f"s{n}", tiles, pg.bank[2:4])
        acc = body.acc
        sb = lambda s, dims, p=P: ctx.enter_context(nc.sbuf_tensor(f"s{n}_{s}", [p, *dims], F32))
        x_rms, h1T, h2T = sb("x_rms", [T, D]), body.xT, sb("h2T", [KD, S])
        squares, sumsq = sb("squares", [T, D]), sb("sumsq", [T])
        qT, kblk, vpad = sb("qT", [KD, S]), sb("kblk", [KD, 2, S]), sb("vpad", [T, 8, 2, 32])
        oT, attnT = sb("oT", [KD, S]), sb("attnT", [KD, S])
        mod, hA, prod = sb("mod", [S], R), sb("hA", [S], R), sb("prod", [S], R)
        o_taken = Signal(ctx, nc, "o_taken", 1, credit=1)
        padded = Signal(ctx, nc, "padded", 0)
        summed = Signal(ctx, nc, "summed", 1)
        rms_ready = Signal(ctx, nc, "rms_ready", 1)
        mod_ready = Signal(ctx, nc, "mod_ready", 1)
        w = {k: pg.w(n, k, KD, D) for k in ("q", "k", "v", "o")}
        A, Bw = pg.w(n, "A", KD, R), pg.w(n, "B", rows=R)
        wg, wu, wd = pg.w(n, "g", tiles, KD, P), pg.w(n, "u", tiles, KD, P), pg.w(n, "d", tiles, D)
        o_bank, y_bank = pg.bank[7], pg.bank[4]
        with nc.Block() as block:
            prefetch(pg, block, n)

            @block.gpsimd
            def _(pool):
                start(pg, pool, n)

                def head(i):
                    body.stage_first(pool)
                    body.root[0].power(pool, i)

                def tail(i, more, before):
                    if more:
                        pool.wait_ge(rms_ready.sem, rms_ready.at(i, 1))
                        nc.gpsimd.tensor_copy(body.xs[:], pg.x[:, i + 1, :, :]).then_inc(body.x_staged.sem, 1)
                    att.gpsimd(pool, i, (lambda: body.norm_root.power(pool, i - 1)) if before else None)
                    if more:
                        body.root[0].power(pool, i + 1)
                batches(pool, head, tail, lambda i: body.norm_root.power(pool, i))

            @block.tensor
            def _(pe):
                start(pg, pe, n)
                att.credits_tensor(pe)
                ff.credits(pe=pe)

                def projections(i):
                    def x():
                        pe.wait_ge(rms_ready.sem, rms_ready.at(i, 1))
                        acc.wait_empty(pe, i, 0)
                        transpose_tokens(nc, pe, acc.bank(0), x_rms, pg.c("ident")).then_inc(acc.full.sem, 1)
                        acc.wait_emptied(pe, i, 0)

                    def features(k, name):
                        acc.wait_empty(pe, i, k)
                        project_features(nc, acc.bank(k), w[name], h1T).then_inc(acc.full.sem, 1)

                    def values():
                        acc.wait_empty(pe, i, 3)
                        for t in range(T):
                            last = project_tokens(nc, acc.bank(3)[:, t * D:(t + 1) * D], w["v"], h1T, t)
                        last.then_inc(acc.full.sem, 1)
                    return [x, lambda: features(1, "q"), lambda: features(2, "k"), values]

                def head(i):
                    for piece in projections(i):
                        piece()

                def modulate(i, out, g):
                    if g == 0:
                        pe.wait_ge(mod_ready.sem, mod_ready.at(i, 1))
                    return nc.tensor.matmul(out, Bw[:, g * P:(g + 1) * P], prod[:], start=False, stop=True)

                def tail(i, more):
                    acc.wait_emptied(pe, i, 3)
                    att.tensor(pe, i, lambda k, u, part, bank: pair_scores(nc, u, qT, kblk, bank),
                               lambda s, u, probsT: pair_values(nc, u, probsT, o_bank, lambda c, g, j: vpad[:, c, g, j, :]),
                               before_last_bank=lambda: pe.wait_ge(body.out_taken.sem, body.out_taken.at(i, 0)),
                               before_values=lambda: pe.wait_ge(o_taken.sem, o_taken.at(i, 0)))
                    pe.wait_ge(o_taken.sem, o_taken.at(i, 1))
                    acc.wait_empty(pe, i, 4)
                    project_features(nc, acc.bank(4), w["o"], oT).then_inc(acc.full.sem, 1)
                    acc.wait_emptied(pe, i, 4)
                    acc.wait_empty(pe, i, 5)
                    for half, src in enumerate((attnT, h2T)):
                        for k in range(KD):
                            last = nc.tensor.matmul(acc.bank(5)[0:R, half * S:(half + 1) * S], A[:, k, :], src[:, k, :],
                                                    start=(k == 0), stop=(k == KD - 1))
                    last.then_inc(acc.full.sem, 1)
                    for s in range(tiles + 2):
                        if s < tiles:
                            ff.gate_up(pe, i, s, h2T, wg, wu, extra=lambda out, g: modulate(i, out, g))
                        if s == 2:
                            pe.wait_ge(body.out_taken.sem, body.out_taken.at(i, 0))
                        if s >= 2:
                            ff.down(pe, i, s - 2, wd, y_bank, first=(s == 2), last_one=(s == tiles + 1))
                    if more:
                        head(i + 1)
                batches(pe, head, tail)

            @block.scalar
            def _(act):
                start(pg, act, n)
                acc.empty.give(act)
                att.credits_scalar(act)
                o_taken.give(act)
                act.wait_ge(padded.sem, 1)
                view = lambda k: shaped(acc.bank(k)[:], (KD, S))

                def sum_squares(i):
                    act.wait_ge(body.x_staged.sem, body.x_staged.at(i, 1))
                    for t in range(T):
                        last = nc.scalar.activation(squares[:, t, :], body.xs[:, t, :], ACT.Square,
                                                    accum_out=sumsq[:, t:t + 1])
                    last.then_inc(summed.sem, 1)

                def takes(i):
                    acc.wait_full(act, i, 0)
                    for name, dst in (("ln1", h1T), ("ln2", h2T)):
                        for k in range(KD):
                            last = nc.scalar.activation(dst[:, k, :], acc.bank(0)[:, k * S:(k + 1) * S], ACT.Copy,
                                                        scale=pg.w(n, name)[:, k:k + 1])
                    last.then_inc(acc.empty.sem, 1)
                    acc.wait_full(act, i, 1)
                    nc.scalar.activation(qT[:], view(1), ACT.Copy, scale=0.25).then_inc(acc.empty.sem, 1)
                    acc.wait_full(act, i, 2)
                    spread_keys(nc, kblk, view(2), pg.c("par2")).then_inc(acc.empty.sem, 1)
                    acc.wait_full(act, i, 3)
                    pad_values(nc, vpad, view(3)).then_inc(acc.empty.sem, 1)

                def head(i):
                    sum_squares(i)
                    takes(i)

                def tail(i, more):
                    att.scalar(act, i)
                    act.wait_ge(att.valued.sem, att.valued.at(i, len(units)))
                    nc.scalar.activation(oT[:], shaped(o_bank[:], (KD, S)), ACT.Copy).then_inc(o_taken.sem, 1)
                    acc.wait_full(act, i, 4)
                    nc.scalar.activation(attnT[:], view(4), ACT.Copy).then_inc(acc.empty.sem, 1)
                    acc.wait_full(act, i, 5)
                    nc.scalar.activation(mod[:], acc.bank(5)[0:R, 0:S], ACT.Tanh)
                    nc.scalar.activation(hA[:], acc.bank(5)[0:R, S:2 * S], ACT.Copy).then_inc(acc.empty.sem, 1)
                    if more:
                        sum_squares(i + 1)
                    for g in range(tiles):
                        ff.scalar(act, i, g)
                    if more:
                        takes(i + 1)
                batches(act, head, tail)

            @block.vector
            def _(dve):
                start(pg, dve, n)
                body.out_taken.give(dve)
                nc.vector.memset(vpad[:], 0.0).then_inc(padded.sem, 1)
                att.credits_vector(dve)
                ff.credits(dve=dve)

                def head(i):
                    dve.wait_ge(summed.sem, summed.at(i, 1))
                    nc.vector.tensor_scalar(body.root[0].t[:], sumsq[:], 1.0 / D, RMS_EPS, ALU.mult, ALU.add)\
                        .then_inc(body.root[0].wanted.sem, 1)
                    body.root[0].wait(dve, i)
                    nc.vector.tensor_tensor(x_rms[:], body.xs[:], over(body.root[0].t[:], 2, D), ALU.mult)\
                        .then_inc(rms_ready.sem, 1)

                def tail(i, more, before):
                    chain = Chain(body.vchain, dve, i)
                    att.vector(dve, i, chain, body.norm_pieces(dve, i - 1) if before else ())
                    chain.done()
                    acc.wait_emptied(dve, i, 5)
                    nc.vector.scalar_tensor_tensor(out=prod[:], in0=mod[:], scalar=0.1, in1=hA[:],
                                                   op0=ALU.mult, op1=ALU.mult).then_inc(mod_ready.sem, 1)
                    for g in range(tiles):
                        ff.vector(dve, i, g)
                    if more:
                        head(i + 1)
                    dve.wait_ge(ff.down_done.sem, ff.down_done.at(i, tiles))
                    body.add(dve, i, y_bank, x_times=2.0, wait_out=False)
                batches(dve, head, tail, lambda i: body.norm(dve, i))


def windowed_attention(pg, n):
    nc = pg.nc
    HK = 4
    H = NH + HK
    with Scope(nc, f"s{n}") as ctx:
        units = pair_units([[(0, P, pg.c("near"))], [(0, S, pg.c("window"))]], [P, S])
        body = Body(pg, ctx, 5, attention_steps(units, False), f"s{n}", roots=(T * H,))
        att = Attention(pg, ctx, f"s{n}", units, False, pg.bank[2:5])
        acc = body.acc
        sb = lambda s, dims: ctx.enter_context(nc.sbuf_tensor(f"s{n}_{s}", [P, *dims], F32))
        qk, turned, v = sb("qk", [T, H, HD]), sb("turned", [T, H, HD]), sb("v", [T, HK, HD])
        sumsq, krep = sb("sumsq", [T, H]), sb("krep", [T, NH, HD])
        qT, kblk, oT, vpad = sb("qT", [KD, S]), sb("kblk", [KD, 2, S]), sb("oT", [KD, S]), sb("vpad", [T, HK, 2, 32])
        o_taken = Signal(ctx, nc, "o_taken", 1, credit=1)
        padded = Signal(ctx, nc, "padded", 0)
        v_ready = Signal(ctx, nc, "v_ready", 1)
        unit_steps = Signal(ctx, nc, "unit_steps", 7)
        unit_ready = Signal(ctx, nc, "unit_ready", 1)
        w, wo = pg.w(n, "w", KD, D + 2 * HK * HD), pg.w(n, "wo", KD, D)
        o_bank, y_bank = pg.bank[7], pg.bank[4]
        with nc.Block() as block:
            prefetch(pg, block, n)

            @block.gpsimd
            def _(pool):
                start(pg, pool, n)

                def head(i):
                    body.root[0].power(pool, i)

                def tail(i, more, before):
                    if more:
                        body.stage_next(pool, i)
                    att.gpsimd(pool, i, (lambda: body.norm_root.power(pool, i - 1)) if before else None,
                               early={12: lambda: head(i + 1)} if more else {})
                batches(pool, lambda i: (body.stage_first(pool), head(i)), tail,
                        lambda i: body.norm_root.power(pool, i))

            @block.tensor
            def _(pe):
                start(pg, pe, n)
                att.credits_tensor(pe)

                def projections(i):
                    def x():
                        body.transpose_x(pe, i)

                    def tokens(k, lo, hi):
                        acc.wait_emptied(pe, i, 0)
                        acc.wait_empty(pe, i, k)
                        for t in range(T):
                            last = project_tokens(nc, acc.bank(k)[:, t * (hi - lo):(t + 1) * (hi - lo)],
                                                  w[:, :, lo:hi], body.xT, t)
                        last.then_inc(acc.full.sem, 1)
                    return [x, lambda: tokens(1, 0, D), lambda: tokens(2, D, D + 2 * HK * HD)]

                def turn(i, fill, src):
                    pe.wait_ge(unit_ready.sem, unit_ready.at(i, 1))
                    acc.wait_empty(pe, i, fill)
                    for t in range(T):
                        for k in range(KD):
                            last = nc.tensor.transpose(acc.bank(fill)[:, k * S + t * P:k * S + (t + 1) * P],
                                                       src[:, t, k * 8:(k + 1) * 8, :].rearrange("p h d -> p (h d)"),
                                                       pg.c("ident"))
                    last.then_inc(acc.full.sem, 1)

                def turns(i):
                    return [lambda: turn(i, 3, qk), lambda: turn(i, 4, krep)]

                def head(i):
                    for piece in projections(i) + turns(i):
                        piece()

                def before_values(i):
                    pe.wait_ge(o_taken.sem, o_taken.at(i, 0))
                    pe.wait_ge(v_ready.sem, v_ready.at(i, 1))

                def tail(i, more):
                    acc.wait_emptied(pe, i, 4)
                    att.tensor(pe, i, lambda k, u, part, bank: pair_scores(nc, u, qT, kblk, bank),
                               lambda s, u, probsT: pair_values(nc, u, probsT, o_bank,
                                                                lambda c, g, j: vpad[:, c, g // 2, j, :]),
                               before_last_bank=lambda: pe.wait_ge(body.out_taken.sem, body.out_taken.at(i, 0)),
                               before_values=lambda: before_values(i), pieces=[None] * 1 + turns(i + 1) if more else (),
                               early=dict(zip((3, 7, 9), projections(i + 1))) if more else {})
                    pe.wait_ge(o_taken.sem, o_taken.at(i, 1))
                    body.project_out(pe, i, oT, wo, y_bank, KD)
                batches(pe, head, tail)

            @block.scalar
            def _(act):
                start(pg, act, n)
                acc.empty.give(act)
                att.credits_scalar(act)
                o_taken.give(act)
                act.wait_ge(padded.sem, 1)

                def takes(i):
                    def queries():
                        acc.wait_full(act, i, 1)
                        nc.scalar.activation(qk[:, :, 0:NH, :].rearrange("p t h d -> p t (h d)"),
                                             shaped(acc.bank(1)[:], (T, D)), ACT.Copy).then_inc(acc.empty.sem, 1)

                    def keys_values():
                        acc.wait_full(act, i, 2)
                        kv = shaped(acc.bank(2)[:, 0:T * 2 * HK * HD], (T, 2, HK * HD))
                        nc.scalar.activation(qk[:, :, NH:H, :].rearrange("p t h d -> p t (h d)"), kv[:, :, 0, :], ACT.Copy)
                        nc.scalar.activation(v[:].rearrange("p t h d -> p t (h d)"), kv[:, :, 1, :], ACT.Copy)\
                            .then_inc(acc.empty.sem, 1)
                    return [lambda: body.take_xT(act, i), queries, keys_values]

                def take_turned(i):
                    def queries():
                        acc.wait_full(act, i, 3)
                        nc.scalar.activation(qT[:], shaped(acc.bank(3)[:], (KD, S)), ACT.Copy).then_inc(acc.empty.sem, 1)

                    def keys():
                        acc.wait_full(act, i, 4)
                        spread_keys(nc, kblk, shaped(acc.bank(4)[:], (KD, S)), pg.c("par2")).then_inc(acc.empty.sem, 1)
                    return [queries, keys]

                def pad(i):
                    acc.wait_emptied(act, i, 2)
                    for j in range(2):
                        last = nc.scalar.activation(vpad[:, :, :, j, j * HD:(j + 1) * HD].rearrange("p t g d -> p (t g) d"),
                                                    v[:].rearrange("p t g d -> p (t g) d"), ACT.Copy)
                    last.then_inc(v_ready.sem, 1)

                def head(i):
                    for take in takes(i) + take_turned(i):
                        take()
                    pad(i)

                def tail(i, more):
                    att.scalar(act, i, [None] * 1 + take_turned(i + 1) if more else (),
                               early=dict(zip((4, 8, 10), takes(i + 1))) if more else {})
                    act.wait_ge(att.valued.sem, att.valued.at(i, len(units)))
                    nc.scalar.activation(oT[:], shaped(o_bank[:], (KD, S)), ACT.Copy).then_inc(o_taken.sem, 1)
                    if more:
                        pad(i + 1)
                batches(act, head, tail)

            @block.vector
            def _(dve):
                start(pg, dve, n)
                body.out_taken.give(dve)
                nc.vector.memset(vpad[:], 0.0).then_inc(padded.sem, 1)
                att.credits_vector(dve)
                cos, sin = (over(shaped(pg.c(k), (T, HD)), 2, H) for k in ("cos", "sin"))
                half = HD // 2

                def head_pieces(i):
                    chain = Chain(unit_steps, dve, i)

                    def cross():
                        acc.wait_emptied(dve, i, 2)
                        nc.vector.tensor_tensor(turned[:, :, :, 0:half], qk[:, :, :, half:HD], sin[:, :, :, 0:half], ALU.mult)
                        chain.step(nc.vector.tensor_tensor(turned[:, :, :, half:HD], qk[:, :, :, 0:half],
                                                           sin[:, :, :, half:HD], ALU.mult))

                    def straight():
                        chain.step(nc.vector.tensor_tensor(qk[:], qk[:], cos, ALU.mult))
                        chain.step(nc.vector.tensor_tensor(qk[:], qk[:], turned[:], ALU.add))

                    def lengths():
                        chain.step(nc.vector.tensor_tensor(turned[:], qk[:], qk[:], ALU.mult))
                        chain.step(nc.vector.tensor_reduce(sumsq[:], turned[:], AX, ALU.add))
                        nc.vector.tensor_scalar(body.root[0].t[:], flat(sumsq[:]), 1e-24, None, ALU.max)\
                            .then_inc(body.root[0].wanted.sem, 1)

                    def scaled():
                        body.root[0].wait(dve, i)
                        rt = shaped(body.root[0].t[:], (T, H))
                        chain.step(nc.vector.tensor_tensor(rt[:, :, 0:NH], rt[:, :, 0:NH], over(pg.w(n, "temp"), 1, T), ALU.mult))
                        chain.step(nc.vector.tensor_tensor(qk[:], qk[:], over(rt, 3, HD), ALU.mult))

                    def repeated():
                        for t in range(T):
                            last = nc.vector.tensor_copy(krep[:, t, :, :].rearrange("p (g r) d -> p g r d", g=HK),
                                                         over(qk[:, t, NH:H, :], 2, NH // HK))
                        last.then_inc(unit_ready.sem, 1)
                        chain.done()
                    return {10: cross, 11: straight, 12: lengths, 15: scaled, 16: repeated}

                def head(i):
                    for piece in head_pieces(i).values():
                        piece()

                def tail(i, more, before):
                    chain = Chain(body.vchain, dve, i)
                    att.vector(dve, i, chain, body.norm_pieces(dve, i - 1) if before else (),
                               early=head_pieces(i + 1) if more else {})
                    chain.done()
                    body.add(dve, i, y_bank)
                batches(dve, head, tail, lambda i: body.norm(dve, i))


def decay_attention(pg, n):
    nc = pg.nc
    W = S + P
    with Scope(nc, f"s{n}") as ctx:
        body = Body(pg, ctx, 5, 0, f"s{n}", roots=(T,))
        acc = body.acc
        sb = lambda s, dims: ctx.enter_context(nc.sbuf_tensor(f"s{n}_{s}", [P, *dims], F32))
        sig = lambda s, per, credit=0: Signal(ctx, nc, s, per, credit)
        raw, th = sb("raw", [2, KD, S]), sb("th", [2, KD, S])
        q2T, k2T, kblk, vpad, uT = sb("q2T", [KD, S]), sb("k2T", [KD, S]), sb("kblk", [KD, 2, S]), sb("vpad", [T, 8, 2, 32]), sb("uT", [KD, S])
        oT, squares = sb("oT", [KD, S]), sb("squares", [KD, S])
        weighted = sb("weighted", [3, W])
        decay = pg.spare(n, 0, NH, W)
        minus_slope = pg.spare(n, NH * W, NH)
        slope_ready, exps_done, decay_ready = sig("slope_ready", 1), sig("exps_done", 1), sig("decay_ready", 1)
        keys_ready = sig("keys_ready", 1)
        scored = sig("scored", NH)
        s_banks, sum_bank = [pg.bank[2], pg.bank[3], pg.bank[5]], pg.bank[6]
        weighted_ready = sig("weighted_ready", NH, len(s_banks))
        valued = sig("valued", NH, 3)
        gated = sig("gated", 1)
        o_taken = sig("o_taken", 1, 1)
        sums_ready = sig("sums_ready", 1)
        silu_steps = sig("silu_steps", 1)
        w, wo = pg.w(n, "w", KD, 4 * D), pg.w(n, "wo", KD, D)
        o_bank, y_bank = pg.bank[7], pg.bank[4]
        with nc.Block() as block:
            prefetch(pg, block, n)

            @block.gpsimd
            def _(pool):
                start(pg, pool, n)

                def tail(i, more, before):
                    if more:
                        body.stage_next(pool, i)
                    if before:
                        body.roots(pool, i - 1)
                batches(pool, lambda i: body.stage_first(pool), tail, lambda i: body.roots(pool, i))

            @block.tensor
            def _(pe):
                start(pg, pe, n)
                valued.give(pe)

                def x(i):
                    body.transpose_x(pe, i)
                    acc.wait_emptied(pe, i, 0)

                def features(i, k, which):
                    acc.wait_empty(pe, i, k)
                    project_features(nc, acc.bank(k), w[:, :, which * D:(which + 1) * D], body.xT).then_inc(acc.full.sem, 1)

                def values(i):
                    acc.wait_empty(pe, i, 3)
                    for t in range(T):
                        last = project_tokens(nc, acc.bank(3)[:, t * D:(t + 1) * D], w[:, :, 2 * D:3 * D], body.xT, t)
                    last.then_inc(acc.full.sem, 1)

                def early(i):
                    return [lambda: x(i), lambda: features(i, 1, 0), lambda: features(i, 2, 1)]

                def late(i):
                    values(i)
                    features(i, 4, 3)

                def head(i):
                    for piece in early(i):
                        piece()
                    late(i)

                def score(i, h):
                    pe.wait_ge(weighted_ready.sem, weighted_ready.at(i, h + 1 - len(s_banks)))
                    r, m, j = 32 * (h % 8 // 2), h // 8, h % 2
                    for c in range(T):
                        last = nc.tensor.matmul(s_banks[h % 3][:, c * S:c * S + S - c * P],
                                                kblk[r:r + 32, m, j, c * P:(c + 1) * P],
                                                q2T[r:r + 32, m, c * P:S], start=True, stop=True)
                    last.then_inc(scored.sem, 1)

                def value(i, h):
                    pe.wait_ge(weighted_ready.sem, weighted_ready.at(i, h + 1))
                    p, pair, j = weighted[:, h % 3, :], h // 2, h % 2
                    r, at = 32 * (pair % 4), (pair // 4) * S
                    nc.tensor.matmul(o_bank[r:r + 32, at:at + S], vpad[:, 0, pair, j, :], p[:, 0:S],
                                     start=(j == 0), stop=False, skip_group_check=True)
                    nc.tensor.matmul(o_bank[r:r + 32, at + P:at + S], vpad[:, 1, pair, j, :], p[:, S:W],
                                     start=False, stop=(j == 1), skip_group_check=True).then_inc(valued.sem, 1)

                def tail(i, more):
                    pieces = early(i + 1) if more else []
                    acc.wait_emptied(pe, i, 4)
                    pe.wait_ge(keys_ready.sem, keys_ready.at(i, 1))
                    for s in range(NH + 2):
                        if s < NH:
                            score(i, s)
                        if s == 2:
                            acc.wait_emptied(pe, i, 3)
                            pe.wait_ge(o_taken.sem, o_taken.at(i, 0))
                        if s >= 2:
                            value(i, s - 2)
                        if s >= NH // 2 and s % 2 == 0 and pieces:
                            pieces.pop(0)()
                    if more:
                        late(i + 1)
                    pe.wait_ge(gated.sem, gated.at(i, 1))
                    body.project_out(pe, i, oT, wo, y_bank, KD)
                    pe.wait_ge(o_taken.sem, o_taken.at(i, 1))
                    for t in range(T):
                        for k in range(KD):
                            last = nc.tensor.matmul(sum_bank[:, t:t + 1], squares[:, k, t * P:(t + 1) * P], pg.w(n, "one"),
                                                    start=(k == 0), stop=(k == KD - 1))
                    last.then_inc(sums_ready.sem, 1)
                batches(pe, head, tail)

            @block.scalar
            def _(act):
                start(pg, act, n)
                acc.empty.give(act)
                o_taken.give(act)
                act.wait_ge(slope_ready.sem, 1)
                for h in range(NH):
                    last = nc.scalar.activation(decay[:, h, 0:S], pg.w(n, "dist"), ACT.Exp, scale=minus_slope[:, h:h + 1])
                last.then_inc(exps_done.sem, 1)

                def take_raw(i, k):
                    acc.wait_full(act, i, 1 + k)
                    view = shaped(acc.bank(1 + k)[:], (KD, S))
                    nc.scalar.activation(raw[:, k, :, :], view, ACT.Copy)
                    nc.scalar.activation(th[:, k, :, :], view, ACT.Tanh, scale=0.5).then_inc(acc.empty.sem, 1)

                def early(i):
                    body.take_xT(act, i)
                    for k in range(2):
                        take_raw(i, k)

                def late(i):
                    acc.wait_full(act, i, 3)
                    pad_values(nc, vpad, shaped(acc.bank(3)[:], (T, D))).then_inc(acc.empty.sem, 1)
                    acc.wait_full(act, i, 4)
                    nc.scalar.activation(uT[:], shaped(acc.bank(4)[:], (KD, S)), ACT.Copy).then_inc(acc.empty.sem, 1)

                def head(i):
                    early(i)
                    late(i)

                def tail(i, more):
                    if more:
                        act.wait_ge(keys_ready.sem, keys_ready.at(i, 1))
                        early(i + 1)
                    act.wait_ge(gated.sem, gated.at(i, 1))
                    nc.scalar.activation(squares[:], shaped(o_bank[:], (KD, S)), ACT.Square).then_inc(o_taken.sem, 1)
                    if more:
                        late(i + 1)
                batches(act, head, tail)

            @block.vector
            def _(dve):
                start(pg, dve, n)
                body.out_taken.give(dve)
                weighted_ready.give(dve)
                nc.vector.memset(vpad[:], 0.0)
                nc.vector.tensor_scalar(minus_slope, pg.w(n, "slope"), -1.0, None, ALU.mult).then_inc(slope_ready.sem, 1)
                dve.wait_ge(exps_done.sem, 1)
                for h in range(NH):
                    last = nc.vector.scalar_tensor_tensor(out=decay[:, h, 0:S], in0=decay[:, h, 0:S], scalar=0.25,
                                                          in1=pg.w(n, "valid"), op0=ALU.mult, op1=ALU.mult)
                last.then_inc(decay_ready.sem, 1)
                dve.wait_ge(decay_ready.sem, 1)
                nc.vector.tensor_copy(decay[:, :, S:W], decay[:, :, 0:P]).then_inc(decay_ready.sem, 1)
                dve.wait_ge(decay_ready.sem, 2)

                def head(i):
                    acc.wait_emptied(dve, i, 2)
                    for k, dst in ((0, q2T), (1, k2T)):
                        last = nc.vector.scalar_tensor_tensor(out=dst[:], in0=th[:, k, :, :], scalar=1.0,
                                                              in1=raw[:, k, :, :], op0=ALU.add, op1=ALU.mult)
                    last.then_inc(silu_steps.sem, 1)
                    dve.wait_ge(silu_steps.sem, silu_steps.at(i, 1))
                    for par in range(2):
                        last = nc.vector.tensor_scalar(kblk[:, :, par, :], k2T[:], pg.c("par2")[:, par:par + 1], None,
                                                       ALU.mult)
                    last.then_inc(keys_ready.sem, 1)

                def divide(i):
                    dve.wait_ge(sums_ready.sem, sums_ready.at(i, 1))
                    nc.vector.tensor_scalar(body.root[0].t[:], sum_bank[:, 0:T], 1.0 / D, RMS_EPS, ALU.mult, ALU.add)\
                        .then_inc(body.root[0].wanted.sem, 1)

                def add(i):
                    rms, y = body.root[0], shaped(y_bank[:], (T, D))
                    rms.wait(dve, i)
                    for t in range(T):
                        last = nc.vector.scalar_tensor_tensor(out=body.r[:, t, :], in0=y[:, t, :], scalar=rms.t[:, t:t + 1],
                                                              in1=pg.x[:, i, t, :], op0=ALU.mult, op1=ALU.add)
                    last.then_inc(body.out_taken.sem, 1)
                    dve.wait_ge(body.out_taken.sem, body.out_taken.at(i, 1))

                def finish(i):
                    divide(i)
                    add(i)
                    body.norm(dve, i)

                def tail(i, more, before):
                    pieces = [lambda: divide(i - 1), None, lambda: add(i - 1), *body.norm_pieces(dve, i - 1)] if before else []
                    for h in range(NH):
                        dve.wait_ge(scored.sem, scored.at(i, h + 1))
                        dve.wait_ge(valued.sem, valued.at(i, h + 1 - 3))
                        nc.vector.tensor_tensor(weighted[:, h % 3, :], s_banks[h % 3][:, 0:W], decay[:, h, :], ALU.mult)\
                            .then_inc(weighted_ready.sem, 1)
                        piece = pieces.pop(0) if pieces else None
                        if piece:
                            piece()
                    acc.wait_emptied(dve, i, 4)
                    dve.wait_ge(valued.sem, valued.at(i, NH))
                    nc.vector.tensor_tensor(oT[:], shaped(o_bank[:], (KD, S)), uT[:], ALU.mult).then_inc(gated.sem, 1)
                    if more:
                        head(i + 1)
                batches(dve, head, tail, finish)


def head_attention(pg, n):
    nc = pg.nc
    with Scope(nc, f"s{n}") as ctx:
        body = Body(pg, ctx, 5, 0, f"s{n}", bias=pg.w(n, "bo"))
        acc = body.acc
        sb = lambda s, dims: ctx.enter_context(nc.sbuf_tensor(f"s{n}_{s}", [P, *dims], F32))
        sig = lambda s, per, credit=0: Signal(ctx, nc, s, per, credit)
        POOL_HEADS = 9
        shares = {"pool": slice(0, POOL_HEADS), "own": slice(POOL_HEADS, NH)}
        qkv = sb("qkv", [T, 3, D])
        pool_products = sb("pool_products", [2, POOL_HEADS, NH, HD])
        own_products = sb("own_products", [2, NH - POOL_HEADS, NH, HD])
        scores, top, sums = sb("scores", [T, NH, NH]), sb("top", [T, NH]), sb("sums", [T, NH])
        o, regrouped, oT = sb("o", [T, NH, HD]), sb("regrouped", [T, D]), sb("oT", [KD, S])
        regroup = nc.dram_tensor(f"regroup{n}", [B, NH, S, HD], F32, kind="Internal").ap()
        pool_ready = [sig("pool_scores", T), sig("pool_values", T)]
        own_ready = [sig("own_scores", T), sig("own_values", T)]
        summed = [sig("scores_summed", 2 * T, 1), sig("values_summed", 2 * T, 1)]
        shifted, exps_ready, probs_ready = sig("shifted", T), sig("exps_ready", T), sig("probs_ready", T)
        soft_steps = sig("soft_steps", 3 * T)
        written = sig("written", 16 * T, 1)
        read_back = sig("read_back", 16)
        turned = sig("turned", 1)
        turned_taken = sig("turned_taken", 1, 1)
        w, wo = pg.w(n, "w", KD, 3 * D), pg.w(n, "wo", KD, D)
        turn_bank, y_bank = pg.bank[2], pg.bank[4]

        def operands(stage, t, mine):
            head = lambda a: shaped(qkv[:, t, a, :], (NH, HD))
            count = mine.stop - mine.start
            if stage == 0:
                return over(head(0)[:, mine, :], 2, NH), over(head(1), 1, count)
            return over(scores[:, t, mine, :], 2, HD), over(head(2).rearrange("p g d -> p d g"), 1, count)

        def regroup_rows(sp):
            written.give(sp)
            with sp.Fori(0, B) as i:
                for t in range(T):
                    sp.wait_ge(summed[1].sem, summed[1].at(i, 2 * t + 2))
                    sp.dma_start(regroup[i, :, t * P:(t + 1) * P, :].rearrange("h p d -> p h d"), o[:, t, :, :])\
                        .then_inc(written.sem, 16)
                sp.wait_ge(written.sem, written.at(i, 16 * T))
                sp.dma_start(regrouped[:], regroup[i].rearrange("h (r c) d -> (h r) (c d)", c=NH)
                             .rearrange("(t p) d -> p t d", p=P)).then_inc(read_back.sem, 16)

        with nc.Block() as block:
            prefetch(pg, block, n, regroup_rows)

            @block.gpsimd
            def _(pool):
                start(pg, pool, n)

                def multiply(stage, i, t):
                    if stage == 0:
                        acc.wait_emptied(pool, i, 1 + 2 * t)
                    else:
                        acc.wait_emptied(pool, i, 2 + 2 * t)
                        pool.wait_ge(probs_ready.sem, probs_ready.at(i, t + 1))
                    pool.wait_ge(summed[stage].sem, summed[stage].at(i, 2 * t))
                    in0, in1 = operands(stage, t, shares["pool"])
                    nc.gpsimd.tensor_tensor(pool_products[:, stage, :, :, :], in0, in1, ALU.mult)\
                        .then_inc(pool_ready[stage].sem, 1)

                def head(i):
                    body.stage_first(pool)
                    multiply(0, i, 0)

                def tail(i, more, before):
                    if more:
                        body.stage_next(pool, i)
                    multiply(0, i, 1)
                    multiply(1, i, 0)
                    if more:
                        multiply(0, i + 1, 0)
                    if before:
                        body.roots(pool, i - 1)
                    multiply(1, i, 1)
                batches(pool, head, tail, lambda i: body.roots(pool, i))

            @block.tensor
            def _(pe):
                start(pg, pe, n)

                def project(i, k, t, cols):
                    acc.wait_empty(pe, i, k)
                    out = acc.bank(k)[:, 0:cols.stop - cols.start]
                    for c in range(KD):
                        nc.tensor.matmul(out, body.xT[:, c, t * P:(t + 1) * P], w[:, c, cols], start=(c == 0), stop=False)
                    nc.tensor.matmul(out, pg.w(n, "first"), pg.w(n, "b")[:, cols], start=False, stop=True)\
                        .then_inc(acc.full.sem, 1)

                def head(i, before=None):
                    if before is not None:
                        acc.wait_emptied(pe, before, 4)
                    body.transpose_x(pe, i)
                    acc.wait_emptied(pe, i, 0)
                    for t in range(T):
                        project(i, 1 + 2 * t, t, slice(0, 2 * D))
                        project(i, 2 + 2 * t, t, slice(2 * D, 3 * D))

                def finish(i):
                    pe.wait_ge(read_back.sem, read_back.at(i, 16))
                    pe.wait_ge(turned_taken.sem, turned_taken.at(i, 0))
                    transpose_tokens(nc, pe, turn_bank, regrouped, pg.c("ident")).then_inc(turned.sem, 1)
                    pe.wait_ge(turned_taken.sem, turned_taken.at(i, 1))
                    body.project_out(pe, i, oT, wo, y_bank, KD)

                def tail(i, more, before):
                    if before:
                        finish(i - 1)
                    if more:
                        head(i + 1, before=i)
                batches(pe, head, tail, finish)

            @block.scalar
            def _(act):
                start(pg, act, n)
                acc.empty.give(act)
                turned_taken.give(act)

                def take(i, k, dst):
                    acc.wait_full(act, i, k)
                    width = dst.shape[-1] * (dst.shape[1] if len(dst.shape) == 3 else 1)
                    src = acc.bank(k)[:, 0:width]
                    nc.scalar.activation(dst, shaped(src, (2, D)) if len(dst.shape) == 3 else src, ACT.Copy)\
                        .then_inc(acc.empty.sem, 1)

                def exps(i, t):
                    act.wait_ge(shifted.sem, shifted.at(i, t + 1))
                    nc.scalar.activation(scores[:, t, :, :], scores[:, t, :, :], ACT.Exp, scale=1.0 / 16)\
                        .then_inc(exps_ready.sem, 1)

                def head(i, before=None):
                    body.take_xT(act, i)
                    for t in range(T):
                        if before is not None:
                            act.wait_ge(summed[0].sem, summed[0].at(before, 2 * t + 2))
                        take(i, 1 + 2 * t, qkv[:, t, 0:2, :])
                        if before is not None:
                            act.wait_ge(summed[1].sem, summed[1].at(before, 2 * t + 2))
                        take(i, 2 + 2 * t, qkv[:, t, 2, :])
                        if t == 0:
                            exps(i, 0)

                def finish(i):
                    act.wait_ge(turned.sem, turned.at(i, 1))
                    nc.scalar.activation(oT[:], shaped(turn_bank[:], (KD, S)), ACT.Copy).then_inc(turned_taken.sem, 1)

                def tail(i, more, before):
                    exps(i, 1)
                    if before:
                        finish(i - 1)
                    if more:
                        head(i + 1, before=i)
                batches(act, head, tail, finish)

            @block.vector
            def _(dve):
                start(pg, dve, n)
                body.out_taken.give(dve)
                for stage in range(2):
                    summed[stage].give(dve)

                def combine(stage, i, t):
                    dst = (scores, o)[stage]
                    acc.wait_emptied(dve, i, 1 + stage + 2 * t)
                    in0, in1 = operands(stage, t, shares["own"])
                    nc.vector.tensor_tensor(own_products[:, stage, :, :, :], in0, in1, ALU.mult)\
                        .then_inc(own_ready[stage].sem, 1)
                    if stage == 1:
                        dve.wait_ge(written.sem, written.at(i, 0))
                    for k, (products, ready, who) in enumerate(((own_products, own_ready, "own"),
                                                                (pool_products, pool_ready, "pool"))):
                        dve.wait_ge(ready[stage].sem, ready[stage].at(i, t + 1))
                        nc.vector.tensor_reduce(dst[:, t, shares[who], :], products[:, stage, :, :, :], AX, ALU.add)\
                            .then_inc(summed[stage].sem, 1)

                def shift(i, t):
                    dve.wait_ge(summed[0].sem, summed[0].at(i, 2 * t + 2))
                    step(i, 3 * t, nc.vector.tensor_reduce(top[:, t, :], scores[:, t, :, :], AX, ALU.max))
                    nc.vector.tensor_tensor(scores[:, t, :, :], scores[:, t, :, :], over(top[:, t, :], 2, NH), ALU.subtract)\
                        .then_inc(shifted.sem, 1)

                def normalise(i, t):
                    dve.wait_ge(exps_ready.sem, exps_ready.at(i, t + 1))
                    step(i, 3 * t + 1, nc.vector.tensor_reduce(sums[:, t, :], scores[:, t, :, :], AX, ALU.add))
                    step(i, 3 * t + 2, nc.vector.reciprocal(sums[:, t, :], sums[:, t, :]))
                    nc.vector.tensor_tensor(scores[:, t, :, :], scores[:, t, :, :], over(sums[:, t, :], 2, NH), ALU.mult)\
                        .then_inc(probs_ready.sem, 1)

                def step(i, k, instruction):
                    instruction.then_inc(soft_steps.sem, 1)
                    dve.wait_ge(soft_steps.sem, soft_steps.at(i, k + 1))

                def values(i, t):
                    dve.wait_ge(probs_ready.sem, probs_ready.at(i, t + 1))
                    combine(1, i, t)

                def head(i):
                    combine(0, i, 0)
                    shift(i, 0)
                    normalise(i, 0)

                def tail(i, more, before):
                    combine(0, i, 1)
                    shift(i, 1)
                    values(i, 0)
                    normalise(i, 1)
                    pieces = body.norm_pieces(dve, i - 1) if before else ()
                    if before:
                        body.add(dve, i - 1, y_bank)
                        pieces[0]()
                    if more:
                        combine(0, i + 1, 0)
                        shift(i + 1, 0)
                    if before:
                        pieces[-1]()
                    values(i, 1)
                    if more:
                        normalise(i + 1, 0)

                batches(dve, head, tail, lambda i: body.add_norm(dve, i, y_bank))


def latent_attention(pg, n, rotate_queries):
    nc = pg.nc
    CQ, DC, PAIRS = 96, 64, NH // 2
    with Scope(nc, f"s{n}") as ctx:
        units = [{"t": t, "g": g, "heads": 8, "keys": NK, "masks": []} for t in range(T) for g in range(2)]
        U = len(units)
        fills = 1 + 4
        body = Body(pg, ctx, fills, attention_steps(units, True), f"s{n}",
                    elsewhere=range(1, 5) if rotate_queries else ())
        att = Attention(pg, ctx, f"s{n}", units, True, pg.bank[2:4])
        acc = body.acc
        sb = lambda s, dims, p=P: ctx.enter_context(nc.sbuf_tensor(f"s{n}_{s}", [p, *dims], F32))
        sig = lambda s, per, credit=0: Signal(ctx, nc, s, per, credit)
        wq, kckv = pg.w(n, "wq", NH, D), pg.w(n, "kckv", NH, DC)
        qr, kr, wo = pg.w(n, "qr", NH, 2 * CQ, rows=DC), pg.w(n, "kr", NH, DC, rows=DC), pg.w(n, "wo", NH, D)
        QR = pg.spare(n, 0, NH, 2, DC, rows=CQ)
        OUT = pg.spare(n, 2048, PAIRS, D)
        if rotate_queries:
            kcq = pg.w(n, "kcq", NH, 2 * CQ)
            BIG = pg.over_weights(n, "kckv", 0, NH, KD, 2 * CQ)
            qcos, qsin = pg.w(n, "qcos", 2, S, rows=CQ), pg.w(n, "qsin", 2, S, rows=CQ)
        else:
            kcq = pg.w(n, "kcq", 2, NH, P, rows=CQ)
            MID = pg.over_weights(n, "kckv", 0, NH, DC)
            Q = pg.over_weights(n, "kckv", NH * DC, KD, NH, DC)
        kv, swapped = sb("kv", [B, DC]), sb("swapped", [B, DC])
        vblk, kblk = sb("vblk", [B, P]), sb("kblk", [B, P])
        v = sb("v", [P])
        qT, oT = sb("qT", [PAIRS, S]), sb("oT", [PAIRS, S])
        v_bank = [pg.bank[7], pg.bank[4]]
        y_bank = pg.bank[4]
        kv_steps = sig("kv_steps", 0)
        kv_spread = sig("kv_spread", 1)
        fold_full, fold_empty = sig("fold_full", 0), sig("fold_empty", 0)
        v_staged = sig("v_staged", 1)
        o_taken = sig("o_taken", U, 2)
        ring = [pg.bank[2], pg.bank[3], pg.bank[5], pg.bank[6]]


        def qr_fold(q):
            def mm(bank):
                for h in range(4 * q, 4 * q + 4):
                    for half in range(2):
                        at = ((h % 4) * 2 + half) * DC
                        last = nc.tensor.matmul(bank[0:CQ, at:at + DC], qr[:, h, half * CQ:(half + 1) * CQ], kr[:, h, :],
                                                start=True, stop=True)
                return last
            return mm, flat(QR[:, 4 * q:4 * q + 4, :, :]), slice(0, CQ), 512

        def out_fold(q):
            def mm(bank):
                for pair in (2 * q, 2 * q + 1):
                    for j in range(2):
                        last = nc.tensor.matmul(bank[j * DC:(j + 1) * DC, (pair % 2) * D:(pair % 2 + 1) * D],
                                                kckv[:, 2 * pair + j, :], wo[:, 2 * pair + j, :], start=True, stop=True)
                return last
            return mm, flat(OUT[:, 2 * q:2 * q + 2, :]), slice(0, P), 512

        def big_fold(h):
            def mm(bank):
                for m in range(KD):
                    last = nc.tensor.matmul(bank[:, m * 2 * CQ:(m + 1) * 2 * CQ], wq[:, h, m * P:(m + 1) * P], kcq[:, h, :],
                                            start=True, stop=True)
                return last
            return mm, flat(BIG[:, h, :, :]), slice(0, P), KD * 2 * CQ

        def mid_fold(q):
            def mm(bank):
                for h in range(8 * q, 8 * q + 8):
                    for half in range(2):
                        last = nc.tensor.matmul(bank[:, (h % 8) * DC:(h % 8 + 1) * DC], kcq[:, half, h, :], QR[:, h, half, :],
                                                start=(half == 0), stop=(half == 1))
                return last
            return mm, flat(MID[:, 8 * q:8 * q + 8, :]), slice(0, P), 512

        def q_fold(q):
            m, quarter = q // 2, q % 2
            def mm(bank):
                for h in range(8 * quarter, 8 * quarter + 8):
                    last = nc.tensor.matmul(bank[:, (h % 8) * DC:(h % 8 + 1) * DC], wq[:, h, m * P:(m + 1) * P], MID[:, h, :],
                                            start=True, stop=True)
                return last
            return mm, flat(Q[:, m, 8 * quarter:8 * quarter + 8, :]), slice(0, P), 512

        stages = [[qr_fold(q) for q in range(4)] + [out_fold(q) for q in range(4)]]
        stages += [[big_fold(h) for h in range(NH)]] if rotate_queries else \
            [[mid_fold(q) for q in range(2)], [q_fold(q) for q in range(4)]]

        if rotate_queries:
            big_full = sig("big_full", NH)
            products_ready = sig("products_ready", NH, len(ring))
            rotated_ready = sig("rotated_ready", NH, 2)
            rotated_used = sig("rotated_used", NH, 3)
            rotated, crossed = sb("rotated", [3, 2, S], CQ), sb("crossed", [2, 2, S], CQ)
        with nc.Block() as block:
            prefetch(pg, block, n)

            @block.gpsimd
            def _(pool):
                start(pg, pool, n)
                if rotate_queries:
                    rotated_ready.give(pool)
                pool.wait_ge(kv_spread.sem, 1)

                def rotate(i):
                    for h in range(NH):
                        pool.wait_ge(products_ready.sem, products_ready.at(i, h + 1))
                        nc.gpsimd.tensor_tensor(rotated[:, h % 3, :, :], rotated[:, h % 3, :, :], crossed[:, h % 2, :, :],
                                                ALU.add).then_inc(rotated_ready.sem, 1)

                def head(i):
                    body.stage_first(pool)
                    if rotate_queries:
                        rotate(i)

                def tail(i, more, before):
                    if more:
                        body.stage_next(pool, i)
                    pool.wait_ge(att.valued.sem, att.valued.at(i, 0))
                    nc.gpsimd.tensor_copy(v[:], vblk[:, i, :]).then_inc(v_staged.sem, 1)
                    att.gpsimd(pool, i, (lambda: body.roots(pool, i - 1)) if before else None)
                    if more and rotate_queries:
                        rotate(i + 1)
                batches(pool, head, tail, lambda i: body.roots(pool, i))

            @block.tensor
            def _(pe):
                start(pg, pe, n)
                k = 0
                for stage in stages:
                    if k:
                        pe.wait_ge(fold_empty.sem, k)
                    for mm, _, _, _ in stage:
                        if k >= len(ring):
                            pe.wait_ge(fold_empty.sem, k + 1 - len(ring))
                        mm(ring[k % len(ring)]).then_inc(fold_full.sem, 1)
                        k += 1
                pe.wait_ge(fold_empty.sem, k)
                pe.wait_ge(kv_spread.sem, 1)
                for b in range(B):
                    last = nc.tensor.transpose(ring[0][:, b * P:(b + 1) * P], vblk[:, b, :], pg.c("ident"))
                last.then_inc(fold_full.sem, 1)
                pe.wait_ge(fold_empty.sem, k + 1)
                att.credits_tensor(pe)
                if rotate_queries:
                    rotated_used.give(pe)

                def rotated_queries(i, s):
                    if s == 0:
                        acc.wait_emptied(pe, i, 0)
                    if s < NH:
                        pe.wait_ge(products_ready.sem, products_ready.at(i, s + 1 - len(ring)))
                        for half in range(2):
                            for m in range(KD):
                                last = nc.tensor.matmul(ring[s % 4][0:CQ, half * S:(half + 1) * S],
                                                        BIG[:, s, m, half * CQ:(half + 1) * CQ], body.xT[:, m, :],
                                                        start=(m == 0), stop=(m == KD - 1))
                        last.then_inc(big_full.sem, 1)
                    h = s - 2
                    if h >= 0:
                        fill, at = 1 + h // 4, (h // 2 % 2) * S
                        if h % 4 == 0:
                            acc.wait_empty(pe, i, fill)
                        pe.wait_ge(rotated_ready.sem, rotated_ready.at(i, h + 1))
                        out = acc.bank(fill)[(h % 2) * DC:(h % 2 + 1) * DC, at:at + S]
                        for half in range(2):
                            last = nc.tensor.matmul(out, QR[:, h, half, :], rotated[:, h % 3, half, :],
                                                    start=(half == 0), stop=(half == 1))
                        last.then_inc(rotated_used.sem, 1)

                def queries(i, f):
                    if f == 0:
                        acc.wait_emptied(pe, i, 0)
                    acc.wait_empty(pe, i, 1 + f)
                    for pair in (2 * f, 2 * f + 1):
                        for m in range(KD):
                            last = nc.tensor.matmul(acc.bank(1 + f)[:, (pair % 2) * S:(pair % 2 + 1) * S],
                                                    flat(Q[:, m, 2 * pair:2 * pair + 2, :]), body.xT[:, m, :],
                                                    start=(m == 0), stop=(m == KD - 1))
                    last.then_inc(acc.full.sem, 1)

                def projections(i):
                    return [] if rotate_queries else [lambda f=f: queries(i, f) for f in range(4)]

                def rotation(i):
                    if rotate_queries:
                        for s in range(NH + 2):
                            rotated_queries(i, s)

                def head(i):
                    body.transpose_x(pe, i)
                    for piece in projections(i):
                        piece()
                    rotation(i)

                def score(i, u, bank):
                    for c in range(4):
                        last = nc.tensor.matmul(bank[:, c * P:(c + 1) * P], qT[:, 4 * u["g"] + c, u["t"] * P:(u["t"] + 1) * P],
                                                kblk[:, i, :], start=True, stop=True)
                    return last

                def value(i, s, probsT):
                    pe.wait_ge(o_taken.sem, o_taken.at(i, s + 1 - 2))
                    return nc.tensor.matmul(v_bank[s % 2][:], v[:], probsT, start=True, stop=True)

                def before_values(i):
                    pe.wait_ge(v_staged.sem, v_staged.at(i, 1))
                    pe.wait_ge(body.out_taken.sem, body.out_taken.at(i, 0))

                def tail(i, more):
                    acc.wait_emptied(pe, i, 4)
                    att.tensor(pe, i, lambda k, u, part, bank: score(i, u, bank), lambda s, u, probsT: value(i, s, probsT),
                               before_values=lambda: before_values(i), pieces=projections(i + 1) if more else (),
                               early={0: lambda: body.transpose_x(pe, i + 1)} if more else {})
                    pe.wait_ge(o_taken.sem, o_taken.at(i, U))
                    body.project_out(pe, i, oT, OUT, y_bank, PAIRS)
                    if more:
                        rotation(i + 1)
                batches(pe, head, tail)

            @block.scalar
            def _(act):
                start(pg, act, n)
                acc.empty.give(act)
                att.credits_scalar(act)
                o_taken.give(act)

                def queries(i, f):
                    if rotate_queries:
                        act.wait_ge(rotated_used.sem, rotated_used.at(i, 4 * f + 4))
                    else:
                        acc.wait_full(act, i, 1 + f)
                    nc.scalar.activation(qT[:, 2 * f:2 * f + 2, :], shaped(acc.bank(1 + f)[:], (2, S)), ACT.Copy)\
                        .then_inc(acc.empty.sem, 1)

                def takes(i):
                    return [] if rotate_queries else [lambda f=f: queries(i, f) for f in range(4)]

                def rotation(i):
                    if rotate_queries:
                        for f in range(4):
                            queries(i, f)

                def head(i):
                    body.take_xT(act, i)
                    for take in takes(i):
                        take()
                    rotation(i)

                def take_output(i, s):
                    u = units[s]
                    act.wait_ge(att.valued.sem, att.valued.at(i, s + 1))
                    nc.scalar.activation(oT[:, 4 * u["g"]:4 * u["g"] + 4, u["t"] * P:(u["t"] + 1) * P],
                                         shaped(v_bank[s % 2][:], (4, P)), ACT.Copy).then_inc(o_taken.sem, 1)

                def tail(i, more):
                    att.scalar(act, i, takes(i + 1) if more else (), after_turn=lambda s: take_output(i, s),
                               early={0: lambda: body.take_xT(act, i + 1)} if more else {})
                    if more:
                        rotation(i + 1)
                batches(act, head, tail)

            @block.vector
            def _(dve):
                start(pg, dve, n)
                body.out_taken.give(dve)
                if rotate_queries:
                    products_ready.give(dve)
                cos, sin = over(pg.c("kcos"), 1, B), over(pg.c("ksin"), 1, B)
                h = DC // 2
                nc.vector.tensor_tensor(swapped[:, :, 0:h], pg.ctx2[:, :, h:DC], sin[:, :, 0:h], ALU.mult)
                nc.vector.tensor_tensor(swapped[:, :, h:DC], pg.ctx2[:, :, 0:h], sin[:, :, h:DC], ALU.mult)
                nc.vector.tensor_tensor(kv[:], pg.ctx2[:], cos, ALU.mult)
                nc.vector.memset(vblk[:], 0.0).then_inc(kv_steps.sem, 1)
                dve.wait_ge(kv_steps.sem, 1)
                nc.vector.tensor_tensor(kv[:], kv[:], swapped[:], ALU.add).then_inc(kv_steps.sem, 1)
                dve.wait_ge(kv_steps.sem, 2)
                nc.vector.tensor_copy(vblk[0:NK, :, 0:DC], kv[0:NK, :, :])
                nc.vector.tensor_copy(vblk[NK:P, :, DC:P], kv[NK:P, :, :]).then_inc(kv_spread.sem, 1)
                k = 0
                for stage in stages:
                    for _, dst, rows, size in stage:
                        dve.wait_ge(fold_full.sem, k + 1)
                        nc.vector.tensor_copy(dst, ring[k % len(ring)][rows, 0:size]).then_inc(fold_empty.sem, 1)
                        k += 1
                dve.wait_ge(fold_full.sem, k + 1)
                nc.vector.tensor_copy(kblk[:], shaped(ring[0][:], (B, P))).then_inc(fold_empty.sem, 1)

                def rotation(i):
                    for h in range(NH if rotate_queries else 0):
                        src = shaped(ring[h % 4][0:CQ, :], (2, S))
                        dve.wait_ge(big_full.sem, big_full.at(i, h + 1))
                        dve.wait_ge(rotated_ready.sem, rotated_ready.at(i, h + 1 - 2))
                        dve.wait_ge(rotated_used.sem, rotated_used.at(i, h + 1 - 3))
                        nc.vector.tensor_tensor(rotated[:, h % 3, :, :], src, qcos, ALU.mult)
                        for half in range(2):
                            last = nc.vector.tensor_tensor(crossed[:, h % 2, half, :], src[:, 1 - half, :],
                                                           qsin[:, half, :], ALU.mult)
                        last.then_inc(products_ready.sem, 1)

                def finish_pieces(i):
                    return [lambda: body.add(dve, i, y_bank)] + body.norm_pieces(dve, i)

                def tail(i, more, before):
                    chain = Chain(body.vchain, dve, i)
                    att.vector(dve, i, chain, finish_pieces(i - 1) if before else ())
                    chain.done()
                    if more:
                        rotation(i + 1)
                batches(dve, rotation, tail, lambda i: body.add_norm(dve, i, y_bank))


def small_xattn(pg, n):
    nc = pg.nc
    with Scope(nc, f"s{n}") as ctx:
        units = [{"t": t, "g": g, "heads": 8, "keys": NK, "masks": [(0, NK, pg.c("causal")[:, 0:NK])] if t == 0 else []}
                 for t in range(T) for g in range(KD)]
        body = Body(pg, ctx, 2, attention_steps(units, True), f"s{n}")
        att = Attention(pg, ctx, f"s{n}", units, True, pg.bank[2:4])
        acc = body.acc
        sb = lambda s, dims: ctx.enter_context(nc.sbuf_tensor(f"s{n}_{s}", [P, *dims], F32))
        qT, oT = sb("qT", [B, KD, S]), sb("oT", [KD, S])
        kblk, vblk = sb("kblk", [B, KD, 8, NK]), sb("vblk", [B, 8, 2, HD])
        kv_ready = Signal(ctx, nc, "kv_ready", 1)
        kv_spread = Signal(ctx, nc, "kv_spread", 1)
        o_taken = Signal(ctx, nc, "o_taken", 1, credit=1)
        ctxT = pg.ctxT
        wq, wo = pg.w(n, "wq", KD, D), pg.w(n, "wo", KD, D)
        wk, wv = pg.w(n, "wk", rows=NK), pg.w(n, "wv", rows=NK)
        o_bank, y_bank = pg.bank[7], pg.bank[4]
        with nc.Block() as block:
            prefetch(pg, block, n)

            @block.gpsimd
            def _(pool):
                start(pg, pool, n)
                att.gpsimd(pool, 0)
                for i in range(B):
                    if i + 1 < B:
                        att.gpsimd(pool, i + 1, (lambda: body.roots(pool, i - 1)) if i else None)
                    elif i:
                        body.roots(pool, i - 1)
                body.roots(pool, B - 1)

            @block.tensor
            def _(pe):
                start(pg, pe, n)
                for m in range(KD):
                    nc.tensor.matmul(pg.bank[2][:, m * S:(m + 1) * S], wk[:, m * P:(m + 1) * P], ctxT[:, :, 0:NK],
                                     start=True, stop=True)
                for b in range(B):
                    last = nc.tensor.matmul(pg.bank[5 + b // 2][:, (b % 2) * D:(b % 2 + 1) * D], ctxT[:, b, :], wv,
                                            start=True, stop=True)
                last.then_inc(kv_ready.sem, 1)
                att.credits_tensor(pe)

                def x(i):
                    acc.wait_empty(pe, i, 0)
                    transpose_tokens(nc, pe, acc.bank(0), pg.x[:, i, :, :], pg.c("ident")).then_inc(acc.full.sem, 1)

                def queries(i):
                    acc.wait_emptied(pe, i, 0)
                    acc.wait_empty(pe, i, 1)
                    project_features(nc, acc.bank(1), wq, body.xT).then_inc(acc.full.sem, 1)

                def score(i):
                    return lambda k, u, part, bank: nc.tensor.matmul(
                        bank[:], qT[:, i, u["g"], u["t"] * P:(u["t"] + 1) * P], kblk[:, i, u["g"], :, :], start=True, stop=True)

                def value(i):
                    def of_unit(s, u, probsT):
                        for c in range(4):
                            at = u["g"] * S + u["t"] * P
                            last = nc.tensor.matmul(o_bank[c * 32:(c + 1) * 32, at:at + P], vblk[:, i, 4 * u["g"] + c, :, :],
                                                    probsT[:, c * P:(c + 1) * P], start=True, stop=True)
                        return last
                    return of_unit
                x(0)
                queries(0)
                x(1)
                pe.wait_ge(kv_spread.sem, 1)
                acc.wait_emptied(pe, 0, 1)
                for u in range(len(units)):
                    att.score_unit(pe, 0, u, score(0))
                queries(1)
                for i in range(B):
                    pe.wait_ge(o_taken.sem, o_taken.at(i, 0))
                    if i + 1 < B:
                        acc.wait_emptied(pe, i + 1, 1)
                    for u in range(len(units) + 1):
                        if u < len(units):
                            att.turn_unit(pe, i, u)
                            if i + 1 < B:
                                att.score_unit(pe, i + 1, u, score(i + 1))
                        if u:
                            att.value_unit(pe, i, u - 1, value(i))
                        if i + 2 < B and u in (0, 2):
                            (x, queries)[u // 2](i + 2)
                    pe.wait_ge(o_taken.sem, o_taken.at(i, 1))
                    body.project_out(pe, i, oT, wo, y_bank, KD)

            @block.scalar
            def _(act):
                start(pg, act, n)
                acc.empty.give(act)
                att.credits_scalar(act)
                o_taken.give(act)

                def take_queries(i):
                    acc.wait_full(act, i, 1)
                    nc.scalar.activation(qT[:, i, :, :], shaped(acc.bank(1)[:], (KD, S)), ACT.Copy, scale=0.25)\
                        .then_inc(acc.empty.sem, 1)
                body.take_xT(act, 0)
                take_queries(0)
                body.take_xT(act, 1)
                for u in range(len(units)):
                    att.exp_unit(act, 0, u)
                take_queries(1)
                for i in range(B):
                    for u in range(len(units)):
                        att.turn(act, i, u)
                        if i + 1 < B:
                            att.exp_unit(act, i + 1, u)
                        if i + 2 < B and u == 0:
                            body.take_xT(act, i + 2)
                        if i + 2 < B and u == 2:
                            take_queries(i + 2)
                    act.wait_ge(att.valued.sem, att.valued.at(i, len(units)))
                    nc.scalar.activation(oT[:], shaped(o_bank[:], (KD, S)), ACT.Copy).then_inc(o_taken.sem, 1)

            @block.vector
            def _(dve):
                start(pg, dve, n)
                body.out_taken.give(dve)
                dve.wait_ge(kv_ready.sem, 1)
                for b in range(B):
                    for m in range(KD):
                        nc.vector.tensor_tensor(kblk[:, b, m, :, :],
                                                over(pg.bank[2][:, m * S + b * NK:m * S + (b + 1) * NK], 1, 8),
                                                over(pg.c("mask8"), 2, NK), ALU.mult)
                    last = nc.vector.tensor_tensor(vblk[:, b, :, :, :],
                                                   shaped(pg.bank[5 + b // 2][:, (b % 2) * D:(b % 2 + 1) * D], (8, 2, HD)),
                                                   over(over(pg.c("half2"), 1, 8), 3, HD), ALU.mult)
                last.then_inc(kv_spread.sem, 1)

                def softmax(i, pieces=()):
                    chain = Chain(body.vchain, dve, i)
                    att.vector(dve, i, chain, pieces)
                    chain.done()
                softmax(0)
                for i in range(B):
                    pieces = [lambda: body.add(dve, i - 1, y_bank), *body.norm_pieces(dve, i - 1)] if i else []
                    if i + 1 < B:
                        softmax(i + 1, pieces)
                    else:
                        for piece in filter(None, pieces):
                            piece()
                body.add_norm(dve, B - 1, y_bank)


def prefetch(pg, block, n, more=None):
    order, at = pg.order, pg.order.index(n)

    def load(sp, m):
        sp.dma_start(pg.arena[m % 2][:, 0:pg.where[m]["size"]], pg.dram[m]).then_inc(pg.loaded[m], 16)
        if m in pg.where["overflow"]:
            sp.dma_start(pg.overflow(m), pg.dram[f"overflow{m}"]).then_inc(pg.loaded[m], 16)

    @block.sync
    def _(sp):
        if at == 0:
            for b in range(2):
                sp.dma_start(pg.x[:, 2 * b:2 * b + 2, :, :],
                             pg.dram["x"][2 * b:2 * b + 2].rearrange("b (t p) d -> p b t d", p=P))\
                    .then_inc(pg.inputs_loaded, 16)
            load(sp, n)
            for half in range(2):
                cols = slice(half * NK, (half + 1) * NK)
                sp.dma_start(pg.ctxT[:, :, cols], pg.dram["ctxT"]).then_inc(pg.inputs_loaded, 16)
            sp.dma_start(pg.ctx2[:], pg.dram["ctx2"]).then_inc(pg.inputs_loaded, 16)
            sp.dma_start(pg.const[:], pg.dram["const"]).then_inc(pg.inputs_loaded, 16)
        if at + 1 < len(order):
            load(sp, order[at + 1])
        if more:
            more(sp)


BUILDERS = {1: small_xattn, 4: small_xattn, 0: head_attention, 7: lambda pg, n: latent_attention(pg, n, False),
            10: lambda pg, n: latent_attention(pg, n, True), 6: differential_attention, 3: decay_attention,
            8: modulated_ffn, 9: windowed_attention,
            2: lambda pg, n: weighted_experts(pg, n, 8, 2, True, 17), 5: top1_experts,
            11: lambda pg, n: weighted_experts(pg, n, 8, 2, False, 11)}


def decoder(nc, where, dram, out):
    with ExitStack() as ctx:
        pg = Program(nc, ctx, where, dram)
        for n in pg.order:
            BUILDERS[n](pg, n)
        with nc.Block() as block:
            @block.sync
            def _(sp):
                sp.dma_start(out.rearrange("b (t p) d -> p b t d", p=P), pg.x[:]).then_inc(pg.stored, 16)
                sp.wait_ge(pg.stored, 16)


def kernel(**inputs):
    import concourse.bacc as bacc
    from concourse.bass_utils import run_bass_kernel_spmd

    w = {k: np.asarray(v) for k, v in inputs.items()}
    consts, L, overflow = layouts(w)
    ctx = w["ctx_512"]
    arrays = {"x": w["x"], "ctxT": np.ascontiguousarray(ctx.transpose(2, 0, 1)),
              "ctx2": np.ascontiguousarray(np.concatenate([ctx.transpose(1, 0, 2)] * 2))}
    where = {"order": SUBLAYERS, "arena": [8, 8]}
    arrays["const"], where["const"] = pack(consts)
    where["const"]["size"] = arrays["const"].shape[1]
    for n in SUBLAYERS:
        arrays[n], where[n] = pack(L[n])
        where[n]["size"] = arrays[n].shape[1]
    for n in SUBLAYERS:
        where["arena"][n % 2] = max(where["arena"][n % 2], where[n]["size"])
        if n in SPARE:
            assert n + 1 not in where or where[n + 1]["size"] <= SPARE_AT[n]
            where["arena"][1 - n % 2] = max(where["arena"][1 - n % 2], SPARE_AT[n] + SPARE[n])
    where["overflow"] = {}
    for n, a in overflow.items():
        if n in SUBLAYERS:
            at = max(where[m]["size"] for m in (n - 1, n + 1) if m in where) if len(SUBLAYERS) > 1 else 0
            arrays[f"overflow{n}"], where["overflow"][n] = np.ascontiguousarray(a), (at, a.shape[1])
            where["arena"][1 - n % 2] = max(where["arena"][1 - n % 2], at + a.shape[1])
    nc = bacc.Bacc("TRN2", target_bir_lowering=False, num_devices=1)
    dram, given = {}, {}
    for name, a in arrays.items():
        label = f"in_{name}_dram" if isinstance(name, str) else f"in_weights_{name}_dram"
        given[label] = a
        dram[name] = nc.dram_tensor(label, a.shape, mybir.dt.from_np(a.dtype), kind="ExternalInput").ap()
    out = nc.dram_tensor("out_0_dram", (B, S, D), F32, kind="ExternalOutput").ap()
    decoder(nc, where, dram, out)
    r = run_bass_kernel_spmd(nc, [given], core_ids=[0])
    return r.results[0]["out_0_dram"]
```
